# Optimizing a Trainium2 kernel written in Bass

```python
import numpy as np
import jax
import jax.numpy as jnp

def _softmax(x, axis=-1):
    return jax.nn.softmax(x, axis=axis)

def _gelu(x):
    return jax.nn.gelu(x, approximate=True)

def _silu(x):
    return jax.nn.silu(x)

def _sigmoid(x):
    return jax.nn.sigmoid(x)

def _layernorm(x, axis=-1, eps=1e-05):
    m = jnp.mean(x, axis=axis, keepdims=True)
    v = jnp.var(x, axis=axis, keepdims=True)
    return (x - m) / jnp.sqrt(v + eps)

def _scatter_add(tgt, idx, src, axis=0):
    return tgt.at[idx].add(src)

def _segment_sum(src, seg, n):
    return jax.ops.segment_sum(src, seg, n)
kernel_name = 'mk_gnn_ffn_d1_gnn_r8_15262c'

def setup_inputs(seed: int=0):
    np.random.seed(seed)
    _w = jnp.asarray

    def _rec_inputs():
        import jax
        import jax.numpy as jnp
        _gk = jax.random.key(seed)
        x = -0.0002117 + 1 * jax.random.normal(jax.random.fold_in(_gk, 1), (3125, 1024), jnp.float32)
        src = jax.random.randint(jax.random.fold_in(_gk, 2), (50000,), 0, 3125, jnp.int32)
        dst = jax.random.randint(jax.random.fold_in(_gk, 3), (50000,), 0, 3125, jnp.int32)
        _o = jnp.argsort(dst, stable=True)
        src = src[_o]
        dst = dst[_o]
        return (x, src, dst)
    x, src, dst = _rec_inputs()

    def _L0_gnn_setup():
        import jax, jax.numpy as jnp
        import numpy as np
        N = 3125
        E = 50000
        H = 4
        C = 256
        D_IN = 1024
        NEG_SLOPE = 0.2
        key = jax.random.key(seed)
        k1, k2, k3, k4, k5, k6 = jax.random.split(key, 6)
        x = jax.random.normal(k1, (N, D_IN), dtype=jnp.float32)
        edge_index = jax.random.randint(k2, (2, E), 0, N, dtype=jnp.int64)
        scale = 1.0 / np.sqrt(D_IN)
        W = jax.random.normal(k3, (D_IN, H * C), dtype=jnp.float32) * scale
        att_src = jax.random.normal(k4, (H, C), dtype=jnp.float32) * 0.1
        att_dst = jax.random.normal(k5, (H, C), dtype=jnp.float32) * 0.1
        bias = jax.random.normal(k6, (H * C,), dtype=jnp.float32) * 0.01
        return {'x': x, 'edge_index': edge_index, 'W': W, 'att_src': att_src, 'att_dst': att_dst, 'bias': bias}
    _L0_gnn_all = _L0_gnn_setup()
    _L0_gnn_in = {k: v for k, v in _L0_gnn_all.items() if k in ('W', 'att_src', 'att_dst', 'bias')}
    del _L0_gnn_all

    def _L0_ffn_setup():
        import jax, jax.numpy as jnp
        import numpy as np
        EPS = 1e-12

        def _l2norm(v):
            n = jnp.sqrt(jnp.sum(v * v, axis=-1, keepdims=True))
            return v / jnp.maximum(n, EPS)
        key = jax.random.key(seed)
        ks = jax.random.split(key, 6)
        B, S, D, F, E = (2, 256, 1024, 512, 8)
        std = 0.02
        return {'x': jax.random.normal(ks[0], (B, S, D), jnp.float32), 'Wp': jax.random.normal(ks[1], (D, D), jnp.float32) * (1.0 / np.sqrt(D)), 'sim_matrix': jax.random.normal(ks[2], (E, D), jnp.float32) * std, 'temperature': jnp.asarray(1.0, jnp.float32), 'W1': jax.random.normal(ks[3], (E, D, F), jnp.float32) * (1.0 / np.sqrt(D)), 'b1': jnp.zeros((E, F), jnp.float32), 'W2': jax.random.normal(ks[4], (E, F, D), jnp.float32) * (1.0 / np.sqrt(F)), 'b2': jnp.zeros((E, D), jnp.float32)}
    _L0_ffn_all = _L0_ffn_setup()
    _L0_ffn_in = {k: v for k, v in _L0_ffn_all.items() if k in ('Wp', 'sim_matrix', 'temperature', 'W1', 'b1', 'W2', 'b2')}
    del _L0_ffn_all
    return {'x': x, 'src': src, 'dst': dst, 'L0_gnn_W': _L0_gnn_in['W'], 'L0_gnn_att_src': _L0_gnn_in['att_src'], 'L0_gnn_att_dst': _L0_gnn_in['att_dst'], 'L0_gnn_bias': _L0_gnn_in['bias'], 'L0_ffn_Wp': _L0_ffn_in['Wp'], 'L0_ffn_sim_matrix': _L0_ffn_in['sim_matrix'], 'L0_ffn_temperature': _L0_ffn_in['temperature'], 'L0_ffn_W1': _L0_ffn_in['W1'], 'L0_ffn_b1': _L0_ffn_in['b1'], 'L0_ffn_W2': _L0_ffn_in['W2'], 'L0_ffn_b2': _L0_ffn_in['b2']}

def reference(x, src, dst, L0_gnn_W, L0_gnn_att_src, L0_gnn_att_dst, L0_gnn_bias, L0_ffn_Wp, L0_ffn_sim_matrix, L0_ffn_temperature, L0_ffn_W1, L0_ffn_b1, L0_ffn_W2, L0_ffn_b2):
    import jax
    import jax.numpy as jnp

    def _L0_gnn_ref(x, edge_index, W, att_src, att_dst, bias):
        import jax, jax.numpy as jnp
        import numpy as np
        N = 3125
        E = 50000
        H = 4
        C = 256
        D_IN = 1024
        NEG_SLOPE = 0.2
        xp = (x @ W).reshape(N, H, C)
        a_src = jnp.einsum('nhc,hc->nh', xp, att_src)
        a_dst = jnp.einsum('nhc,hc->nh', xp, att_dst)
        loops = jnp.arange(N, dtype=edge_index.dtype)
        src = jnp.concatenate([edge_index[0], loops])
        dst = jnp.concatenate([edge_index[1], loops])
        e = jax.nn.leaky_relu(a_src[src] + a_dst[dst], NEG_SLOPE)
        m = jax.ops.segment_max(e, dst, num_segments=N)
        ee = jnp.exp(e - m[dst])
        z = jax.ops.segment_sum(ee, dst, num_segments=N)
        alpha = ee / z[dst]
        msgs = xp[src] * alpha[:, :, None]
        out = jax.ops.segment_sum(msgs, dst, num_segments=N)
        out = out.reshape(N, H * C) + bias
        return jax.nn.relu(out)

    def _L0_ffn_ref(x, Wp, sim_matrix, temperature, W1, b1, W2, b2):
        import jax, jax.numpy as jnp
        import numpy as np
        EPS = 1e-12

        def _l2norm(v):
            n = jnp.sqrt(jnp.sum(v * v, axis=-1, keepdims=True))
            return v / jnp.maximum(n, EPS)
        E = sim_matrix.shape[0]
        top_k = 2
        proj = jnp.einsum('bsd,ed->bse', x, Wp)
        pn = _l2norm(proj)
        sn = _l2norm(sim_matrix)
        gate_scores = jnp.einsum('bsd,ed->bse', pn, sn) / temperature
        top_v, top_i = jax.lax.top_k(gate_scores, top_k)
        gate_probs = jax.nn.softmax(top_v, axis=-1)
        comb = jnp.sum(jax.nn.one_hot(top_i, E, dtype=x.dtype) * gate_probs[..., None], axis=-2)
        h = jax.nn.gelu(jnp.einsum('bsd,edf->ebsf', x, W1) + b1[:, None, None, :], approximate=False)
        eo = jnp.einsum('ebsf,efd->ebsd', h, W2) + b2[:, None, None, :]
        out = jnp.einsum('ebsd,bse->bsd', eo, comb)
        return out
    edge_index = jnp.stack([src, dst])
    x = x + _L0_gnn_ref(_layernorm(x, axis=-1), edge_index, L0_gnn_W, L0_gnn_att_src, L0_gnn_att_dst, L0_gnn_bias)
    x = x + _L0_ffn_ref(_layernorm(x, axis=-1)[None], L0_ffn_Wp, L0_ffn_sim_matrix, L0_ffn_temperature, L0_ffn_W1, L0_ffn_b1, L0_ffn_W2, L0_ffn_b2)[0]
    return x

_drawn_inputs = setup_inputs


def setup_inputs(seed=0):
    import zlib

    import numpy as np

    out = dict(_drawn_inputs(seed))
    spreads = {'L0_ffn_b1': (0.0, 0.1), 'L0_ffn_b2': (0.0, 0.1)}
    factors = {}
    for name, (base, spread) in spreads.items():
        noise = np.random.default_rng([zlib.crc32(name.encode()), seed]).standard_normal(out[name].shape)
        drawn = base * np.exp(spread * noise) if base else spread * noise
        out[name] = jnp.asarray(drawn.astype(out[name].dtype))
    for name, factor in factors.items():
        out[name] = (out[name] * factor).astype(out[name].dtype)
    return out
```

```python
from contextlib import ExitStack

import concourse.bass as bass
from concourse import mybir

F32 = mybir.dt.float32
I32 = mybir.dt.int32
U32 = mybir.dt.uint32
ALU = mybir.AluOpType
ACT = mybir.ActivationFunctionType
AX = mybir.AxisListType

P = 128
NODES, EDGES, D = 3125, 50000, 1024
HEADS, C = 4, 256
NX, FF = 8, 512
ROWS = 125
BLOCKS = NODES // ROWS
KD, KF = D // P, FF // P
TILES = -(-EDGES // P)
VISITS = TILES + BLOCKS
VP = VISITS // 4
ROW4 = 4 * P
CHUNK = VISITS // 8
HI = -(-NODES // P)
PACK = 2 + 2 * HEADS
PAIRS = 2 * NODES
XTILES = (PAIRS + NX * (P - 1)) // P
BIG = 1e30
LN_EPS = 1e-5
NORM_EPS = 1e-12
SLOPE = 0.2


def steps(eng, n, body):
    body(0, 0, 0)
    body(1, 0, 1)
    with eng.Fori(1, n // 2) as j:
        body(2 * j, j, 0)
        body(2 * j + 1, j, 1)
    if n % 2:
        body(n - 1, n // 2, 0)


def early(i, n):
    return isinstance(i, int) and i < n


def rows_of(t, i):
    if isinstance(i, int):
        return t[ROWS * i:ROWS * (i + 1), :]
    return t[bass.ds(ROWS * i, ROWS), :]


def at(t, i):
    return t[:, i] if isinstance(i, int) else t[:, bass.ds(i, 1)].squeeze(1)


def wait_apart(eng, met, sem, value):
    if not isinstance(value, int):
        eng.lower_val(value)
    eng.wait_ge(met, 1)
    eng.wait_ge(sem, value)


class Chain:

    def __init__(self, eng, sem, base=0):
        self.eng, self.sem, self.n = eng, sem, base

    def __call__(self, instruction, apart=None):
        instruction.then_inc(self.sem, 1)
        self.n = self.n + 1
        if apart is not None:
            wait_apart(self.eng, apart, self.sem, self.n)
        else:
            self.eng.wait_ge(self.sem, self.n)


def program(nc, x, src, dst, W, att_src, att_dst, bias, Wp, sim, temp, W1, b1, W2, b2, out):
    names = iter(range(1000))

    def dram(name, shape, dt=F32):
        return nc.dram_tensor(name, shape, dt).ap()

    src_d = dram("src_padded", (VISITS - BLOCKS + 1, P), I32)
    dst_d = dram("dst_padded", (VISITS - BLOCKS + 1, P), I32)
    lo_d = dram("src_lo_by_visit", (VISITS, P))
    dloc_d = dram("dst_local_by_visit", (VISITS, P))
    xp_d = dram("projected", (NODES, D))
    st_d = dram("node_terms", (NODES, 2 * HEADS))
    x2_d = dram("x_after_gnn", (NODES, D))
    x2n_d = dram("x_after_gnn_normed", (NODES, D))
    tok_d = dram("token_of_slot", (XTILES * P, 1), I32)
    eo_d = dram("expert_rows", (XTILES * P, D))

    ctx = ExitStack()

    def sem(name):
        return ctx.enter_context(nc.semaphore(name))

    def sbuf(c, name, shape, dt=F32):
        return c.enter_context(nc.sbuf_tensor(name, shape, dt))

    def psum(c, name, shape):
        return c.enter_context(nc.psum_tensor(name, shape, F32))

    s_met = sem("always_met")

    with ctx:
        shifted = sbuf(ctx, "shifted", [P, P + 2])
        ident = shifted[:, 1:P + 1]
        iota_col = sbuf(ctx, "iota_col", [P, 1])
        unit = sbuf(ctx, "unit", [P, 1])
        iota_row = sbuf(ctx, "iota_row", [P, P])
        ones = sbuf(ctx, "ones", [P, P])
        rows_i = sbuf(ctx, "visit_rows", [1, 4, VISITS], I32)
        block_r, first_r, last_r, par_r = (rows_i[:, n, :] for n in range(4))
        WpT = sbuf(ctx, "WpT", [P, KD, D])
        Msim = sbuf(ctx, "Msim", [P, KD, NX])
        stN = sbuf(ctx, "node_terms_sb", [ROWS, BLOCKS, 2 * HEADS])
        nsq = sbuf(ctx, "proj_sq", [ROWS, BLOCKS])
        scores = sbuf(ctx, "scores", [ROWS, BLOCKS, NX])
        slot_i = sbuf(ctx, "slots", [ROWS, BLOCKS, 2], I32)
        gates = sbuf(ctx, "gates", [ROWS, BLOCKS, 2])
        comb = sbuf(ctx, "comb", [ROWS, BLOCKS, NX])
        xe_i = sbuf(ctx, "expert_of_tile", [1, XTILES], I32)

        edge_ctx = ExitStack()
        srcT = sbuf(edge_ctx, "srcT", [P, VISITS], I32)
        dlocT = sbuf(edge_ctx, "dlocT", [P, VISITS])
        hiT = sbuf(edge_ctx, "hiT", [P, VISITS])
        PK = sbuf(edge_ctx, "PK", [P, VISITS, PACK])
        dstV = sbuf(edge_ctx, "dstV", [VP, ROW4])

        with ExitStack() as c:
            e_i = [sbuf(c, f"edges_i{n}", [98, ROW4], I32) for n in range(2)]
            dst_f = sbuf(c, "dst_f", [98, ROW4])
            junk = sbuf(c, "junk", [98, ROW4])
            cnt = sbuf(c, "cnt", [98, BLOCKS - 1])
            thr_i = sbuf(c, "thr_i", [P, 2, BLOCKS - 1], I32)
            thr = sbuf(c, "thr", [P, 2, BLOCKS - 1])
            visit_v = sbuf(c, "visit_v", [VP, 4])
            visit_r = sbuf(c, "visit_r", [1, VISITS])
            cmp_v = sbuf(c, "cmp_v", [VP, 4, BLOCKS - 1])
            cmp_r = sbuf(c, "cmp_r", [1, VISITS, BLOCKS - 1])
            b_v = sbuf(c, "b_v", [VP, 4])
            nb_v = sbuf(c, "nb_v", [VP, 4])
            tile_v = sbuf(c, "tile_v", [VP, 4])
            tile_i = sbuf(c, "tile_i", [VP, 4], I32)
            b_r = sbuf(c, "b_r", [1, VISITS + 2])
            flag_r = sbuf(c, "flag_r", [1, 2, VISITS])
            srcVi = sbuf(c, "srcVi", [VP, ROW4], I32)
            dstVi = sbuf(c, "dstVi", [VP, ROW4], I32)
            bitsVi = sbuf(c, "bitsVi", [VP, 2, ROW4], I32)
            fV = sbuf(c, "fV", [VP, 4, ROW4])
            cnt_ps = psum(c, "cnt_ps", [P, 512])
            t_ps = psum(c, "t_ps", [P, 3, 4, P])
            s_const, s_pad, s_edges, s_dram = sem("ix_const"), sem("ix_pad"), sem("ix_edges"), sem("ix_dram")
            s_chain, s_cnt, s_cntps, s_idx = sem("ix_chain"), sem("ix_cnt"), sem("ix_cntps"), sem("ix_idx")
            s_vload, s_vals, s_tr, s_vstore = sem("ix_vload"), sem("ix_vals"), sem("ix_tr"), sem("ix_vstore")
            s_sel = sem("ix_sel")
            full = (EDGES // ROW4)
            with nc.Block() as block:
                @block.gpsimd
                def _(pool):
                    pool.memset(shifted[:, :], 0.0).then_inc(s_sel, 1)
                    pool.memset(ones[:, :], 1.0).then_inc(s_const, 1)
                    pool.memset(unit[:, :], 1.0).then_inc(s_met, 1)
                    pool.iota(iota_col[:, :], pattern=[[0, 1]], base=0, channel_multiplier=1,
                              allow_small_or_imprecise_dtypes=True).then_inc(s_const, 1)
                    pool.iota(iota_row[:, :], pattern=[[1, P]], base=0, channel_multiplier=0,
                              allow_small_or_imprecise_dtypes=True).then_inc(s_const, 1)
                    pool.iota(visit_v[:, :], pattern=[[1, 4]], base=0, channel_multiplier=4,
                              allow_small_or_imprecise_dtypes=True).then_inc(s_const, 1)
                    pool.iota(visit_r[:, :], pattern=[[1, VISITS]], base=0, channel_multiplier=0,
                              allow_small_or_imprecise_dtypes=True).then_inc(s_const, 1)
                    pool.wait_ge(s_sel, 1)
                    pool.affine_select(out=shifted[:, :], in_=shifted[:, :], compare_op=ALU.not_equal,
                                       fill=1.0, base=1, pattern=[[-1, P + 2]],
                                       channel_multiplier=1).then_inc(s_const, 1)
                    pool.wait_ge(s_idx, 1)
                    pool.wait_ge(s_dram, 32)
                    for q in range(4):
                        for dram_t, sb_t in ((src_d, srcVi), (dst_d, dstVi)):
                            pool.indirect_dma_start(
                                out=sb_t[:, q * P:(q + 1) * P], out_offset=None, in_=dram_t[:, :],
                                in_offset=bass.IndirectOffsetOnAxis(ap=tile_i[:, q:q + 1], axis=0),
                            ).then_inc(s_vload, 16)

                @block.sync
                def _(sp):
                    sp.wait_ge(s_pad, 2)
                    for t, d in ((e_i[0], src), (e_i[1], dst)):
                        sp.dma_start(t[0:full, :], d[0:full * ROW4].rearrange("(p n) -> p n", n=ROW4)).then_inc(s_edges, 16)
                        sp.dma_start(t[full:full + 1, 0:EDGES - full * ROW4],
                                     d[full * ROW4:EDGES].rearrange("(a n) -> a n", a=1)).then_inc(s_edges, 16)
                    sp.wait_ge(s_edges, 64)
                    for t, d in ((e_i[0], src_d), (e_i[1], dst_d)):
                        sp.dma_start(d.rearrange("(p r) n -> p (r n)", r=4), t[:, :]).then_inc(s_dram, 16)
                    sp.wait_ge(s_vals, 1)
                    sp.dma_start(lo_d.rearrange("(p r) n -> p (r n)", r=4), fV[:, 2, :]).then_inc(s_vstore, 16)
                    sp.dma_start(dloc_d.rearrange("(p r) n -> p (r n)", r=4), fV[:, 3, :]).then_inc(s_vstore, 16)
                    sp.wait_ge(s_vstore, 32)

                @block.vector
                def _(dve):
                    link = Chain(dve, s_chain)
                    dve.memset(e_i[0][:, :], 0).then_inc(s_pad, 1)
                    dve.memset(e_i[1][:, :], NODES).then_inc(s_pad, 1)
                    link(dve.memset(b_r[:, :], -1.0))
                    dve.wait_ge(s_edges, 64)
                    link(dve.tensor_copy(dst_f[:, :], e_i[1][:, :]))
                    for b in range(1, BLOCKS):
                        dve.tensor_scalar(junk[:, :], dst_f[:, :], float(ROWS * b), None, ALU.is_lt, ALU.add,
                                          accum_out=cnt[:, b - 1:b]).then_inc(s_cnt, 1)
                        dve.wait_ge(s_cnt, b)
                    dve.wait_ge(s_cntps, 1)
                    dve.wait_ge(s_const, 6)
                    link(dve.tensor_copy(thr_i[:, 0, :], cnt_ps[:, 0:BLOCKS - 1]))
                    link(dve.tensor_scalar(thr_i[:, 1, :], thr_i[:, 0, :], 7, None, ALU.arith_shift_right))
                    link(dve.tensor_copy(thr[:, 0, :], thr_i[:, 1, :]))
                    link(dve.tensor_tensor(thr[:, 1, :], thr[:, 0, :], iota_row[:, 1:BLOCKS], ALU.add))
                    link(dve.tensor_tensor(cmp_v[:, :, :], visit_v[:, :].unsqueeze(2).broadcast_to([VP, 4, BLOCKS - 1]),
                                           thr[0:VP, 1, :].unsqueeze(1).broadcast_to([VP, 4, BLOCKS - 1]), ALU.is_ge))
                    link(dve.tensor_reduce(b_v[:, :], cmp_v[:, :, :], AX.X, ALU.add))
                    link(dve.tensor_tensor(tile_v[:, :], visit_v[:, :], b_v[:, :], ALU.subtract))
                    dve.tensor_copy(tile_i[:, :], tile_v[:, :]).then_inc(s_idx, 1)
                    link(dve.tensor_scalar(nb_v[:, :], b_v[:, :], float(ROWS), None, ALU.mult))
                    link(dve.tensor_tensor(cmp_r[:, :, :], visit_r[:, :].unsqueeze(2).broadcast_to([1, VISITS, BLOCKS - 1]),
                                           thr[0:1, 1, :].unsqueeze(1).broadcast_to([1, VISITS, BLOCKS - 1]), ALU.is_ge))
                    link(dve.tensor_reduce(b_r[:, 1:VISITS + 1], cmp_r[:, :, :], AX.X, ALU.add))
                    link(dve.tensor_tensor(flag_r[:, 0, :], b_r[:, 1:VISITS + 1], b_r[:, 0:VISITS], ALU.not_equal))
                    link(dve.tensor_tensor(flag_r[:, 1, :], b_r[:, 1:VISITS + 1], b_r[:, 2:VISITS + 2], ALU.not_equal))
                    link(dve.tensor_copy(block_r, b_r[:, 1:VISITS + 1]))
                    dve.tensor_copy(first_r, flag_r[:, 0, :])
                    dve.tensor_copy(last_r, flag_r[:, 1, :])
                    dve.tensor_scalar(par_r, block_r, 1, None, ALU.bitwise_and)
                    dve.wait_ge(s_vload, 128)
                    dve.tensor_scalar(bitsVi[:, 0, :], srcVi[:, :], 7, None, ALU.arith_shift_right)
                    link(dve.tensor_scalar(bitsVi[:, 1, :], srcVi[:, :], P - 1, None, ALU.bitwise_and))
                    dve.tensor_copy(fV[:, 0, :], srcVi[:, :])
                    dve.tensor_copy(fV[:, 1:3, :], bitsVi[:, :, :])
                    link(dve.tensor_copy(dstV[:, :], dstVi[:, :]))
                    for q in range(4):
                        ins = dve.tensor_scalar(fV[:, 3, q * P:(q + 1) * P], dstV[:, q * P:(q + 1) * P],
                                                nb_v[:, q:q + 1], None, ALU.subtract)
                    ins.then_inc(s_vals, 1)
                    dve.wait_ge(s_tr, 3)
                    for n, t in enumerate((srcT, hiT, dlocT)):
                        dve.tensor_copy(t[:, :].rearrange("k (p q) -> k q p", q=4), t_ps[:, n, :, 0:VP])

                @block.tensor
                def _(pe):
                    pe.wait_ge(s_cnt, BLOCKS - 1)
                    pe.wait_ge(s_const, 6)
                    pe.matmul(cnt_ps[:, 0:BLOCKS - 1], ones[0:98, :], cnt[:, :], start=True, stop=True).then_inc(s_cntps, 1)
                    pe.wait_ge(s_vals, 1)
                    for n, f in enumerate((0, 1, 3)):
                        for q in range(4):
                            ins = pe.transpose(t_ps[:, n, q, 0:VP], fV[:, f, q * P:(q + 1) * P], ident[0:VP, 0:VP])
                        ins.then_inc(s_tr, 1)

        with ExitStack() as c:
            Wp_sb = sbuf(c, "Wp_sb", [P, KD, D])
            sim_sb = sbuf(c, "sim_sb", [NX, D])
            simn = sbuf(c, "simn", [NX, D])
            sq = sbuf(c, "sim_sq", [NX, D])
            col = sbuf(c, "sim_col", [NX, 4])
            simT = sbuf(c, "simT", [P, KD, NX])
            w_ps = psum(c, "w_ps", [P, 4, 512])
            m_ps = psum(c, "m_ps", [P, 2, KD, NX])
            s_ld, s_c, s_n, s_sn = sem("rw_load"), sem("rw_chain"), sem("rw_norm"), sem("rw_sim")
            s_wt, s_we, s_st, s_se, s_m = sem("rw_wt"), sem("rw_wevac"), sem("rw_simt"), sem("rw_simevac"), sem("rw_m")
            with nc.Block() as block:
                @block.sync
                def _(sp):
                    sp.dma_start(sim_sb[:, :], sim).then_inc(s_ld, 16)
                    sp.dma_start(Wp_sb[:, :, :], Wp.rearrange("(k p) d -> p k d", p=P)).then_inc(s_ld, 16)

                @block.scalar
                def _(act):
                    act.wait_ge(s_c, 2)
                    act.activation(col[:, 1:2], col[:, 0:1], ACT.Sqrt).then_inc(s_n, 1)
                    for n in range(2 * KD):
                        act.wait_ge(s_wt, n + 1)
                        act.activation(WpT[:, n // 2, (n % 2) * 512:(n % 2 + 1) * 512], w_ps[:, n % 4, :],
                                       ACT.Copy).then_inc(s_we, 1)

                @block.vector
                def _(dve):
                    link = Chain(dve, s_c)
                    dve.wait_ge(s_ld, 32)
                    link(dve.tensor_tensor(sq[:, :], sim_sb[:, :], sim_sb[:, :], ALU.mult))
                    link(dve.tensor_reduce(col[:, 0:1], sq[:, :], AX.X, ALU.add))
                    dve.wait_ge(s_n, 1)
                    link(dve.tensor_scalar(col[:, 2:3], col[:, 1:2], NORM_EPS, None, ALU.max))
                    link(dve.reciprocal(col[:, 3:4], col[:, 2:3]))
                    dve.tensor_scalar(simn[:, :], sim_sb[:, :], col[:, 3:4], None, ALU.mult).then_inc(s_sn, 1)
                    dve.wait_ge(s_st, 1)
                    dve.tensor_copy(simT[:, :, :], m_ps[:, 0, :, :]).then_inc(s_se, 1)
                    dve.wait_ge(s_m, 1)
                    dve.tensor_copy(Msim[:, :, :], m_ps[:, 1, :, :])

                @block.tensor
                def _(pe):
                    pe.wait_ge(s_sn, 1)
                    for k in range(KD):
                        ins = pe.transpose(m_ps[:, 0, k, :], simn[:, k * P:(k + 1) * P], ident[0:NX, 0:NX])
                    ins.then_inc(s_st, 1)
                    pe.wait_ge(s_se, 1)
                    for k in range(KD):
                        for e in range(KD):
                            ins = pe.matmul(m_ps[:, 1, k, :], Wp_sb[:, e, k * P:(k + 1) * P], simT[:, e, :],
                                            start=(e == 0), stop=(e == KD - 1))
                    ins.then_inc(s_m, 1)
                    for n in range(2 * KD):
                        if n >= 4:
                            pe.wait_ge(s_we, n - 3)
                        for q in range(4):
                            e = (n % 2) * 4 + q
                            ins = pe.transpose(w_ps[:, n % 4, q * P:(q + 1) * P],
                                               Wp_sb[:, e, (n // 2) * P:(n // 2 + 1) * P], ident)
                        ins.then_inc(s_wt, 1)

        with ExitStack() as c:
            W_sb = sbuf(c, "W_sb", [P, KD, D])
            att = sbuf(c, "att", [ROWS, 2, D])
            xt = sbuf(c, "xt", [ROWS, 2, D])
            xn = sbuf(c, "xn", [ROWS, 2, D])
            xnT = sbuf(c, "xnT", [P, 2, KD, ROWS])
            xp = sbuf(c, "xp", [ROWS, 2, D])
            prod = sbuf(c, "prod", [ROWS, 2, D])
            stat = sbuf(c, "stat", [ROWS, 2, 2, 6])
            ln = sbuf(c, "ln", [ROWS, 2, 10])
            tr_ps = psum(c, "tr_ps", [P, KD, P])
            pj_ps = psum(c, "pj_ps", [P, 2, D])
            s_w, s_ln, s_var, s_std = sem("pj_w"), sem("pj_ln"), sem("pj_var"), sem("pj_std")
            s_x = [sem(f"pj_x{p}") for p in range(2)]
            s_xn, s_tr, s_xnT, s_mm, s_xp = sem("pj_xn"), sem("pj_tr"), sem("pj_xnT"), sem("pj_mm"), sem("pj_xp")
            s_prod, s_st = sem("pj_prod"), sem("pj_st")
            s_out = [sem(f"pj_out{p}") for p in range(2)]
            with nc.Block() as block:
                @block.sync
                def _(sp):
                    sp.dma_start(W_sb[:, :, :], W.rearrange("(k p) n -> p k n", p=P)).then_inc(s_w, 16)
                    for n, a in enumerate((att_src, att_dst)):
                        sp.dma_start(att[:, n, :], a.rearrange("h c -> (h c)").partition_broadcast(ROWS)).then_inc(s_w, 16)

                    def load(i, j, p):
                        if not early(i, 2):
                            sp.wait_ge(s_xn, i - 1)
                        sp.dma_start(xt[:, p, :], rows_of(x, i)).then_inc(s_x[p], 16)
                    steps(sp, BLOCKS, load)

                @block.gpsimd
                def _(pool):
                    def store(i, j, p):
                        pool.wait_ge(s_xp, i + 1)
                        pool.dma_start(rows_of(xp_d, i), xp[:, p, :]).then_inc(s_out[p], 16)
                    steps(pool, BLOCKS, store)
                    pool.wait_ge(s_out[0], 16 * (BLOCKS - BLOCKS // 2))
                    pool.wait_ge(s_out[1], 16 * (BLOCKS // 2))

                @block.scalar
                def _(act):
                    def evac_proj(i, p):
                        act.wait_ge(s_mm, i + 1)
                        if not early(i, 2):
                            act.wait_ge(s_st, i - 1)
                            act.wait_ge(s_out[p], 8 * i if p == 0 else 8 * (i - 1))
                        act.activation(xp[:, p, :], pj_ps[0:ROWS, p, :], ACT.Copy).then_inc(s_xp, 1)

                    def body(i, j, p):
                        act.wait_ge(s_var, i + 1)
                        act.activation(ln[:, p, 3:4], ln[:, p, 2:3], ACT.Sqrt).then_inc(s_std, 1)
                        act.wait_ge(s_tr, i + 1)
                        if not early(i, 2):
                            act.wait_ge(s_mm, i - 1)
                        act.activation(xnT[:, p, :, :], tr_ps[:, :, 0:ROWS], ACT.Copy).then_inc(s_xnT, 1)
                        if not early(i, 1):
                            evac_proj(i - 1, 1 - p)
                    steps(act, BLOCKS, body)
                    evac_proj(BLOCKS - 1, (BLOCKS - 1) % 2)

                @block.vector
                def _(dve):
                    def terms(i, p):
                        dve.wait_ge(s_xp, i + 1)
                        if not early(i, 1):
                            dve.wait_ge(s_st, i)
                        link = Chain(dve, s_prod, i)
                        for n in range(2):
                            ins = dve.tensor_tensor(prod[:, n, :], xp[:, p, :], att[:, n, :], ALU.mult)
                        link(ins)
                        dst_ap = (stN[:, i, :] if isinstance(i, int) else stN[:, bass.ds(i, 1), :].squeeze(1))
                        dve.tensor_reduce(dst_ap, prod[:, :, :].rearrange("r n (h c) -> r (n h) c", h=HEADS),
                                          AX.X, ALU.add).then_inc(s_st, 1)

                    def body(i, j, p):
                        dve.wait_ge(s_x[p], 16 * (j + 1))
                        layer_norm(dve, xt[:, p, :], xn[:, p, :], stat[:, p, :, :], ln[:, p, :], s_ln, s_var, s_std, s_met, i,
                                   None if early(i, 2) else (s_tr, i - 1), s_xn)
                        if early(i, 1):
                            return
                        terms(i - 1, 1 - p)
                    dve.wait_ge(s_w, 48)
                    steps(dve, BLOCKS, body)
                    terms(BLOCKS - 1, (BLOCKS - 1) % 2)

                @block.tensor
                def _(pe):
                    def turn(i, p):
                        pe.wait_ge(s_xn, i + 1)
                        if not early(i, 1):
                            pe.wait_ge(s_xnT, i)
                        for k in range(KD):
                            ins = pe.transpose(tr_ps[:, k, 0:ROWS], xn[:, p, k * P:(k + 1) * P], ident[0:ROWS, 0:ROWS])
                        ins.then_inc(s_tr, 1)

                    def body(i, j, p):
                        if not (isinstance(i, int) and i == BLOCKS - 1):
                            turn(i + 1, 1 - p)
                        pe.wait_ge(s_xnT, i + 1)
                        if not early(i, 2):
                            pe.wait_ge(s_xp, i - 1)
                        for n in range(2):
                            for k in range(KD):
                                ins = pe.matmul(pj_ps[0:ROWS, p, n * 512:(n + 1) * 512], xnT[:, p, k, :],
                                                W_sb[:, k, n * 512:(n + 1) * 512], start=(k == 0), stop=(k == KD - 1))
                        ins.then_inc(s_mm, 1)
                    turn(0, 0)
                    pe.wait_ge(s_w, 48)
                    steps(pe, BLOCKS, body)

        with ExitStack() as c:
            lo_tab = sbuf(c, "lo_tab", [P, HI, HEADS])
            lo_b = sbuf(c, "lo_b", [P, 2, CHUNK, P])
            dl_b = sbuf(c, "dl_b", [ROWS, 2, CHUNK, P])
            hi_oh = sbuf(c, "hi_oh", [P, 4, HI])
            pick = sbuf(c, "pick", [P, 4, HEADS, HI])
            sT = sbuf(c, "sT", [P, VISITS, HEADS])
            dT = sbuf(c, "dT", [P, VISITS, 2 * HEADS])
            s_ps = [psum(c, f"s_ps{n}", [P, 4, HI * HEADS]) for n in range(2)]
            d_ps = [psum(c, f"d_ps{n}", [P, 512]) for n in range(2)]
            s_stw, s_tab, s_zero = sem("ed_stw"), sem("ed_tab"), sem("ed_zero")
            s_row = [sem(f"ed_row{p}") for p in range(2)]
            s_oh, s_grp, s_got, s_sel = sem("ed_oh"), sem("ed_grp"), sem("ed_got"), sem("ed_sel")
            GR = CHUNK // 4
            with nc.Block() as block:
                @block.sync
                def _(sp):
                    sp.dma_start(st_d.rearrange("(b r) h -> r b h", r=ROWS), stN[:, :, :]).then_inc(s_stw, 16)
                    sp.wait_ge(s_stw, 16)
                    sp.wait_ge(s_zero, 1)
                    whole = NODES // P
                    sp.dma_start(lo_tab[:, 0:whole, :],
                                 st_d[0:whole * P, 0:HEADS].rearrange("(a p) h -> p a h", p=P)).then_inc(s_tab, 16)
                    sp.dma_start(lo_tab[0:NODES - whole * P, whole, :], st_d[whole * P:NODES, 0:HEADS]).then_inc(s_tab, 16)

                    def load(i, j, p):
                        if not early(i, 2):
                            sp.wait_ge(s_grp, GR * (i - 1))
                        for t, d, n in ((lo_b, lo_d, P), (dl_b, dloc_d, ROWS)):
                            part = d[CHUNK * i:CHUNK * (i + 1), :] if isinstance(i, int) else d[bass.ds(CHUNK * i, CHUNK), :]
                            sp.dma_start(t[:, p, :, :], part.partition_broadcast(n)).then_inc(s_row[p], 16)
                    steps(sp, 8, load)

                @block.vector
                def _(dve):
                    dve.memset(lo_tab[:, :, :], 0.0).then_inc(s_zero, 1)

                    def build(i, j, p):
                        dve.wait_ge(s_row[p], 32 * (j + 1))
                        dve.tensor_scalar(lo_b[:, p, :, :], lo_b[:, p, :, :], iota_col[:, 0:1], None, ALU.is_equal)
                        dve.tensor_scalar(dl_b[:, p, :, :], dl_b[:, p, :, :], iota_col[0:ROWS, 0:1], None,
                                          ALU.is_equal).then_inc(s_oh, 1)

                    def body(i, j, p):
                        if not (isinstance(i, int) and i == 7):
                            build(i + 1, j + p, 1 - p)
                        for q in range(GR):
                            n = GR * i + q
                            v = 4 * n
                            sl = slice(v, v + 4) if isinstance(v, int) else bass.ds(v, 4)
                            if not early(n, 1):
                                dve.wait_ge(s_got, n)
                            dve.tensor_tensor(hi_oh[:, :, :], iota_row[:, 0:HI].unsqueeze(1).broadcast_to([P, 4, HI]),
                                              hiT[:, sl].unsqueeze(2).broadcast_to([P, 4, HI]), ALU.is_equal).then_inc(s_sel, 1)
                            dve.wait_ge(s_sel, 2 * n + 1)
                            dve.wait_ge(s_grp, n + 1)
                            dve.tensor_tensor(pick[:, :, :, :], s_ps[(p + q) % 2][:, :, :].rearrange("k v (a h) -> k v h a", h=HEADS),
                                              hi_oh[:, :, :].unsqueeze(2).broadcast_to([P, 4, HEADS, HI]), ALU.mult).then_inc(s_sel, 1)
                            dve.wait_ge(s_sel, 2 * n + 2)
                            dve.tensor_reduce(sT[:, sl, :], pick[:, :, :, :], AX.X, ALU.add)
                            dve.tensor_copy(dT[:, sl, :], d_ps[(p + q) % 2][:, 0:8 * HEADS].rearrange("k (v h) -> k v h", v=4)).then_inc(s_got, 1)
                    build(0, 0, 0)
                    body(0, 0, 0)
                    with dve.Fori(0, 3) as j:
                        body(2 * j + 1, j, 1)
                        body(2 * j + 2, j + 1, 0)
                    body(7, 3, 1)

                @block.tensor
                def _(pe):
                    pe.wait_ge(s_tab, 32)

                    def body(i, j, p):
                        pe.wait_ge(s_oh, i + 1)
                        for q in range(GR):
                            n = GR * i + q
                            if not early(n, 2):
                                pe.wait_ge(s_got, n - 1)
                            for u in range(4):
                                v = 4 * n + u
                                pe.matmul(s_ps[(p + q) % 2][:, u, :], lo_b[:, p, 4 * q + u, :],
                                          lo_tab[:, :, :].rearrange("k a h -> k (a h)"), start=True, stop=True)
                                b = pe.value_load(block_r[:, v:v + 1] if isinstance(v, int) else block_r[:, bass.ds(v, 1)],
                                                  min_val=0, max_val=BLOCKS - 1)
                                ins = pe.matmul(d_ps[(p + q) % 2][:, 2 * HEADS * u:2 * HEADS * (u + 1)], dl_b[:, p, 4 * q + u, :],
                                                stN[:, bass.ds(b, 1), :].squeeze(1), start=True, stop=True)
                            ins.then_inc(s_grp, 1)
                    steps(pe, 8, body)

            with ExitStack() as c2:
                sV = lo_b[0:VP, 0, 0:4 * HEADS, :].rearrange("p (h q) k -> p h (q k)", h=HEADS)
                run = lo_b[0:VP, 0, 4 * HEADS:8 * HEADS, :].rearrange("p (h q) k -> p h (q k)", h=HEADS)
                run2 = lo_b[0:VP, 0, 8 * HEADS:12 * HEADS, :].rearrange("p (h q) k -> p h (q k)", h=HEADS)
                pen = sbuf(c2, "pen", [VP, 2, ROW4])
                ids = sbuf(c2, "ids", [VP, 2])
                cc = sbuf(c2, "cc", [VP, 2, 16])
                last4 = sbuf(c2, "last4", [VP, 2, 2, HEADS])
                sm = sbuf(c2, "sm", [HEADS, 2, 3, VP])
                carry = sbuf(c2, "carry", [VP, 2, 2, HEADS])
                spare = lo_b[:, 1, :, :].rearrange("k v n -> k (v n)")
                n_vh = VISITS * HEADS
                mT = spare[:, 0:n_vh].rearrange("k (v h) -> k v h", h=HEADS)
                work = spare[:, n_vh:3 * n_vh].rearrange("k (n v h) -> k n v h", n=2, h=HEADS)
                v_ps = [psum(c2, f"v_ps{h}", [P, 4, P]) for h in range(HEADS)]
                q_ps, r_ps = s_ps[0], s_ps[1]
                s_tv, s_ev, s_c, s_pq, s_dq, s_run, s_tb, s_d, s_e = (
                    sem("mx_tv"), sem("mx_ev"), sem("mx_chain"), sem("mx_pe"), sem("mx_dve"), sem("mx_run"),
                    sem("mx_tb"), sem("mx_d"), sem("mx_e"))
                with nc.Block() as block:
                    @block.tensor
                    def _(pe):
                        for h in range(HEADS):
                            for q in range(4):
                                ins = pe.transpose(v_ps[h][0:VP, q, :], sT[:, q::4, h], ident)
                            ins.then_inc(s_tv, 1)
                        flat = lambda t: t[:, :, :].rearrange("k v a -> k (v a)")
                        for w in range(2):
                            fwd = w == 0
                            hop = shifted[0:VP, 0:VP] if fwd else shifted[0:VP, 2:VP + 2]
                            src_id = ids[:, 1:2] if fwd else ids[:, 0:1]
                            pe.wait_ge(s_dq, 5 * w + 1)
                            pe.matmul(flat(q_ps)[0:VP, 0:1], hop, src_id, start=True, stop=True).then_inc(s_pq, 1)
                            pe.wait_ge(s_dq, 5 * w + 2)
                            pe.transpose(flat(r_ps)[0:HEADS, 0:VP], last4[:, w, 0, :], ident[0:VP, 0:VP])
                            pe.transpose(flat(r_ps)[0:HEADS, P:P + VP], last4[:, w, 1, :], ident[0:VP, 0:VP]).then_inc(s_pq, 1)
                            pe.wait_ge(s_dq, 5 * w + 3)
                            pe.transpose(flat(q_ps)[0:VP, 8:8 + HEADS], sm[:, w, 2, :], ident[0:HEADS, 0:HEADS]).then_inc(s_pq, 1)
                            pe.wait_ge(s_dq, 5 * w + 4)
                            pe.matmul(flat(q_ps)[0:VP, 16:16 + HEADS], hop, carry[:, w, 0, :], start=True, stop=True).then_inc(s_pq, 1)
                        pe.wait_ge(s_dq, 10)
                        for h in range(HEADS):
                            for q in range(4):
                                ins = pe.transpose(v_ps[h][:, q, 0:VP], run[:, h, q * P:(q + 1) * P], ident[0:VP, 0:VP])
                            ins.then_inc(s_tb, 1)

                    @block.scalar
                    def _(act):
                        for h in range(HEADS):
                            act.wait_ge(s_tv, h + 1)
                            act.activation(sV[:, h, :], v_ps[h][0:VP, :, :].rearrange("k q n -> k (q n)"), ACT.Copy).then_inc(s_ev, 1)
                        act.wait_ge(s_d, 1)
                        act.activation(PK[:, :, 1:1 + HEADS], work[:, 0, :, :], ACT.Exp).then_inc(s_e, 1)

                    @block.vector
                    def _(dve):
                        link = Chain(dve, s_c)
                        flat = lambda t: t[:, :, :].rearrange("k v a -> k (v a)")
                        dve.tensor_scalar(ids[:, 0:1], dstV[:, 0:1], 1.0, None, ALU.add)
                        dve.tensor_scalar(ids[:, 1:2], dstV[:, ROW4 - 1:ROW4], 1.0, None, ALU.add)
                        dve.memset(pen[:, :, :], 0.0)
                        link(dve.memset(PK[:, :, PACK - 1:PACK], 1.0))
                        link(dve.tensor_tensor(pen[:, 0, 1:ROW4], dstV[:, 1:ROW4], dstV[:, 0:ROW4 - 1], ALU.not_equal))
                        link(dve.tensor_copy(pen[:, 1, 0:ROW4 - 1], pen[:, 0, 1:ROW4]))
                        link(dve.tensor_scalar(pen[:, :, :], pen[:, :, :], -BIG, None, ALU.mult))
                        dve.wait_ge(s_ev, HEADS)
                        for w in range(2):
                            fwd = w == 0
                            turn = (lambda a: a) if fwd else (lambda a: a[:, ::-1])
                            data = sV if fwd else run2
                            res = run2 if fwd else run
                            end = ROW4 - 1 if fwd else 0
                            f_id, l_id = (ids[:, 0:1], ids[:, 1:2]) if fwd else (ids[:, 1:2], ids[:, 0:1])
                            k = cc[:, w, :]
                            for h in range(HEADS):
                                ins = dve.tensor_tensor_scan(turn(res[:, h, :]), turn(pen[:, w, :]), turn(data[:, h, :]), -BIG, ALU.add, ALU.max)
                            link(ins)
                            dve.tensor_copy(last4[:, w, 0, :], res[:, :, end]).then_inc(s_dq, 1)
                            dve.wait_ge(s_pq, 4 * w + 1)
                            link(dve.tensor_tensor(k[:, 0:1], flat(q_ps)[0:VP, 0:1], f_id, ALU.is_equal))
                            link(dve.tensor_tensor(k[:, 1:2], f_id, l_id, ALU.is_equal))
                            link(dve.tensor_tensor(k[:, 2:3], k[:, 0:1], k[:, 1:2], ALU.mult))
                            link(dve.tensor_scalar(k[:, 3:5], k[:, 0:3:2], -1.0, BIG, ALU.add, ALU.mult))
                            link(dve.tensor_copy(last4[:, w, 1, :], k[:, 4:5].broadcast_to([VP, HEADS])))
                            dve.tensor_copy(k[:, 8:9], k[:, 4:5]).then_inc(s_dq, 1)
                            dve.wait_ge(s_pq, 4 * w + 2)
                            dve.tensor_copy(sm[:, w, 0, :], flat(r_ps)[0:HEADS, 0:VP])
                            link(dve.tensor_copy(sm[:, w, 1, :], flat(r_ps)[0:HEADS, P:P + VP]))
                            dve.tensor_tensor_scan(turn(sm[:, w, 2, :]), turn(sm[:, w, 1, :]), turn(sm[:, w, 0, :]), -BIG, ALU.add, ALU.max).then_inc(s_dq, 1)
                            dve.wait_ge(s_pq, 4 * w + 3)
                            dve.tensor_copy(carry[:, w, 0, :], flat(q_ps)[0:VP, 8:8 + HEADS]).then_inc(s_dq, 1)
                            dve.wait_ge(s_pq, 4 * w + 4)
                            link(dve.tensor_scalar(carry[:, w, 1, :], flat(q_ps)[0:VP, 16:16 + HEADS], k[:, 3:4], None, ALU.add))
                            for h in range(HEADS):
                                ins = dve.tensor_tensor_scan(turn(res[:, h, :]), turn(pen[:, w, :]), turn(data[:, h, :]),
                                                             carry[:, w, 1, h:h + 1], ALU.add, ALU.max)
                            ins.then_inc(s_dq, 1)
                            dve.wait_ge(s_dq, 5 * w + 5)
                        for h in range(HEADS):
                            dve.wait_ge(s_tb, h + 1)
                            ins = dve.tensor_copy(mT[:, :, h].rearrange("k (p q) -> k q p", q=4), v_ps[h][:, :, 0:VP])
                        link(ins)
                        mx = PK[:, :, 1 + HEADS:1 + 2 * HEADS]
                        t_d = dT[:, :, HEADS:2 * HEADS]
                        dve.tensor_copy(PK[:, :, 0:1], dlocT[:, :].unsqueeze(2))
                        link(dve.tensor_tensor(mx, mT[:, :, :], dT[:, :, 0:HEADS], ALU.max))
                        link(dve.tensor_tensor(work[:, 0, :, :], mx, t_d, ALU.add))
                        link(dve.tensor_tensor(work[:, 1, :, :], sT[:, :, :], t_d, ALU.add))
                        fw = work[:, :, :, :].rearrange("k n v h -> k n (v h)")
                        link(dve.scalar_tensor_tensor(fw, fw, SLOPE, fw, ALU.mult, ALU.max))
                        link(dve.tensor_tensor(work[:, 0, :, :], work[:, 1, :, :], work[:, 0, :, :], ALU.subtract))
                        dve.tensor_scalar(work[:, 0, :, :], work[:, 0, :, :], 0.0, None, ALU.min).then_inc(s_d, 1)

        acc_ctx = ExitStack()
        if True:
            acc = sbuf(acc_ctx, "acc", [ROWS, BLOCKS, D])
            sacc = sbuf(acc_ctx, "sacc", [ROWS, BLOCKS, PACK - 1])
            c = ExitStack()
            with c:
                rows = sbuf(c, "rows", [P, 4, D])
                O = sbuf(c, "O", [P, 4, 1 + HEADS, ROWS])
                pk = sbuf(c, "pk", [P, 2, 4, PACK])
                idx = sbuf(c, "idx", [P, 2, 4], I32)
                main_ps = psum(c, "main_ps", [P, 2, D])
                small_ps = psum(c, "small_ps", [P, 2, 512])
                s_idx, s_done, s_pk, s_built, s_free = sem("ms_idx"), sem("ms_done"), sem("ms_pk"), sem("ms_built"), sem("ms_free")
                s_row = [sem(f"ms_row{k}") for k in range(4)]
                GROUPS = VISITS // 4
                with nc.Block() as block:
                    @block.gpsimd
                    def _(pool):
                        def body(i, j, p):
                            sl = slice(4 * i, 4 * i + 4) if isinstance(i, int) else bass.ds(4 * i, 4)
                            pool.tensor_copy(idx[:, p, :], srcT[:, sl]).then_inc(s_idx, 1)
                            wait_apart(pool, s_met, s_idx, i + 1)
                            for k in range(4):
                                if not early(i, 1):
                                    wait_apart(pool, s_met, s_done, 4 * i - 3 + k)
                                pool.indirect_dma_start(
                                    out=rows[:, k, :], out_offset=None, in_=xp_d[:, :],
                                    in_offset=bass.IndirectOffsetOnAxis(ap=idx[:, p, k:k + 1], axis=0)).then_inc(s_row[k], 16)
                        steps(pool, GROUPS, body)

                    @block.vector
                    def _(dve):
                        def evac(v):
                            dve.wait_ge(s_done, v + 1)
                            one = lambda r: r[:, v:v + 1] if isinstance(v, int) else r[:, bass.ds(v, 1)]
                            last = dve.value_load(one(last_r), min_val=0, max_val=1)
                            with dve.If(last == 1):
                                b = dve.value_load(one(block_r), min_val=0, max_val=BLOCKS - 1)
                                q = dve.value_load(one(par_r), min_val=0, max_val=1)
                                dve.tensor_copy(acc[:, bass.ds(b, 1), :], main_ps[0:ROWS, bass.ds(q, 1), :])
                                dve.tensor_copy(sacc[:, bass.ds(b, 1), :],
                                                small_ps[0:ROWS, bass.ds(q, 1), 0:PACK - 1]).then_inc(s_free, 1)
                            with dve.Else():
                                dve.nop()

                        def body(i, j, p):
                            sl = slice(4 * i, 4 * i + 4) if isinstance(i, int) else bass.ds(4 * i, 4)
                            if not early(i, 2):
                                dve.wait_ge(s_done, 4 * (i - 1))
                            dve.tensor_copy(pk[:, p, :, :], PK[:, sl, :]).then_inc(s_pk, 1)
                            dve.wait_ge(s_pk, i + 1)
                            for k in range(4):
                                if not early(i, 1):
                                    dve.wait_ge(s_done, 4 * i - 3 + k)
                                dve.tensor_scalar(O[:, k, 0, :], iota_row[:, 0:ROWS], pk[:, p, k, 0:1], None, ALU.is_equal)
                                for h in range(HEADS):
                                    ins = dve.tensor_scalar(O[:, k, 1 + h, :], iota_row[:, 0:ROWS], pk[:, p, k, 0:1],
                                                            pk[:, p, k, 1 + h:2 + h], ALU.is_equal, ALU.mult)
                                ins.then_inc(s_built, 1)
                                if not (early(i, 1) and k < 2):
                                    evac(4 * i + k - 2)
                        dve.memset(pk[:, 0, :, :], 0.0).then_inc(s_free, 1)
                        dve.memset(pk[:, 1, :, :], 0.0).then_inc(s_free, 1)
                        dve.wait_ge(s_free, 2)
                        steps(dve, GROUPS, body)
                        evac(VISITS - 2)
                        evac(VISITS - 1)

                    @block.tensor
                    def _(pe):
                        def products(p, k, q, first):
                            half = main_ps[0:ROWS, bass.ds(q, 1), :].squeeze(1)
                            pe.matmul(small_ps[0:ROWS, bass.ds(q, 1), 0:PACK - 1].squeeze(1), O[:, k, 0, :], pk[:, p, k, 1:PACK],
                                      start=first, stop=True, skip_group_check=True)
                            for h in range(HEADS):
                                ins = pe.matmul(half[:, h * C:(h + 1) * C], O[:, k, 1 + h, :], rows[:, k, h * C:(h + 1) * C],
                                                start=first and h % 2 == 0, stop=True, skip_group_check=True)
                            ins.then_inc(s_done, 1)

                        def body(i, j, p):
                            for k in range(4):
                                v = 4 * i + k
                                one = lambda r: r[:, v:v + 1] if isinstance(v, int) else r[:, bass.ds(v, 1)]
                                first = pe.value_load(one(first_r), min_val=0, max_val=1)
                                b = pe.value_load(one(block_r), min_val=0, max_val=BLOCKS - 1)
                                q = pe.value_load(one(par_r), min_val=0, max_val=1)
                                pe.wait_ge(s_built, v + 1)
                                pe.wait_ge(s_row[k], 16 * (i + 1))
                                with pe.If(first == 1):
                                    pe.wait_ge(s_free, b + 1)
                                    products(p, k, q, True)
                                with pe.Else():
                                    products(p, k, q, False)
                        steps(pe, GROUPS, body)

        with edge_ctx, acc_ctx:
            with ExitStack() as c:
                xt = sbuf(c, "n_xt", [ROWS, 2, D])
                own = sbuf(c, "n_own", [ROWS, 2, D])
                x2 = sbuf(c, "n_x2", [ROWS, 2, D])
                xn = sbuf(c, "n_xn", [ROWS, 2, D])
                spare = PK[:, :, :].rearrange("k v n -> k (v n)")
                xnT = spare[:, 0:2 * KD * ROWS].rearrange("k (p c r) -> k p c r", p=2, c=KD)
                bias_b = spare[0:ROWS, 2 * KD * ROWS:2 * KD * ROWS + D]
                stat = sbuf(c, "n_stat", [ROWS, 2, 2, 6])
                ln = sbuf(c, "n_ln", [ROWS, 2, 10])
                wk = sbuf(c, "n_wk", [ROWS, 4, BLOCKS, HEADS])
                cn = sbuf(c, "n_cn", [ROWS, 3, BLOCKS])
                tr_ps = psum(c, "n_tr", [P, KD, P])
                pj_ps = psum(c, "n_pj", [P, 2, D])
                sc_ps = psum(c, "n_sc", [P, 2, 512])
                s_b, s_ch, s_d, s_e = sem("nd_bias"), sem("nd_chain"), sem("nd_d"), sem("nd_e")
                s_x = [sem(f"nd_x{p}") for p in range(2)]
                s_own, s_x2c, s_x2, s_ln, s_var, s_std = sem("nd_own"), sem("nd_x2c"), sem("nd_x2"), sem("nd_ln"), sem("nd_var"), sem("nd_std")
                s_xn, s_tr, s_xnT, s_mm, s_sq, s_sc = sem("nd_xn"), sem("nd_tr"), sem("nd_xnT"), sem("nd_mm"), sem("nd_sq"), sem("nd_sc")
                s_out = [sem(f"nd_out{p}") for p in range(2)]
                w_own, z_inv = wk[:, 2, :, :], wk[:, 3, :, :]
                with nc.Block() as block:
                    @block.sync
                    def _(sp):
                        sp.dma_start(bias_b[:, :], bias.partition_broadcast(ROWS)).then_inc(s_b, 16)

                        def load(i, j, p):
                            if not early(i, 2):
                                sp.wait_ge(s_x2, i - 1)
                            sp.dma_start(xt[:, p, :], rows_of(x, i)).then_inc(s_x[p], 16)
                            sp.dma_start(own[:, p, :], rows_of(xp_d, i)).then_inc(s_x[p], 16)
                        steps(sp, BLOCKS, load)

                    @block.gpsimd
                    def _(pool):
                        def store(i, j, p):
                            pool.wait_ge(s_xn, i + 1)
                            pool.dma_start(rows_of(x2_d, i), x2[:, p, :]).then_inc(s_out[p], 16)
                            pool.dma_start(rows_of(x2n_d, i), xn[:, p, :]).then_inc(s_out[p], 16)
                        steps(pool, BLOCKS, store)
                        pool.wait_ge(s_out[0], 32 * (BLOCKS - BLOCKS // 2))
                        pool.wait_ge(s_out[1], 32 * (BLOCKS // 2))

                    @block.vector
                    def _(dve):
                        link = Chain(dve, s_ch)
                        s_n, t_n = stN[:, :, 0:HEADS], stN[:, :, HEADS:2 * HEADS]
                        wide = lambda a: a.unsqueeze(2).broadcast_to([ROWS, BLOCKS, HEADS])
                        link(dve.tensor_scalar(cn[:, 0, :], sacc[:, :, 2 * HEADS], 1.0, None, ALU.max))
                        link(dve.reciprocal(cn[:, 1, :], cn[:, 0, :]))
                        link(dve.tensor_scalar(cn[:, 0, :], sacc[:, :, 2 * HEADS], 1.0, None, ALU.min))
                        link(dve.tensor_scalar(cn[:, 2, :], cn[:, 0, :], -1.0, BIG, ALU.add, ALU.mult))
                        link(dve.tensor_tensor(wk[:, 0, :, :], sacc[:, :, HEADS:2 * HEADS], wide(cn[:, 1, :]), ALU.mult))
                        link(dve.tensor_tensor(wk[:, 0, :, :], wk[:, 0, :, :], wide(cn[:, 2, :]), ALU.add))
                        link(dve.tensor_tensor(wk[:, 0, :, :], wk[:, 0, :, :], s_n, ALU.max))
                        link(dve.tensor_tensor(wk[:, 0, :, :], wk[:, 0, :, :], t_n, ALU.add))
                        link(dve.tensor_tensor(wk[:, 1, :, :], s_n, t_n, ALU.add))
                        fl = wk[:, 0:2, :, :].rearrange("r n b h -> r (n b h)")
                        link(dve.scalar_tensor_tensor(fl, fl, SLOPE, fl, ALU.mult, ALU.max))
                        link(dve.tensor_tensor(wk[:, 0, :, :], wk[:, 1, :, :], wk[:, 0, :, :], ALU.subtract))
                        dve.tensor_scalar(wk[:, 1, :, :], wk[:, 0, :, :], 0.0, None, ALU.min).then_inc(s_d, 1)
                        dve.wait_ge(s_e, 1)
                        link(dve.tensor_tensor(wk[:, 1, :, :], wk[:, 0, :, :], sacc[:, :, 0:HEADS], ALU.add))
                        link(dve.reciprocal(z_inv, wk[:, 1, :, :]))
                        dve.tensor_tensor(w_own, wk[:, 0, :, :], z_inv, ALU.mult).then_inc(s_d, 1)
                        dve.wait_ge(s_b, 16)

                        def take_scores(i, p):
                            dve.wait_ge(s_mm, i + 1)
                            dve.tensor_copy(scores[:, i, :] if isinstance(i, int) else scores[:, bass.ds(i, 1), :].squeeze(1),
                                            sc_ps[0:ROWS, p, 0:NX]).then_inc(s_sc, 1)

                        def body(i, j, p):
                            link = Chain(dve, s_x2c, 2 * i)
                            dve.wait_ge(s_own, i + 1)
                            if not early(i, 2):
                                dve.wait_ge(s_out[p], 32 * j)
                            for h in range(HEADS):
                                sl = slice(h * C, (h + 1) * C)
                                a = acc[:, i, sl] if isinstance(i, int) else acc[:, bass.ds(i, 1), sl].squeeze(1)
                                z = z_inv[:, i, h:h + 1] if isinstance(i, int) else z_inv[:, bass.ds(i, 1), h:h + 1].squeeze(1)
                                ins = dve.scalar_tensor_tensor(x2[:, p, sl], a, z, own[:, p, sl], ALU.mult, ALU.add)
                            link(ins)
                            link(dve.tensor_tensor(own[:, p, :], x2[:, p, :], bias_b[:, :], ALU.add))
                            dve.scalar_tensor_tensor(x2[:, p, :], own[:, p, :], 0.0, xt[:, p, :], ALU.max, ALU.add).then_inc(s_x2, 1)
                            dve.wait_ge(s_x2, i + 1)
                            layer_norm(dve, x2[:, p, :], xn[:, p, :], stat[:, p, :, :], ln[:, p, :], s_ln, s_var, s_std, s_met, i,
                                       None if early(i, 2) else (s_tr, i - 1), s_xn)
                            if not early(i, 1):
                                take_scores(i - 1, 1 - p)
                        steps(dve, BLOCKS, body)
                        take_scores(BLOCKS - 1, (BLOCKS - 1) % 2)

                    @block.scalar
                    def _(act):
                        act.wait_ge(s_d, 1)
                        act.activation(wk[:, 0, :, :], wk[:, 1, :, :], ACT.Exp).then_inc(s_e, 1)
                        act.wait_ge(s_d, 2)

                        def square(i, p):
                            act.wait_ge(s_mm, i + 1)
                            act.activation(pj_ps[0:ROWS, p, :], pj_ps[0:ROWS, p, :], ACT.Square,
                                           accum_out=nsq[:, i:i + 1] if isinstance(i, int) else nsq[:, bass.ds(i, 1)]).then_inc(s_sq, 1)

                        def scale_own(i, j, p):
                            act.wait_ge(s_x[p], 32 * (j + 1))
                            for h in range(HEADS):
                                w = w_own[:, i, h:h + 1] if isinstance(i, int) else w_own[:, bass.ds(i, 1), h:h + 1].squeeze(1)
                                ins = act.activation(own[:, p, h * C:(h + 1) * C], own[:, p, h * C:(h + 1) * C], ACT.Copy, scale=w)
                            ins.then_inc(s_own, 1)

                        def body(i, j, p):
                            scale_own(i, j, p)
                            act.wait_ge(s_var, i + 1)
                            act.activation(ln[:, p, 3:4], ln[:, p, 2:3], ACT.Sqrt).then_inc(s_std, 1)
                            act.wait_ge(s_tr, i + 1)
                            if not early(i, 2):
                                act.wait_ge(s_mm, i - 1)
                            act.activation(xnT[:, p, :, :], tr_ps[:, :, 0:ROWS], ACT.Copy).then_inc(s_xnT, 1)
                            if not early(i, 1):
                                square(i - 1, 1 - p)
                        steps(act, BLOCKS, body)
                        square(BLOCKS - 1, (BLOCKS - 1) % 2)

                    @block.tensor
                    def _(pe):
                        def turn(i, p):
                            pe.wait_ge(s_xn, i + 1)
                            if not early(i, 1):
                                pe.wait_ge(s_xnT, i)
                            for k in range(KD):
                                ins = pe.transpose(tr_ps[:, k, 0:ROWS], xn[:, p, k * P:(k + 1) * P], ident[0:ROWS, 0:ROWS])
                            ins.then_inc(s_tr, 1)

                        def body(i, j, p):
                            if not (isinstance(i, int) and i == BLOCKS - 1):
                                turn(i + 1, 1 - p)
                            pe.wait_ge(s_xnT, i + 1)
                            if not early(i, 2):
                                pe.wait_ge(s_sq, i - 1)
                                pe.wait_ge(s_sc, i - 1)
                            for n in range(2):
                                for k in range(KD):
                                    pe.matmul(pj_ps[0:ROWS, p, n * 512:(n + 1) * 512], xnT[:, p, k, :],
                                              WpT[:, k, n * 512:(n + 1) * 512], start=(k == 0), stop=(k == KD - 1))
                            for k in range(KD):
                                ins = pe.matmul(sc_ps[0:ROWS, p, 0:NX], xnT[:, p, k, :], Msim[:, k, :],
                                                start=(k == 0), stop=(k == KD - 1))
                            ins.then_inc(s_mm, 1)
                        turn(0, 0)
                        steps(pe, BLOCKS, body)

        with ExitStack() as c:
            tcol = sbuf(c, "tcol", [ROWS, 2])
            rn = sbuf(c, "rn", [ROWS, 3, BLOCKS])
            top = sbuf(c, "top", [ROWS, BLOCKS, 8])
            top_u = sbuf(c, "top_u", [ROWS, BLOCKS, 8], U32)
            top_f = sbuf(c, "top_f", [ROWS, BLOCKS, 2])
            oh = sbuf(c, "oh", [ROWS, 2, BLOCKS, NX])
            both = sbuf(c, "both", [ROWS, BLOCKS, NX])
            strict = sbuf(c, "strict", [ROWS, ROWS])
            base = sbuf(c, "base", [ROWS, BLOCKS + 1, NX])
            tot = sbuf(c, "tot", [ROWS, BLOCKS, NX])
            pad_i = sbuf(c, "pad_i", [ROWS, 2, NX], I32)
            start_e = sbuf(c, "start_e", [ROWS, NX + 1])
            padded = sbuf(c, "padded", [ROWS, NX])
            place = sbuf(c, "place", [ROWS, BLOCKS, NX])
            hit = sbuf(c, "hit", [ROWS, 2, BLOCKS, NX])
            slot_f = sbuf(c, "slot_f", [ROWS, 2, BLOCKS])
            dif = sbuf(c, "dif", [ROWS, 3, BLOCKS])
            token = sbuf(c, "token", [ROWS, BLOCKS], I32)
            tile_r = sbuf(c, "tile_r", [1, XTILES])
            xcmp = sbuf(c, "xcmp", [1, XTILES, NX - 1])
            xe_f = sbuf(c, "xe_f", [1, XTILES])
            zero_i = sbuf(c, "zero_i", [XTILES, P], I32)
            b_ps = psum(c, "b_ps", [P, 2, 256])
            b_ps2 = psum(c, "b_ps2", [P, 2, 256])
            s_t, s_k, s_n, s_c, s_sm, s_em = sem("rt_temp"), sem("rt_const"), sem("rt_n"), sem("rt_chain"), sem("rt_sm"), sem("rt_em")
            s_oh, s_mm, s_slot, s_z, s_sc, s_q = sem("rt_oh"), sem("rt_mm"), sem("rt_slot"), sem("rt_zero"), sem("rt_scatter"), sem("rt_q")
            with nc.Block() as block:
                @block.sync
                def _(sp):
                    sp.dma_start(tcol[:, 0:1], temp.partition_broadcast(ROWS)).then_inc(s_t, 16)
                    sp.wait_ge(s_q, 1)
                    sp.dma_start(tok_d.rearrange("(a b) n -> a (b n)", b=P), zero_i[:, :]).then_inc(s_z, 16)

                @block.gpsimd
                def _(pool):
                    pool.memset(zero_i[:, :], 0).then_inc(s_q, 1)
                    pool.memset(strict[:, :], 1.0).then_inc(s_k, 1)
                    pool.iota(token[:, :], pattern=[[ROWS, BLOCKS]], base=0, channel_multiplier=1).then_inc(s_k, 1)
                    pool.iota(tile_r[:, :], pattern=[[P, XTILES]], base=0, channel_multiplier=0,
                              allow_small_or_imprecise_dtypes=True).then_inc(s_k, 1)
                    pool.wait_ge(s_k, 3)
                    pool.affine_select(out=strict[:, :], in_=strict[:, :], compare_op=ALU.is_gt, fill=0.0, base=0,
                                       pattern=[[1, ROWS]], channel_multiplier=-1).then_inc(s_k, 1)
                    pool.wait_ge(s_slot, 1)
                    pool.wait_ge(s_z, 16)
                    for b in range(BLOCKS):
                        for n in range(2):
                            pool.indirect_dma_start(out=tok_d[:, :], out_offset=bass.IndirectOffsetOnAxis(ap=slot_i[:, b, n:n + 1], axis=0),
                                                    in_=token[:, b:b + 1], in_offset=None).then_inc(s_sc, 16)
                    pool.wait_ge(s_sc, 32 * BLOCKS)

                @block.scalar
                def _(act):
                    act.activation(rn[:, 0, :], nsq[:, :], ACT.Sqrt).then_inc(s_n, 1)
                    act.wait_ge(s_sm, 1)
                    act.activation(dif[:, 1, :], dif[:, 0, :], ACT.Exp).then_inc(s_em, 1)

                @block.vector
                def _(dve):
                    link = Chain(dve, s_c)
                    wide = lambda a: a.unsqueeze(2).broadcast_to([ROWS, BLOCKS, NX])
                    dve.wait_ge(s_n, 1)
                    dve.wait_ge(s_t, 16)
                    link(dve.reciprocal(tcol[:, 1:2], tcol[:, 0:1]))
                    link(dve.tensor_scalar(rn[:, 1, :], rn[:, 0, :], NORM_EPS, None, ALU.max))
                    link(dve.reciprocal(rn[:, 2, :], rn[:, 1, :]))
                    link(dve.tensor_scalar(rn[:, 0, :], rn[:, 2, :], tcol[:, 1:2], None, ALU.mult))
                    link(dve.tensor_tensor(scores[:, :, :], scores[:, :, :], wide(rn[:, 0, :]), ALU.mult))
                    for b in range(BLOCKS):
                        ins = dve.max(top[:, b, :], scores[:, b, :])
                    link(ins)
                    for b in range(BLOCKS):
                        ins = dve.max_index(top_u[:, b, :], top[:, b, :], scores[:, b, :])
                    link(ins)
                    dve.tensor_tensor(dif[:, 0, :], top[:, :, 1], top[:, :, 0], ALU.subtract).then_inc(s_sm, 1)
                    link(dve.tensor_copy(top_f[:, :, :], top_u[:, :, 0:2]))
                    for n in range(2):
                        ins = dve.tensor_tensor(oh[:, n, :, :], iota_row[0:ROWS, 0:NX].unsqueeze(1).broadcast_to([ROWS, BLOCKS, NX]),
                                                wide(top_f[:, :, n]), ALU.is_equal)
                    link(ins)
                    dve.tensor_tensor(both[:, :, :], oh[:, 0, :, :], oh[:, 1, :, :], ALU.add).then_inc(s_oh, 1)
                    dve.memset(base[:, 0, :], 0.0)
                    dve.wait_ge(s_em, 1)
                    link(dve.tensor_scalar(dif[:, 2, :], dif[:, 1, :], 1.0, None, ALU.add))
                    link(dve.reciprocal(gates[:, :, 0], dif[:, 2, :]))
                    link(dve.tensor_tensor(gates[:, :, 1], gates[:, :, 0], dif[:, 1, :], ALU.mult))
                    for n in range(2):
                        ins = dve.tensor_tensor(hit[:, n, :, :], oh[:, n, :, :], wide(gates[:, :, n]), ALU.mult)
                    link(ins)
                    link(dve.tensor_tensor(comb[:, :, :], hit[:, 0, :, :], hit[:, 1, :, :], ALU.add))
                    dve.wait_ge(s_mm, 2)
                    link(dve.tensor_copy(tot[:, :, :], b_ps[0:ROWS, 0, 0:BLOCKS * NX].rearrange("r (b e) -> r b e", e=NX)))
                    for b in range(BLOCKS):
                        link(dve.tensor_tensor(base[:, b + 1, :], base[:, b, :], tot[:, b, :], ALU.add))
                    link(dve.tensor_scalar(padded[:, :], base[:, BLOCKS, :], float(P - 1), None, ALU.add))
                    link(dve.tensor_copy(pad_i[:, 0, :], padded[:, :]))
                    link(dve.tensor_scalar(pad_i[:, 1, :], pad_i[:, 0, :], -P, None, ALU.bitwise_and))
                    link(dve.memset(start_e[:, :], 0.0))
                    link(dve.tensor_copy(padded[:, :], pad_i[:, 1, :]))
                    for e in range(NX):
                        link(dve.tensor_tensor(start_e[:, e + 1:e + 2], start_e[:, e:e + 1], padded[:, e:e + 1], ALU.add))
                    link(dve.tensor_tensor(place[:, :, :], base[:, 0:BLOCKS, :],
                                           start_e[:, 0:NX].unsqueeze(1).broadcast_to([ROWS, BLOCKS, NX]), ALU.add))
                    link(dve.tensor_tensor(tot[:, :, :], place[:, :, :],
                                           b_ps2[0:ROWS, 0, 0:BLOCKS * NX].rearrange("r (b e) -> r b e", e=NX), ALU.add))
                    for n in range(2):
                        ins = dve.tensor_tensor(hit[:, n, :, :], oh[:, n, :, :], tot[:, :, :], ALU.mult)
                    link(ins)
                    link(dve.tensor_reduce(slot_f[:, :, :], hit[:, :, :, :], AX.X, ALU.add))
                    dve.tensor_copy(slot_i[:, :, :].rearrange("r b n -> r n b"), slot_f[:, :, :]).then_inc(s_slot, 1)
                    dve.wait_ge(s_k, 4)
                    link(dve.tensor_tensor(xcmp[:, :, :], tile_r[:, :].unsqueeze(2).broadcast_to([1, XTILES, NX - 1]),
                                           start_e[0:1, 1:NX].unsqueeze(1).broadcast_to([1, XTILES, NX - 1]), ALU.is_ge))
                    link(dve.tensor_reduce(xe_f[:, :], xcmp[:, :, :], AX.X, ALU.add))
                    dve.tensor_copy(xe_i[:, :], xe_f[:, :])

                @block.tensor
                def _(pe):
                    pe.wait_ge(s_oh, 1)
                    pe.wait_ge(s_k, 4)
                    flat = both[:, :, :].rearrange("r b e -> r (b e)")
                    pe.matmul(b_ps[0:ROWS, 0, 0:BLOCKS * NX], ones[0:ROWS, 0:ROWS], flat, start=True, stop=True).then_inc(s_mm, 1)
                    pe.matmul(b_ps2[0:ROWS, 0, 0:BLOCKS * NX], strict[:, :], flat, start=True, stop=True).then_inc(s_mm, 1)

        with ExitStack() as c:
            tok_r = sbuf(c, "tok_r", [XTILES, P], I32)
            tok_f = sbuf(c, "tok_f", [XTILES, P])
            tokT = sbuf(c, "tokT", [P, XTILES], I32)
            b1_r = sbuf(c, "b1_r", [NX * KF, P])
            b1T = sbuf(c, "b1T", [P, NX, KF])
            xi = sbuf(c, "xi", [P, 2, 1], I32)
            xg = sbuf(c, "xg", [P, 2, D])
            xgT = sbuf(c, "xgT", [P, 2, KD, P])
            w1 = sbuf(c, "w1", [P, 2, KD, FF])
            w2 = sbuf(c, "w2", [P, 2, KF, D])
            hT = sbuf(c, "hT", [P, 2, KF, P])
            eo = sbuf(c, "eo", [P, 2, D])
            tr_ps = psum(c, "x_tr", [P, KD, P])
            h_ps = psum(c, "x_h", [P, 2, KF, P])
            o_ps = psum(c, "x_o", [P, 2, D])
            s_ld, s_c, s_t0, s_xi = sem("xp_load"), sem("xp_chain"), sem("xp_t0"), sem("xp_xi")
            s_g = [sem(f"xp_g{p}") for p in range(2)]
            s_w = [sem(f"xp_w{p}") for p in range(2)]
            s_st = [sem(f"xp_st{p}") for p in range(2)]
            s_tr, s_xT, s_h, s_gel, s_o, s_eo = sem("xp_tr"), sem("xp_xT"), sem("xp_h"), sem("xp_gelu"), sem("xp_o"), sem("xp_eo")
            with nc.Block() as block:
                @block.sync
                def _(sp):
                    sp.dma_start(tok_r[:, :], tok_d.rearrange("(a b) n -> a (b n)", b=P)).then_inc(s_ld, 16)
                    sp.dma_start(b1_r[:, :], b1.rearrange("e (f p) -> (e f) p", p=P)).then_inc(s_ld, 16)

                    def body(i, j, p):
                        e = sp.value_load(xe_i[:, i:i + 1] if isinstance(i, int) else xe_i[:, bass.ds(i, 1)], min_val=0, max_val=NX - 1)
                        if not early(i, 2):
                            sp.wait_ge(s_o, i - 1)
                        sp.dma_start(w1[:, p, :, :], W1[bass.ds(e, 1), :, :].rearrange("a (k p) f -> p (a k) f", p=P)).then_inc(s_w[p], 16)
                        sp.dma_start(w2[:, p, :, :], W2[bass.ds(e, 1), :, :].rearrange("a (k p) f -> p (a k) f", p=P)).then_inc(s_w[p], 16)
                    steps(sp, XTILES, body)

                @block.gpsimd
                def _(pool):
                    pool.wait_ge(s_c, 2)

                    def store(i, j, p):
                        pool.wait_ge(s_eo, i + 1)
                        d = eo_d[P * i:P * (i + 1), :] if isinstance(i, int) else eo_d[bass.ds(P * i, P), :]
                        pool.dma_start(d, eo[:, p, :]).then_inc(s_st[p], 16)

                    def body(i, j, p):
                        if not early(i, 2):
                            pool.wait_ge(s_tr, i - 1)
                        pool.tensor_copy(xi[:, p, :], tokT[:, i:i + 1] if isinstance(i, int) else tokT[:, bass.ds(i, 1)]).then_inc(s_xi, 1)
                        wait_apart(pool, s_met, s_xi, i + 1)
                        pool.indirect_dma_start(out=xg[:, p, :], out_offset=None, in_=x2n_d[:, :],
                                                in_offset=bass.IndirectOffsetOnAxis(ap=xi[:, p, :], axis=0)).then_inc(s_g[p], 16)
                        if not early(i, 2):
                            store(i - 2, j, p)
                    steps(pool, XTILES, body)
                    store(XTILES - 2, 0, 0)
                    store(XTILES - 1, 0, 1)
                    pool.wait_ge(s_st[0], 8 * XTILES)
                    pool.wait_ge(s_st[1], 8 * XTILES)

                @block.vector
                def _(dve):
                    dve.wait_ge(s_ld, 32)
                    dve.tensor_copy(tok_f[:, :], tok_r[:, :]).then_inc(s_c, 1)
                    dve.wait_ge(s_t0, 1)
                    dve.tensor_copy(b1T[:, :, :].rearrange("p e f -> p (e f)"), o_ps[:, 0, 0:NX * KF])
                    dve.tensor_copy(tokT[:, :], o_ps[:, 1, 0:XTILES]).then_inc(s_c, 1)

                    def body(i, j, p):
                        dve.wait_ge(s_o, i + 1)
                        if not early(i, 2):
                            dve.wait_ge(s_st[p], 16 * j)
                        dve.tensor_copy(eo[:, p, :], o_ps[:, p, :]).then_inc(s_eo, 1)
                    steps(dve, XTILES, body)

                @block.scalar
                def _(act):
                    act.wait_ge(s_c, 2)

                    def gelu(i, p):
                        e = act.value_load(xe_i[:, i:i + 1] if isinstance(i, int) else xe_i[:, bass.ds(i, 1)], min_val=0, max_val=NX - 1)
                        act.wait_ge(s_h, i + 1)
                        if not early(i, 2):
                            act.wait_ge(s_o, i - 1)
                        for f in range(KF):
                            ins = act.activation(hT[:, p, f, :], h_ps[:, p, f, :], ACT.Gelu, bias=b1T[:, bass.ds(e, 1), f:f + 1].squeeze(1))
                        ins.then_inc(s_gel, 1)

                    def body(i, j, p):
                        act.wait_ge(s_tr, i + 1)
                        if not early(i, 2):
                            act.wait_ge(s_h, i - 1)
                        act.activation(xgT[:, p, :, :], tr_ps[:, :, :], ACT.Copy).then_inc(s_xT, 1)
                        if not early(i, 1):
                            gelu(i - 1, 1 - p)
                    steps(act, XTILES, body)
                    gelu(XTILES - 1, (XTILES - 1) % 2)

                @block.tensor
                def _(pe):
                    pe.wait_ge(s_c, 1)
                    pe.transpose(o_ps[:, 0, 0:NX * KF], b1_r[:, :], ident[0:NX * KF, 0:NX * KF])
                    pe.transpose(o_ps[:, 1, 0:XTILES], tok_f[:, :], ident[0:XTILES, 0:XTILES]).then_inc(s_t0, 1)
                    pe.wait_ge(s_c, 2)

                    def turn(i, p, g):
                        pe.wait_ge(s_g[p], g)
                        if not early(i, 1):
                            pe.wait_ge(s_xT, i)
                        for k in range(KD):
                            ins = pe.transpose(tr_ps[:, k, :], xg[:, p, k * P:(k + 1) * P], ident)
                        ins.then_inc(s_tr, 1)

                    def second(i, p):
                        pe.wait_ge(s_gel, i + 1)
                        if not early(i, 2):
                            pe.wait_ge(s_eo, i - 1)
                        for n in range(2):
                            for f in range(KF):
                                ins = pe.matmul(o_ps[:, p, n * 512:(n + 1) * 512], hT[:, p, f, :], w2[:, p, f, n * 512:(n + 1) * 512],
                                                start=(f == 0), stop=(f == KF - 1))
                        ins.then_inc(s_o, 1)

                    def body(i, j, p):
                        pe.wait_ge(s_xT, i + 1)
                        pe.wait_ge(s_w[p], 32 * (j + 1))
                        if not early(i, 2):
                            pe.wait_ge(s_gel, i - 1)
                        for f in range(KF):
                            for k in range(KD):
                                ins = pe.matmul(h_ps[:, p, f, :], w1[:, p, k, f * P:(f + 1) * P], xgT[:, p, k, :],
                                                start=(k == 0), stop=(k == KD - 1))
                        ins.then_inc(s_h, 1)
                        if not (isinstance(i, int) and i == XTILES - 1):
                            turn(i + 1, 1 - p, 16 * (j + 1 + p))
                        second(i, p)
                    turn(0, 0, 16)
                    steps_even(pe, XTILES, body)

        with ExitStack() as c:
            b2_sb = sbuf(c, "b2_sb", [NX, D])
            s_cs = sem("cb_comb")
            comb_s = sbuf(c, "comb_s", [ROWS, 2, NX])
            combT = sbuf(c, "combT", [NX, 2, ROWS])
            ci = sbuf(c, "ci", [ROWS, 2, 2], I32)
            x2 = sbuf(c, "c_x2", [ROWS, 2, D])
            r = [sbuf(c, f"c_r{n}", [ROWS, 2, D]) for n in range(2)]
            y = sbuf(c, "c_y", [ROWS, 2, D])
            t_ps = psum(c, "c_t", [P, 2, 512])
            b_ps = psum(c, "c_b", [P, 2, D])
            s_b2, s_ci, s_tr, s_cT, s_bb, s_y, s_yc = sem("cb_b2"), sem("cb_ci"), sem("cb_tr"), sem("cb_cT"), sem("cb_bb"), sem("cb_y"), sem("cb_yc")
            s_x = [sem(f"cb_x{p}") for p in range(2)]
            s_r = [sem(f"cb_r{p}") for p in range(2)]
            s_out = [sem(f"cb_out{p}") for p in range(2)]
            with nc.Block() as block:
                @block.sync
                def _(sp):
                    sp.dma_start(b2_sb[:, :], b2).then_inc(s_b2, 16)

                    def body(i, j, p):
                        if not early(i, 2):
                            sp.wait_ge(s_y, i - 1)
                        sp.dma_start(x2[:, p, :], rows_of(x2_d, i)).then_inc(s_x[p], 16)
                        if not early(i, 1):
                            store(i - 1, 1 - p)

                    def store(i, p):
                        sp.wait_ge(s_y, i + 1)
                        sp.dma_start(rows_of(out, i), y[:, p, :]).then_inc(s_out[p], 16)
                    steps(sp, BLOCKS, body)
                    store(BLOCKS - 1, (BLOCKS - 1) % 2)
                    sp.wait_ge(s_out[0], 16 * (BLOCKS - BLOCKS // 2))
                    sp.wait_ge(s_out[1], 16 * (BLOCKS // 2))

                @block.gpsimd
                def _(pool):
                    def body(i, j, p):
                        s = slot_i[:, i, :] if isinstance(i, int) else slot_i[:, bass.ds(i, 1), :].squeeze(1)
                        if not early(i, 2):
                            pool.wait_ge(s_y, i - 1)
                        pool.tensor_copy(ci[:, p, :], s).then_inc(s_ci, 1)
                        wait_apart(pool, s_met, s_ci, i + 1)
                        for n in range(2):
                            pool.indirect_dma_start(out=r[n][:, p, :], out_offset=None, in_=eo_d[:, :],
                                                    in_offset=bass.IndirectOffsetOnAxis(ap=ci[:, p, n:n + 1], axis=0)).then_inc(s_r[p], 16)
                    steps(pool, BLOCKS, body)

                @block.tensor
                def _(pe):
                    pe.wait_ge(s_b2, 16)

                    def body(i, j, p):
                        pe.wait_ge(s_cs, i + 1)
                        if not early(i, 2):
                            pe.wait_ge(s_cT, i - 1)
                        pe.transpose(t_ps[0:NX, p, 0:ROWS], comb_s[:, p, :], ident[0:ROWS, 0:ROWS]).then_inc(s_tr, 1)
                        pe.wait_ge(s_cT, i + 1)
                        if not early(i, 2):
                            pe.wait_ge(s_y, i - 1)
                        for n in range(2):
                            ins = pe.matmul(b_ps[0:ROWS, p, n * 512:(n + 1) * 512], combT[:, p, :], b2_sb[:, n * 512:(n + 1) * 512], start=True, stop=True)
                        ins.then_inc(s_bb, 1)

                    steps(pe, BLOCKS, body)

                @block.scalar
                def _(act):
                    def body(i, j, p):
                        cb = comb[:, i, :] if isinstance(i, int) else comb[:, bass.ds(i, 1), :].squeeze(1)
                        if not early(i, 2):
                            act.wait_ge(s_tr, i - 1)
                        act.activation(comb_s[:, p, :], cb, ACT.Copy).then_inc(s_cs, 1)
                        act.wait_ge(s_tr, i + 1)
                        if not early(i, 2):
                            act.wait_ge(s_bb, i - 1)
                        act.activation(combT[:, p, :], t_ps[0:NX, p, 0:ROWS], ACT.Copy).then_inc(s_cT, 1)
                    steps(act, BLOCKS, body)

                @block.vector
                def _(dve):
                    def body(i, j, p):
                        link = Chain(dve, s_yc, 2 * i)
                        g = lambda n: (gates[:, i, n:n + 1] if isinstance(i, int) else gates[:, bass.ds(i, 1), n:n + 1].squeeze(1))
                        dve.wait_ge(s_x[p], 16 * (j + 1))
                        dve.wait_ge(s_bb, i + 1)
                        if not early(i, 2):
                            dve.wait_ge(s_out[p], 16 * j)
                        link(dve.tensor_tensor(y[:, p, :], x2[:, p, :], b_ps[0:ROWS, p, :], ALU.add))
                        dve.wait_ge(s_r[p], 32 * (j + 1))
                        link(dve.scalar_tensor_tensor(y[:, p, :], r[0][:, p, :], g(0), y[:, p, :], ALU.mult, ALU.add))
                        dve.scalar_tensor_tensor(y[:, p, :], r[1][:, p, :], g(1), y[:, p, :], ALU.mult, ALU.add).then_inc(s_y, 1)
                    steps(dve, BLOCKS, body)


def steps_even(eng, n, body):
    body(0, 0, 0)
    body(1, 0, 1)
    with eng.Fori(1, n // 2 - 1) as j:
        body(2 * j, j, 0)
        body(2 * j + 1, j, 1)
    body(n - 2, n // 2 - 1, 0)
    body(n - 1, n // 2 - 1, 1)


def layer_norm(dve, xt, xn, stat, ln, s_ln, s_var, s_std, s_met, i, free, s_xn):
    link = Chain(dve, s_ln, 6 * i)
    dve.bn_stats(stat[:, 0, :], xt[:, 0:512])
    link(dve.bn_stats(stat[:, 1, :], xt[:, 512:1024]), s_met)
    link(dve.bn_aggr(ln[:, 0:2], stat))
    dve.tensor_scalar(ln[:, 2:3], ln[:, 1:2], LN_EPS, None, ALU.add).then_inc(s_var, 1)
    dve.wait_ge(s_std, i + 1)
    link(dve.reciprocal(ln[:, 4:5], ln[:, 3:4]))
    link(dve.tensor_scalar(ln[:, 5:6], ln[:, 4:5], ln[:, 4:5], ln[:, 2:3], ALU.mult, ALU.mult))
    link(dve.tensor_scalar(ln[:, 6:7], ln[:, 5:6], -0.5, 1.5, ALU.mult, ALU.add))
    link(dve.tensor_tensor(ln[:, 7:8], ln[:, 6:7], ln[:, 4:5], ALU.mult))
    if free is not None:
        dve.wait_ge(*free)
    dve.tensor_scalar(xn, xt, ln[:, 0:1], ln[:, 7:8], ALU.subtract, ALU.mult).then_inc(s_xn, 1)


_INS = ['x', 'src', 'dst', 'L0_gnn_W', 'L0_gnn_att_src', 'L0_gnn_att_dst', 'L0_gnn_bias', 'L0_ffn_Wp',
        'L0_ffn_sim_matrix', 'L0_ffn_temperature', 'L0_ffn_W1', 'L0_ffn_b1', 'L0_ffn_W2', 'L0_ffn_b2']


def kernel(**inputs):
    import numpy as _np
    import concourse.bacc as _bacc
    from concourse import mybir as _mybir
    from concourse.bass_utils import run_bass_kernel_spmd as _run

    nc = _bacc.Bacc("TRN2", target_bir_lowering=False, num_devices=1)
    arrays, args = {}, []
    for name in _INS:
        a = _np.ascontiguousarray(inputs[name])
        if a.ndim == 0:
            a = a.reshape(1)
        arrays[f"in_{name}_dram"] = a
        args.append(nc.dram_tensor(f"in_{name}_dram", a.shape, _mybir.dt.from_np(a.dtype), kind="ExternalInput").ap())
    args.append(nc.dram_tensor("out_0_dram", (NODES, D), F32, kind="ExternalOutput").ap())
    program(nc, *args)
    r = _run(nc, [arrays], core_ids=[0])
    return r.results[0]["out_0_dram"]
```

```python
from contextlib import ExitStack

import concourse.bass as bass
from concourse import mybir

F32 = mybir.dt.float32
I32 = mybir.dt.int32
U32 = mybir.dt.uint32
F16 = mybir.dt.float16
ALU = mybir.AluOpType
ACT = mybir.ActivationFunctionType
AX = mybir.AxisListType

P = 128
NODES, EDGES, D = 3125, 50000, 1024
HEADS, C = 4, 256
NX, FF = 8, 512
ROWS = 125
BLOCKS = NODES // ROWS
KD, KF = D // P, FF // P
TILES = -(-EDGES // P)
VISITS = TILES + BLOCKS
VP = VISITS // 4
ROW4 = 4 * P
CHUNK = VISITS // 8
HI = -(-NODES // P)
WS = 64.0
SUMS = 2 * HEADS + 1
PACK = 2 + 2 * SUMS
PAIRS = 2 * NODES
XTILES = (PAIRS + NX * P - 1) // P
WPIECES, WCOLS = 4, 2 * D * FF // P // 4
BIG = 1e30
LN_EPS = 1e-5
NORM_EPS = 1e-12
SLOPE = 0.2


def steps(eng, n, body):
    body(0, 0, 0)
    body(1, 0, 1)
    with eng.Fori(1, n // 2) as j:
        body(2 * j, j, 0)
        body(2 * j + 1, j, 1)
    if n % 2:
        body(n - 1, n // 2, 0)


def early(i, n):
    return isinstance(i, int) and i < n


def rows_of(t, i):
    if isinstance(i, int):
        return t[ROWS * i:ROWS * (i + 1), :]
    return t[bass.ds(ROWS * i, ROWS), :]


def at(t, i):
    return t[:, i] if isinstance(i, int) else t[:, bass.ds(i, 1)].squeeze(1)


def wait_apart(eng, met, sem, value):
    if not isinstance(value, int):
        eng.lower_val(value)
    eng.wait_ge(met, 1)
    eng.wait_ge(sem, value)


class Chain:

    def __init__(self, eng, sem, base=0):
        self.eng, self.sem, self.n = eng, sem, base

    def __call__(self, instruction, apart=None):
        instruction.then_inc(self.sem, 1)
        self.n = self.n + 1
        if apart is not None:
            wait_apart(self.eng, apart, self.sem, self.n)
        else:
            self.eng.wait_ge(self.sem, self.n)


def program(nc, x, src, dst, W, att_src, att_dst, bias, Wp, sim, temp, W1, b1, W2, b2, out):
    names = iter(range(1000))

    def dram(name, shape, dt=F32):
        return nc.dram_tensor(name, shape, dt).ap()

    src_d = dram("src_padded", (VISITS - BLOCKS + 1, P), I32)
    dst_d = dram("dst_padded", (VISITS - BLOCKS + 1, P), I32)
    lo_d = dram("src_lo_by_visit", (VISITS, P), F16)
    dloc_d = dram("dst_local_by_visit", (VISITS, P), F16)
    xp_d = dram("projected", (NODES, 2 * D), F16)
    st_d = dram("node_terms", (NODES, 4 * HEADS), F16)
    x2_d = dram("x_after_gnn", (NODES, D))
    x2n_d = dram("x_after_gnn_normed", (NODES, 2 * D), F16)
    tok_d = dram("token_of_slot", (XTILES * P, 1), I32)
    eo_d = dram("expert_rows", (XTILES * P, D))

    ctx = ExitStack()

    def sem(name):
        return ctx.enter_context(nc.semaphore(name))

    def sbuf(c, name, shape, dt=F32):
        return c.enter_context(nc.sbuf_tensor(name, shape, dt))

    def psum(c, name, shape):
        return c.enter_context(nc.psum_tensor(name, shape, F32))

    s_met = sem("always_met")

    with ctx:
        shifted = sbuf(ctx, "shifted", [P, P + 2])
        ident = shifted[:, 1:P + 1]
        iota_col = sbuf(ctx, "iota_col", [P, 1])
        unit = sbuf(ctx, "unit", [P, 1])
        iota_row = sbuf(ctx, "iota_row", [P, P])
        ones = sbuf(ctx, "ones", [P, P])
        rows_i = sbuf(ctx, "visit_rows", [1, 3, VISITS], I32)
        block_r, first_r, last_r = (rows_i[:, n, :] for n in range(3))
        WpT = sbuf(ctx, "WpT", [P, 2, KD, D], F16)
        Msim = sbuf(ctx, "Msim", [P, 2, KD, NX], F16)
        ident16 = sbuf(ctx, "ident16", [P, P], F16)
        iota16 = sbuf(ctx, "iota16", [P, P], F16)
        stN = sbuf(ctx, "node_terms_sb", [ROWS, BLOCKS, 2 * HEADS])
        nsq = sbuf(ctx, "proj_sq", [ROWS, BLOCKS])
        scores = sbuf(ctx, "scores", [ROWS, BLOCKS, NX])
        slot_i = sbuf(ctx, "slots", [ROWS, BLOCKS, 2], I32)
        gates = sbuf(ctx, "gates", [ROWS, BLOCKS, 2])
        comb = sbuf(ctx, "comb", [ROWS, BLOCKS, NX])
        x_i = sbuf(ctx, "tile_experts", [1, 3, XTILES], I32)

        edge_ctx = ExitStack()
        srcT = sbuf(edge_ctx, "srcT", [P, VISITS], I32)
        dlocT = sbuf(edge_ctx, "dlocT", [P, VISITS])
        PK = sbuf(edge_ctx, "PK", [P, VISITS, PACK], F16)
        early_ctx = ExitStack()
        hiT = sbuf(early_ctx, "hiT", [P, VISITS])
        dstV = sbuf(early_ctx, "dstV", [VP, ROW4])

        with ExitStack() as c:
            e_i = [sbuf(c, f"edges_i{n}", [98, ROW4], I32) for n in range(2)]
            dst_f = sbuf(c, "dst_f", [98, ROW4])
            junk = sbuf(c, "junk", [98, ROW4])
            cnt = sbuf(c, "cnt", [98, BLOCKS - 1])
            thr_i = sbuf(c, "thr_i", [P, 2, BLOCKS - 1], I32)
            thr = sbuf(c, "thr", [P, 2, BLOCKS - 1])
            visit_v = sbuf(c, "visit_v", [VP, 4])
            visit_r = sbuf(c, "visit_r", [1, VISITS])
            cmp_v = sbuf(c, "cmp_v", [VP, 4, BLOCKS - 1])
            cmp_r = sbuf(c, "cmp_r", [1, VISITS, BLOCKS - 1])
            b_v = sbuf(c, "b_v", [VP, 4])
            nb_v = sbuf(c, "nb_v", [VP, 4])
            tile_v = sbuf(c, "tile_v", [VP, 4])
            tile_i = sbuf(c, "tile_i", [VP, 4], I32)
            b_r = sbuf(c, "b_r", [1, VISITS + 2])
            flag_r = sbuf(c, "flag_r", [1, 2, VISITS])
            srcVi = sbuf(c, "srcVi", [VP, ROW4], I32)
            dstVi = sbuf(c, "dstVi", [VP, ROW4], I32)
            bitsVi = sbuf(c, "bitsVi", [VP, 2, ROW4], I32)
            fV = sbuf(c, "fV", [VP, 4, ROW4])
            rowV = sbuf(c, "rowV", [VP, 2, ROW4], F16)
            cnt_ps = psum(c, "cnt_ps", [P, 512])
            t_ps = psum(c, "t_ps", [P, 3, 4, P])
            s_const, s_pad, s_edges, s_dram = sem("ix_const"), sem("ix_pad"), sem("ix_edges"), sem("ix_dram")
            s_chain, s_cnt, s_cntps, s_idx = sem("ix_chain"), sem("ix_cnt"), sem("ix_cntps"), sem("ix_idx")
            s_vload, s_vals, s_tr, s_vstore = sem("ix_vload"), sem("ix_vals"), sem("ix_tr"), sem("ix_vstore")
            s_sel, s_rowv = sem("ix_sel"), sem("ix_rowv")
            full = (EDGES // ROW4)
            with nc.Block() as block:
                @block.gpsimd
                def _(pool):
                    pool.memset(shifted[:, :], 0.0).then_inc(s_sel, 1)
                    pool.memset(ones[:, :], 1.0).then_inc(s_const, 1)
                    pool.memset(unit[:, :], 1.0).then_inc(s_met, 1)
                    pool.iota(iota_col[:, :], pattern=[[0, 1]], base=0, channel_multiplier=1,
                              allow_small_or_imprecise_dtypes=True).then_inc(s_const, 1)
                    pool.iota(iota_row[:, :], pattern=[[1, P]], base=0, channel_multiplier=0,
                              allow_small_or_imprecise_dtypes=True).then_inc(s_const, 1)
                    pool.iota(visit_v[:, :], pattern=[[1, 4]], base=0, channel_multiplier=4,
                              allow_small_or_imprecise_dtypes=True).then_inc(s_const, 1)
                    pool.iota(visit_r[:, :], pattern=[[1, VISITS]], base=0, channel_multiplier=0,
                              allow_small_or_imprecise_dtypes=True).then_inc(s_const, 1)
                    pool.wait_ge(s_sel, 1)
                    pool.affine_select(out=shifted[:, :], in_=shifted[:, :], compare_op=ALU.not_equal,
                                       fill=1.0, base=1, pattern=[[-1, P + 2]],
                                       channel_multiplier=1).then_inc(s_const, 1)
                    pool.wait_ge(s_idx, 1)
                    pool.wait_ge(s_dram, 32)
                    for q in range(4):
                        for dram_t, sb_t in ((src_d, srcVi), (dst_d, dstVi)):
                            pool.indirect_dma_start(
                                out=sb_t[:, q * P:(q + 1) * P], out_offset=None, in_=dram_t[:, :],
                                in_offset=bass.IndirectOffsetOnAxis(ap=tile_i[:, q:q + 1], axis=0),
                            ).then_inc(s_vload, 16)

                @block.sync
                def _(sp):
                    sp.wait_ge(s_pad, 2)
                    for t, d in ((e_i[0], src), (e_i[1], dst)):
                        sp.dma_start(t[0:full, :], d[0:full * ROW4].rearrange("(p n) -> p n", n=ROW4)).then_inc(s_edges, 16)
                        sp.dma_start(t[full:full + 1, 0:EDGES - full * ROW4],
                                     d[full * ROW4:EDGES].rearrange("(a n) -> a n", a=1)).then_inc(s_edges, 16)
                    sp.wait_ge(s_edges, 64)
                    for t, d in ((e_i[0], src_d), (e_i[1], dst_d)):
                        sp.dma_start(d.rearrange("(p r) n -> p (r n)", r=4), t[:, :]).then_inc(s_dram, 16)
                    sp.wait_ge(s_rowv, 1)
                    sp.dma_start(lo_d.rearrange("(p r) n -> p (r n)", r=4), rowV[:, 0, :]).then_inc(s_vstore, 16)
                    sp.dma_start(dloc_d.rearrange("(p r) n -> p (r n)", r=4), rowV[:, 1, :]).then_inc(s_vstore, 16)
                    sp.wait_ge(s_vstore, 32)

                @block.vector
                def _(dve):
                    link = Chain(dve, s_chain)
                    dve.memset(e_i[0][:, :], 0).then_inc(s_pad, 1)
                    dve.memset(e_i[1][:, :], NODES).then_inc(s_pad, 1)
                    link(dve.memset(b_r[:, :], -1.0))
                    dve.wait_ge(s_edges, 64)
                    link(dve.tensor_copy(dst_f[:, :], e_i[1][:, :]))
                    for b in range(1, BLOCKS):
                        dve.tensor_scalar(junk[:, :], dst_f[:, :], float(ROWS * b), None, ALU.is_lt, ALU.add,
                                          accum_out=cnt[:, b - 1:b]).then_inc(s_cnt, 1)
                        dve.wait_ge(s_cnt, b)
                    dve.wait_ge(s_cntps, 1)
                    dve.wait_ge(s_const, 6)
                    link(dve.tensor_copy(thr_i[:, 0, :], cnt_ps[:, 0:BLOCKS - 1]))
                    link(dve.tensor_scalar(thr_i[:, 1, :], thr_i[:, 0, :], 7, None, ALU.arith_shift_right))
                    link(dve.tensor_copy(thr[:, 0, :], thr_i[:, 1, :]))
                    link(dve.tensor_tensor(thr[:, 1, :], thr[:, 0, :], iota_row[:, 1:BLOCKS], ALU.add))
                    link(dve.tensor_tensor(cmp_v[:, :, :], visit_v[:, :].unsqueeze(2).broadcast_to([VP, 4, BLOCKS - 1]),
                                           thr[0:VP, 1, :].unsqueeze(1).broadcast_to([VP, 4, BLOCKS - 1]), ALU.is_ge))
                    link(dve.tensor_reduce(b_v[:, :], cmp_v[:, :, :], AX.X, ALU.add))
                    link(dve.tensor_tensor(tile_v[:, :], visit_v[:, :], b_v[:, :], ALU.subtract))
                    dve.tensor_copy(tile_i[:, :], tile_v[:, :]).then_inc(s_idx, 1)
                    link(dve.tensor_scalar(nb_v[:, :], b_v[:, :], float(ROWS), None, ALU.mult))
                    link(dve.tensor_tensor(cmp_r[:, :, :], visit_r[:, :].unsqueeze(2).broadcast_to([1, VISITS, BLOCKS - 1]),
                                           thr[0:1, 1, :].unsqueeze(1).broadcast_to([1, VISITS, BLOCKS - 1]), ALU.is_ge))
                    link(dve.tensor_reduce(b_r[:, 1:VISITS + 1], cmp_r[:, :, :], AX.X, ALU.add))
                    link(dve.tensor_tensor(flag_r[:, 0, :], b_r[:, 1:VISITS + 1], b_r[:, 0:VISITS], ALU.not_equal))
                    link(dve.tensor_tensor(flag_r[:, 1, :], b_r[:, 1:VISITS + 1], b_r[:, 2:VISITS + 2], ALU.not_equal))
                    link(dve.tensor_copy(block_r, b_r[:, 1:VISITS + 1]))
                    dve.tensor_copy(first_r, flag_r[:, 0, :])
                    dve.tensor_copy(last_r, flag_r[:, 1, :])
                    dve.tensor_copy(ident16[:, :], ident)
                    dve.tensor_copy(iota16[:, :], iota_row[:, :])
                    dve.wait_ge(s_vload, 128)
                    dve.tensor_scalar(bitsVi[:, 0, :], srcVi[:, :], 7, None, ALU.arith_shift_right)
                    link(dve.tensor_scalar(bitsVi[:, 1, :], srcVi[:, :], P - 1, None, ALU.bitwise_and))
                    dve.tensor_copy(fV[:, 0, :], srcVi[:, :])
                    dve.tensor_copy(fV[:, 1:3, :], bitsVi[:, :, :])
                    link(dve.tensor_copy(dstV[:, :], dstVi[:, :]))
                    for q in range(4):
                        ins = dve.tensor_scalar(fV[:, 3, q * P:(q + 1) * P], dstV[:, q * P:(q + 1) * P],
                                                nb_v[:, q:q + 1], None, ALU.subtract)
                    ins.then_inc(s_vals, 1)
                    dve.wait_ge(s_vals, 1)
                    dve.tensor_copy(rowV[:, :, :], fV[:, 2:4, :]).then_inc(s_rowv, 1)
                    dve.wait_ge(s_tr, 3)
                    for n, t in enumerate((srcT, hiT, dlocT)):
                        dve.tensor_copy(t[:, :].rearrange("k (p q) -> k q p", q=4), t_ps[:, n, :, 0:VP])

                @block.tensor
                def _(pe):
                    pe.wait_ge(s_cnt, BLOCKS - 1)
                    pe.wait_ge(s_const, 6)
                    pe.matmul(cnt_ps[:, 0:BLOCKS - 1], ones[0:98, :], cnt[:, :], start=True, stop=True).then_inc(s_cntps, 1)
                    pe.wait_ge(s_vals, 1)
                    for n, f in enumerate((0, 1, 3)):
                        for q in range(4):
                            ins = pe.transpose(t_ps[:, n, q, 0:VP], fV[:, f, q * P:(q + 1) * P], ident[0:VP, 0:VP])
                        ins.then_inc(s_tr, 1)

        w_ctx = ExitStack()
        W_sb = sbuf(w_ctx, "W_sb", [P, 2, KD, D], F16)
        Watt = sbuf(w_ctx, "Watt", [P, 2, KD, 2 * HEADS], F16)
        with ExitStack() as c:
            Wp_f = sbuf(c, "Wp_f", [P, KD, D])
            W_f = sbuf(c, "W_f", [P, KD, D])
            att = sbuf(c, "att", [P, 2, D])
            prod = sbuf(c, "w_prod", [P, 2, D])
            watt_f = sbuf(c, "watt_f", [P, KD, 2 * HEADS])
            sim_sb = sbuf(c, "sim_sb", [NX, D])
            simn = sbuf(c, "simn", [NX, D])
            sq = sbuf(c, "sim_sq", [NX, D])
            col = sbuf(c, "sim_col", [NX, 4])
            simT = sbuf(c, "simT", [P, KD, NX])
            w_ps = psum(c, "w_ps", [P, 4, 512])
            m_ps = psum(c, "m_ps", [P, 2, KD, NX])
            s_sim, s_ldp, s_ldw, s_c, s_n, s_sn = sem("rw_sim_in"), sem("rw_wp_in"), sem("rw_w_in"), sem("rw_chain"), sem("rw_norm"), sem("rw_sim")
            s_wt, s_we, s_wl, s_st, s_se, s_m = sem("rw_wt"), sem("rw_whi"), sem("rw_wlo"), sem("rw_simt"), sem("rw_simevac"), sem("rw_m")
            s_wh, s_pr = sem("rw_w_hi"), sem("rw_prod")
            with nc.Block() as block:
                @block.sync
                def _(sp):
                    sp.dma_start(sim_sb[:, :], sim).then_inc(s_sim, 16)
                    sp.dma_start(Wp_f[:, :, :], Wp.rearrange("(k p) d -> p k d", p=P)).then_inc(s_ldp, 16)
                    sp.dma_start(W_f[:, :, :], W.rearrange("(k p) n -> p k n", p=P)).then_inc(s_ldw, 16)
                    for n, a in enumerate((att_src, att_dst)):
                        sp.dma_start(att[:, n, :], a.rearrange("h c -> (h c)").partition_broadcast(P)).then_inc(s_ldw, 16)

                @block.scalar
                def _(act):
                    act.wait_ge(s_c, 2)
                    act.activation(col[:, 1:2], col[:, 0:1], ACT.Sqrt).then_inc(s_n, 1)
                    for n in range(2 * KD):
                        act.wait_ge(s_wt, n + 1)
                        act.activation(WpT[:, 0, n // 2, (n % 2) * 512:(n % 2 + 1) * 512], w_ps[:, n % 4, :],
                                       ACT.Copy, scale=WS).then_inc(s_we, 1)
                    act.wait_ge(s_ldw, 48)
                    for k in range(KD):
                        act.activation(W_sb[:, 0, k, :], W_f[:, k, :], ACT.Copy, scale=WS).then_inc(s_wh, 1)

                @block.vector
                def _(dve):
                    link = Chain(dve, s_c)
                    dve.wait_ge(s_sim, 16)
                    link(dve.tensor_tensor(sq[:, :], sim_sb[:, :], sim_sb[:, :], ALU.mult))
                    link(dve.tensor_reduce(col[:, 0:1], sq[:, :], AX.X, ALU.add))
                    dve.wait_ge(s_n, 1)
                    link(dve.tensor_scalar(col[:, 2:3], col[:, 1:2], NORM_EPS, None, ALU.max))
                    link(dve.reciprocal(col[:, 3:4], col[:, 2:3]))
                    dve.tensor_scalar(simn[:, :], sim_sb[:, :], col[:, 3:4], None, ALU.mult).then_inc(s_sn, 1)
                    dve.wait_ge(s_st, 1)
                    dve.tensor_copy(simT[:, :, :], m_ps[:, 0, :, :]).then_inc(s_se, 1)
                    for n in range(2 * KD):
                        dve.wait_ge(s_we, n + 1)
                        cols = slice((n % 2) * 512, (n % 2 + 1) * 512)
                        dve.scalar_tensor_tensor(WpT[:, 1, n // 2, cols], w_ps[:, n % 4, :], WS, WpT[:, 0, n // 2, cols],
                                                 ALU.mult, ALU.subtract).then_inc(s_wl, 1)
                    dve.wait_ge(s_m, 1)
                    link(dve.tensor_scalar(Msim[:, 0, :, :], m_ps[:, 1, :, :], WS, None, ALU.mult))
                    dve.scalar_tensor_tensor(Msim[:, 1, :, :], m_ps[:, 1, :, :], WS, Msim[:, 0, :, :], ALU.mult, ALU.subtract)
                    dve.wait_ge(s_ldw, 48)
                    for k in range(KD):
                        if k:
                            dve.wait_ge(s_pr, 2 * k)
                        for n in range(2):
                            ins = dve.tensor_tensor(prod[:, n, :], W_f[:, k, :], att[:, n, :], ALU.mult)
                        ins.then_inc(s_pr, 1)
                        dve.wait_ge(s_pr, 2 * k + 1)
                        dve.tensor_reduce(watt_f[:, k, :], prod[:, :, :].rearrange("r n (h c) -> r (n h) c", h=HEADS),
                                          AX.X, ALU.add).then_inc(s_pr, 1)
                        dve.wait_ge(s_wh, k + 1)
                        dve.scalar_tensor_tensor(W_sb[:, 1, k, :], W_f[:, k, :], WS, W_sb[:, 0, k, :], ALU.mult, ALU.subtract)
                    dve.wait_ge(s_pr, 2 * KD)
                    link(dve.tensor_scalar(Watt[:, 0, :, :], watt_f[:, :, :], WS, None, ALU.mult))
                    dve.scalar_tensor_tensor(Watt[:, 1, :, :], watt_f[:, :, :], WS, Watt[:, 0, :, :], ALU.mult, ALU.subtract)

                @block.tensor
                def _(pe):
                    pe.wait_ge(s_sn, 1)
                    for k in range(KD):
                        ins = pe.transpose(m_ps[:, 0, k, :], simn[:, k * P:(k + 1) * P], ident[0:NX, 0:NX])
                    ins.then_inc(s_st, 1)
                    pe.wait_ge(s_ldp, 16)
                    for n in range(2 * KD):
                        if n >= 4:
                            pe.wait_ge(s_wl, n - 3)
                        for q in range(4):
                            e = (n % 2) * 4 + q
                            ins = pe.transpose(w_ps[:, n % 4, q * P:(q + 1) * P],
                                               Wp_f[:, e, (n // 2) * P:(n // 2 + 1) * P], ident)
                        ins.then_inc(s_wt, 1)
                    pe.wait_ge(s_se, 1)
                    for k in range(KD):
                        for e in range(KD):
                            ins = pe.matmul(m_ps[:, 1, k, :], Wp_f[:, e, k * P:(k + 1) * P], simT[:, e, :],
                                            start=(e == 0), stop=(e == KD - 1))
                    ins.then_inc(s_m, 1)

        with w_ctx, ExitStack() as c:
            xt = sbuf(c, "xt", [ROWS, 2, D])
            xn = sbuf(c, "xn", [ROWS, D])
            xs = sbuf(c, "xs", [ROWS, 2, 2, D], F16)
            xsT = sbuf(c, "xsT", [P, 2, 2, KD, ROWS], F16)
            xp = sbuf(c, "xp", [ROWS, 2, 2, D], F16)
            stat = sbuf(c, "stat", [ROWS, 2, 2, 6])
            ln = sbuf(c, "ln", [ROWS, 2, 10])
            tr_ps = c.enter_context(nc.psum_tensor("tr_ps", [P, 2, KD, P], F16))
            pj_ps = psum(c, "pj_ps", [P, 2, D])
            st_ps = psum(c, "st_ps", [P, 2, 512])
            s_ln, s_var, s_std = sem("pj_ln"), sem("pj_var"), sem("pj_std")
            s_x = [sem(f"pj_x{p}") for p in range(2)]
            s_xf, s_xh, s_xn, s_tr, s_xnT, s_mm, s_xp, s_lo = (
                sem("pj_xf"), sem("pj_xh"), sem("pj_xn"), sem("pj_tr"), sem("pj_xnT"), sem("pj_mm"), sem("pj_xp"), sem("pj_lo"))
            s_out = [sem(f"pj_out{p}") for p in range(2)]
            with nc.Block() as block:
                @block.sync
                def _(sp):
                    def load(i, j, p):
                        if not early(i, 2):
                            sp.wait_ge(s_xf, i - 1)
                        sp.dma_start(xt[:, p, :], rows_of(x, i)).then_inc(s_x[p], 16)
                    steps(sp, BLOCKS, load)

                @block.gpsimd
                def _(pool):
                    def store(i, j, p):
                        pool.wait_ge(s_lo, i + 1)
                        pool.dma_start(rows_of(xp_d, i), xp[:, p, :, :].rearrange("r n d -> r (n d)")).then_inc(s_out[p], 16)
                    steps(pool, BLOCKS, store)
                    pool.wait_ge(s_out[0], 16 * (BLOCKS - BLOCKS // 2))
                    pool.wait_ge(s_out[1], 16 * (BLOCKS // 2))

                @block.scalar
                def _(act):
                    def hi_proj(i, p):
                        act.wait_ge(s_mm, i + 1)
                        if not early(i, 2):
                            act.wait_ge(s_out[p], 8 * i if p == 0 else 8 * (i - 1))
                        act.activation(xp[:, p, 0, :], pj_ps[0:ROWS, p, :], ACT.Copy, scale=1.0 / WS).then_inc(s_xp, 1)

                    def body(i, j, p):
                        act.wait_ge(s_var, i + 1)
                        act.activation(ln[:, p, 3:4], ln[:, p, 2:3], ACT.Sqrt).then_inc(s_std, 1)
                        act.wait_ge(s_xf, i + 1)
                        if not early(i, 2):
                            act.wait_ge(s_tr, i - 1)
                        act.activation(xs[:, p, 0, :], xn[:, :], ACT.Copy).then_inc(s_xh, 1)
                        act.wait_ge(s_tr, i + 1)
                        if not early(i, 2):
                            act.wait_ge(s_mm, i - 1)
                        act.activation(xsT[:, p, :, :, :], tr_ps[:, :, :, 0:ROWS], ACT.Copy).then_inc(s_xnT, 1)
                        if not early(i, 1):
                            hi_proj(i - 1, 1 - p)
                    steps(act, BLOCKS, body)
                    hi_proj(BLOCKS - 1, (BLOCKS - 1) % 2)

                @block.vector
                def _(dve):
                    def lo_proj(i, p):
                        dve.wait_ge(s_xp, i + 1)
                        dve.tensor_scalar(at(stN, i), st_ps[0:ROWS, p, 0:2 * HEADS], 1.0 / WS, None, ALU.mult)
                        dve.scalar_tensor_tensor(xp[:, p, 1, :], pj_ps[0:ROWS, p, :], 1.0 / WS, xp[:, p, 0, :],
                                                 ALU.mult, ALU.subtract).then_inc(s_lo, 1)

                    def body(i, j, p):
                        dve.wait_ge(s_x[p], 16 * (j + 1))
                        layer_norm(dve, xt[:, p, :], xn[:, :], xs[:, p, :, :], stat[:, p, :, :], ln[:, p, :],
                                   s_ln, s_var, s_std, s_met, s_xf, s_xh, s_xn, i)
                        if not early(i, 1):
                            lo_proj(i - 1, 1 - p)
                    steps(dve, BLOCKS, body)
                    lo_proj(BLOCKS - 1, (BLOCKS - 1) % 2)

                @block.tensor
                def _(pe):
                    def turn(i, p):
                        pe.wait_ge(s_xn, i + 1)
                        if not early(i, 1):
                            pe.wait_ge(s_xnT, i)
                        turn_parts(pe, tr_ps, xs[:, p, :, :], ident16).then_inc(s_tr, 1)

                    def body(i, j, p):
                        pe.wait_ge(s_xnT, i + 1)
                        if not early(i, 2):
                            pe.wait_ge(s_lo, i - 1)
                        lhs = xsT[:, p, :, :, :]
                        product(pe, pj_ps[0:ROWS, p, 0:512], lhs, W_sb[:, :, :, 0:512], range(KD), KD)
                        product(pe, st_ps[0:ROWS, p, 0:2 * HEADS], lhs, Watt[:, :, :, :], range(KD), KD)
                        product(pe, pj_ps[0:ROWS, p, 512:D], lhs, W_sb[:, :, :, 512:D], range(KD // 2), KD)
                        if not (isinstance(i, int) and i == BLOCKS - 1):
                            turn(i + 1, 1 - p)
                        product(pe, pj_ps[0:ROWS, p, 512:D], lhs, W_sb[:, :, :, 512:D], range(KD // 2, KD), KD).then_inc(s_mm, 1)
                    turn(0, 0)
                    steps(pe, BLOCKS, body)

        with ExitStack() as c:
            st16 = sbuf(c, "node_terms_parts", [ROWS, BLOCKS, 4 * HEADS], F16)
            lo_tab = sbuf(c, "lo_tab", [P, HI, 4 * HEADS], F16)
            lo_b = sbuf(c, "lo_b", [P, 2, CHUNK, P], F16)
            dl_b = sbuf(c, "dl_b", [ROWS, 2, CHUNK, P], F16)
            hi_oh = sbuf(c, "hi_oh", [P, 4, HI])
            pick = sbuf(c, "pick", [P, 4, HEADS, HI])
            sT = sbuf(c, "sT", [P, VISITS, HEADS])
            dT = sbuf(c, "dT", [P, VISITS, 2 * HEADS])
            s_ps = [psum(c, f"s_ps{n}", [P, 4, HI * HEADS]) for n in range(2)]
            d_ps = [psum(c, f"d_ps{n}", [P, 512]) for n in range(2)]
            s_stw, s_tab, s_zero, s_st16 = sem("ed_stw"), sem("ed_tab"), sem("ed_zero"), sem("ed_st16")
            s_row = [sem(f"ed_row{p}") for p in range(2)]
            s_oh, s_grp, s_got, s_sel = sem("ed_oh"), sem("ed_grp"), sem("ed_got"), sem("ed_sel")
            GR = CHUNK // 4
            with nc.Block() as block:
                @block.sync
                def _(sp):
                    sp.wait_ge(s_st16, 2)
                    sp.dma_start(st_d.rearrange("(b r) h -> r b h", r=ROWS), st16[:, :, :]).then_inc(s_stw, 16)
                    sp.wait_ge(s_stw, 16)
                    sp.wait_ge(s_zero, 1)
                    whole = NODES // P
                    sp.dma_start(lo_tab[:, 0:whole, :],
                                 st_d[0:whole * P, :].rearrange("(a p) h -> p a h", p=P)).then_inc(s_tab, 16)
                    sp.dma_start(lo_tab[0:NODES - whole * P, whole, :], st_d[whole * P:NODES, :]).then_inc(s_tab, 16)

                    def load(i, j, p):
                        if not early(i, 2):
                            sp.wait_ge(s_grp, GR * (i - 1))
                        for t, d, n in ((lo_b, lo_d, P), (dl_b, dloc_d, ROWS)):
                            part = d[CHUNK * i:CHUNK * (i + 1), :] if isinstance(i, int) else d[bass.ds(CHUNK * i, CHUNK), :]
                            sp.dma_start(t[:, p, :, :], part.partition_broadcast(n)).then_inc(s_row[p], 16)
                    steps(sp, 8, load)

                @block.vector
                def _(dve):
                    dve.memset(lo_tab[:, :, :], 0.0).then_inc(s_zero, 1)
                    dve.tensor_copy(st16[:, :, 0:2 * HEADS], stN[:, :, :]).then_inc(s_st16, 1)
                    dve.wait_ge(s_st16, 1)
                    dve.tensor_tensor(st16[:, :, 2 * HEADS:], stN[:, :, :], st16[:, :, 0:2 * HEADS], ALU.subtract).then_inc(s_st16, 1)

                    def build(i, j, p):
                        dve.wait_ge(s_row[p], 32 * (j + 1))
                        dve.tensor_scalar(lo_b[:, p, :, :], lo_b[:, p, :, :], iota_col[:, 0:1], None, ALU.is_equal)
                        dve.tensor_scalar(dl_b[:, p, :, :], dl_b[:, p, :, :], iota_col[0:ROWS, 0:1], None,
                                          ALU.is_equal).then_inc(s_oh, 1)

                    def body(i, j, p):
                        for q in range(GR):
                            if q == GR - 4 and not (isinstance(i, int) and i == 7):
                                build(i + 1, j + p, 1 - p)
                            n = GR * i + q
                            v = 4 * n
                            sl = slice(v, v + 4) if isinstance(v, int) else bass.ds(v, 4)
                            if not early(n, 1):
                                dve.wait_ge(s_got, n)
                            dve.tensor_tensor(hi_oh[:, :, :], iota_row[:, 0:HI].unsqueeze(1).broadcast_to([P, 4, HI]),
                                              hiT[:, sl].unsqueeze(2).broadcast_to([P, 4, HI]), ALU.is_equal).then_inc(s_sel, 1)
                            dve.wait_ge(s_sel, 2 * n + 1)
                            dve.wait_ge(s_grp, n + 1)
                            dve.tensor_tensor(pick[:, :, :, :], s_ps[(p + q) % 2][:, :, :].rearrange("k v (a h) -> k v h a", h=HEADS),
                                              hi_oh[:, :, :].unsqueeze(2).broadcast_to([P, 4, HEADS, HI]), ALU.mult).then_inc(s_sel, 1)
                            dve.wait_ge(s_sel, 2 * n + 2)
                            dve.tensor_reduce(sT[:, sl, :], pick[:, :, :, :], AX.X, ALU.add)
                            dve.tensor_copy(dT[:, sl, :], d_ps[(p + q) % 2][:, 0:8 * HEADS].rearrange("k (v h) -> k v h", v=4)).then_inc(s_got, 1)
                    build(0, 0, 0)
                    body(0, 0, 0)
                    with dve.Fori(0, 3) as j:
                        body(2 * j + 1, j, 1)
                        body(2 * j + 2, j + 1, 0)
                    body(7, 3, 1)

                @block.tensor
                def _(pe):
                    pe.wait_ge(s_tab, 32)

                    def body(i, j, p):
                        pe.wait_ge(s_oh, i + 1)
                        for q in range(GR):
                            n = GR * i + q
                            if not early(n, 2):
                                pe.wait_ge(s_got, n - 1)
                            for u in range(4):
                                v = 4 * n + u
                                for part in range(2):
                                    h0 = 2 * HEADS * part
                                    pe.matmul(s_ps[(p + q) % 2][:, u, :].rearrange("k (a h) -> k a h", h=HEADS), lo_b[:, p, 4 * q + u, :],
                                              lo_tab[:, :, h0:h0 + HEADS], start=(part == 0), stop=(part == 1))
                                b = pe.value_load(block_r[:, v:v + 1] if isinstance(v, int) else block_r[:, bass.ds(v, 1)],
                                                  min_val=0, max_val=BLOCKS - 1)
                                for part in range(2):
                                    h0 = 2 * HEADS * part
                                    ins = pe.matmul(d_ps[(p + q) % 2][:, 2 * HEADS * u:2 * HEADS * (u + 1)], dl_b[:, p, 4 * q + u, :],
                                                    st16[:, bass.ds(b, 1), h0:h0 + 2 * HEADS].squeeze(1), start=(part == 0), stop=(part == 1))
                            ins.then_inc(s_grp, 1)
                    steps(pe, 8, body)

            with ExitStack() as c2:
                sV = sbuf(c2, "sV", [VP, HEADS, ROW4])
                run = sbuf(c2, "run", [VP, HEADS, ROW4])
                run2 = sbuf(c2, "run2", [VP, HEADS, ROW4])
                pen = sbuf(c2, "pen", [VP, 2, ROW4])
                ids = sbuf(c2, "ids", [VP, 2])
                cc = sbuf(c2, "cc", [VP, 2, 16])
                last4 = sbuf(c2, "last4", [VP, 2, 2, HEADS])
                sm = sbuf(c2, "sm", [HEADS, 2, 3, VP])
                carry = sbuf(c2, "carry", [VP, 2, 2, HEADS])
                mT = sbuf(c2, "mT", [P, VISITS, HEADS])
                mx = sbuf(c2, "mx", [P, VISITS, HEADS])
                work = sbuf(c2, "work", [P, 2, VISITS, HEADS])
                v_ps = [psum(c2, f"v_ps{h}", [P, 4, P]) for h in range(HEADS)]
                q_ps, r_ps = s_ps[0], s_ps[1]
                s_tv, s_ev, s_c, s_pq, s_dq, s_run, s_tb, s_d, s_e = (
                    sem("mx_tv"), sem("mx_ev"), sem("mx_chain"), sem("mx_pe"), sem("mx_dve"), sem("mx_run"),
                    sem("mx_tb"), sem("mx_d"), sem("mx_e"))
                with nc.Block() as block:
                    @block.tensor
                    def _(pe):
                        for h in range(HEADS):
                            for q in range(4):
                                ins = pe.transpose(v_ps[h][0:VP, q, :], sT[:, q::4, h], ident)
                            ins.then_inc(s_tv, 1)
                        flat = lambda t: t[:, :, :].rearrange("k v a -> k (v a)")
                        for w in range(2):
                            fwd = w == 0
                            hop = shifted[0:VP, 0:VP] if fwd else shifted[0:VP, 2:VP + 2]
                            src_id = ids[:, 1:2] if fwd else ids[:, 0:1]
                            pe.wait_ge(s_dq, 5 * w + 1)
                            pe.matmul(flat(q_ps)[0:VP, 0:1], hop, src_id, start=True, stop=True).then_inc(s_pq, 1)
                            pe.wait_ge(s_dq, 5 * w + 2)
                            pe.transpose(flat(r_ps)[0:HEADS, 0:VP], last4[:, w, 0, :], ident[0:VP, 0:VP])
                            pe.transpose(flat(r_ps)[0:HEADS, P:P + VP], last4[:, w, 1, :], ident[0:VP, 0:VP]).then_inc(s_pq, 1)
                            pe.wait_ge(s_dq, 5 * w + 3)
                            pe.transpose(flat(q_ps)[0:VP, 8:8 + HEADS], sm[:, w, 2, :], ident[0:HEADS, 0:HEADS]).then_inc(s_pq, 1)
                            pe.wait_ge(s_dq, 5 * w + 4)
                            pe.matmul(flat(q_ps)[0:VP, 16:16 + HEADS], hop, carry[:, w, 0, :], start=True, stop=True).then_inc(s_pq, 1)
                        pe.wait_ge(s_dq, 10)
                        for h in range(HEADS):
                            for q in range(4):
                                ins = pe.transpose(v_ps[h][:, q, 0:VP], run[:, h, q * P:(q + 1) * P], ident[0:VP, 0:VP])
                            ins.then_inc(s_tb, 1)

                    @block.scalar
                    def _(act):
                        for h in range(HEADS):
                            act.wait_ge(s_tv, h + 1)
                            act.activation(sV[:, h, :], v_ps[h][0:VP, :, :].rearrange("k q n -> k (q n)"), ACT.Copy).then_inc(s_ev, 1)
                        act.wait_ge(s_d, 1)
                        act.activation(work[:, 1, :, :], work[:, 0, :, :], ACT.Exp).then_inc(s_e, 1)

                    @block.vector
                    def _(dve):
                        link = Chain(dve, s_c)
                        flat = lambda t: t[:, :, :].rearrange("k v a -> k (v a)")
                        dve.tensor_scalar(ids[:, 0:1], dstV[:, 0:1], 1.0, None, ALU.add)
                        dve.tensor_scalar(ids[:, 1:2], dstV[:, ROW4 - 1:ROW4], 1.0, None, ALU.add)
                        dve.memset(pen[:, :, :], 0.0)
                        dve.memset(PK[:, :, SUMS:SUMS + 1], 1.0)
                        link(dve.memset(PK[:, :, 2 * SUMS:PACK], 0.0))
                        link(dve.tensor_tensor(pen[:, 0, 1:ROW4], dstV[:, 1:ROW4], dstV[:, 0:ROW4 - 1], ALU.not_equal))
                        link(dve.tensor_copy(pen[:, 1, 0:ROW4 - 1], pen[:, 0, 1:ROW4]))
                        link(dve.tensor_scalar(pen[:, :, :], pen[:, :, :], -BIG, None, ALU.mult))
                        dve.wait_ge(s_ev, HEADS)
                        for w in range(2):
                            fwd = w == 0
                            turn = (lambda a: a) if fwd else (lambda a: a[:, ::-1])
                            data = sV if fwd else run2
                            res = run2 if fwd else run
                            end = ROW4 - 1 if fwd else 0
                            f_id, l_id = (ids[:, 0:1], ids[:, 1:2]) if fwd else (ids[:, 1:2], ids[:, 0:1])
                            k = cc[:, w, :]
                            for h in range(HEADS):
                                ins = dve.tensor_tensor_scan(turn(res[:, h, :]), turn(pen[:, w, :]), turn(data[:, h, :]), -BIG, ALU.add, ALU.max)
                            link(ins)
                            dve.tensor_copy(last4[:, w, 0, :], res[:, :, end]).then_inc(s_dq, 1)
                            dve.wait_ge(s_pq, 4 * w + 1)
                            link(dve.tensor_tensor(k[:, 0:1], flat(q_ps)[0:VP, 0:1], f_id, ALU.is_equal))
                            link(dve.tensor_tensor(k[:, 1:2], f_id, l_id, ALU.is_equal))
                            link(dve.tensor_tensor(k[:, 2:3], k[:, 0:1], k[:, 1:2], ALU.mult))
                            link(dve.tensor_scalar(k[:, 3:5], k[:, 0:3:2], -1.0, BIG, ALU.add, ALU.mult))
                            link(dve.tensor_copy(last4[:, w, 1, :], k[:, 4:5].broadcast_to([VP, HEADS])))
                            dve.tensor_copy(k[:, 8:9], k[:, 4:5]).then_inc(s_dq, 1)
                            dve.wait_ge(s_pq, 4 * w + 2)
                            dve.tensor_copy(sm[:, w, 0, :], flat(r_ps)[0:HEADS, 0:VP])
                            link(dve.tensor_copy(sm[:, w, 1, :], flat(r_ps)[0:HEADS, P:P + VP]))
                            dve.tensor_tensor_scan(turn(sm[:, w, 2, :]), turn(sm[:, w, 1, :]), turn(sm[:, w, 0, :]), -BIG, ALU.add, ALU.max).then_inc(s_dq, 1)
                            dve.wait_ge(s_pq, 4 * w + 3)
                            dve.tensor_copy(carry[:, w, 0, :], flat(q_ps)[0:VP, 8:8 + HEADS]).then_inc(s_dq, 1)
                            dve.wait_ge(s_pq, 4 * w + 4)
                            link(dve.tensor_scalar(carry[:, w, 1, :], flat(q_ps)[0:VP, 16:16 + HEADS], k[:, 3:4], None, ALU.add))
                            for h in range(HEADS):
                                ins = dve.tensor_tensor_scan(turn(res[:, h, :]), turn(pen[:, w, :]), turn(data[:, h, :]),
                                                             carry[:, w, 1, h:h + 1], ALU.add, ALU.max)
                            ins.then_inc(s_dq, 1)
                            dve.wait_ge(s_dq, 5 * w + 5)
                        for h in range(HEADS):
                            dve.wait_ge(s_tb, h + 1)
                            ins = dve.tensor_copy(mT[:, :, h].rearrange("k (p q) -> k q p", q=4), v_ps[h][:, :, 0:VP])
                        link(ins)
                        t_d = dT[:, :, HEADS:2 * HEADS]
                        dve.tensor_copy(PK[:, :, 0:1], dlocT[:, :].unsqueeze(2))
                        link(dve.tensor_tensor(mx[:, :, :], mT[:, :, :], dT[:, :, 0:HEADS], ALU.max))
                        link(dve.tensor_tensor(work[:, 0, :, :], mx[:, :, :], t_d, ALU.add))
                        link(dve.tensor_tensor(work[:, 1, :, :], sT[:, :, :], t_d, ALU.add))
                        fw = work[:, :, :, :].rearrange("k n v h -> k n (v h)")
                        link(dve.scalar_tensor_tensor(fw, fw, SLOPE, fw, ALU.mult, ALU.max))
                        link(dve.tensor_tensor(work[:, 0, :, :], work[:, 1, :, :], work[:, 0, :, :], ALU.subtract))
                        dve.tensor_scalar(work[:, 0, :, :], work[:, 0, :, :], 0.0, None, ALU.min).then_inc(s_d, 1)
                        his = [slice(1 + HEADS, 1 + 2 * HEADS), slice(1, 1 + HEADS)]
                        for n, t in enumerate((mx[:, :, :], work[:, 1, :, :])):
                            if n == 1:
                                dve.wait_ge(s_e, 1)
                            lo = slice(his[n].start + SUMS, his[n].stop + SUMS)
                            link(dve.tensor_copy(PK[:, :, his[n]], t))
                            dve.tensor_tensor(PK[:, :, lo], t, PK[:, :, his[n]], ALU.subtract)
        early_ctx.close()

        acc_ctx = ExitStack()
        if True:
            acc = sbuf(acc_ctx, "acc", [ROWS, BLOCKS, D])
            sacc = sbuf(acc_ctx, "sacc", [ROWS, BLOCKS, 2 * SUMS])
            c = ExitStack()
            with c:
                rows = sbuf(c, "rows", [P, 8, 2, D], F16)
                O = sbuf(c, "O", [P, 4, 1 + 2 * HEADS, P], F16)
                pk = sbuf(c, "pk", [P, 2, 4, PACK])
                pk16 = sbuf(c, "pk16", [P, 2, 4, PACK], F16)
                idx = sbuf(c, "idx", [P, 2, 4], I32)
                main_ps = psum(c, "main_ps", [P, D])
                small_ps = psum(c, "small_ps", [P, 512])
                s_idx, s_done, s_pk, s_built, s_seen = sem("ms_idx"), sem("ms_done"), sem("ms_pk"), sem("ms_built"), sem("ms_seen")
                s_row = [sem(f"ms_row{k}") for k in range(8)]
                GROUPS = VISITS // 4
                with nc.Block() as block:
                    @block.gpsimd
                    def _(pool):
                        def body(i, j, p):
                            sl = slice(4 * i, 4 * i + 4) if isinstance(i, int) else bass.ds(4 * i, 4)
                            if not early(i, 2):
                                for k in range(4):
                                    wait_apart(pool, s_met, s_row[4 * p + k], 16 * j)
                            pool.tensor_copy(idx[:, p, :], srcT[:, sl]).then_inc(s_idx, 1)
                            wait_apart(pool, s_met, s_idx, i + 1)
                            for k in range(4):
                                if not early(i, 2):
                                    wait_apart(pool, s_met, s_done, 4 * i - 7 + k)
                                pool.indirect_dma_start(
                                    out=rows[:, 4 * p + k, :, :].rearrange("k n d -> k (n d)"), out_offset=None, in_=xp_d[:, :],
                                    in_offset=bass.IndirectOffsetOnAxis(ap=idx[:, p, k:k + 1], axis=0)).then_inc(s_row[4 * p + k], 16)
                        steps(pool, GROUPS, body)

                    @block.vector
                    def _(dve):
                        def evac(v):
                            dve.wait_ge(s_done, v + 1)
                            one = lambda r: r[:, v:v + 1] if isinstance(v, int) else r[:, bass.ds(v, 1)]
                            last = dve.value_load(one(last_r), min_val=0, max_val=1)
                            with dve.If(last == 1):
                                b = dve.value_load(one(block_r), min_val=0, max_val=BLOCKS - 1)
                                dve.tensor_copy(acc[:, bass.ds(b, 1), :].squeeze(1), main_ps[0:ROWS, :]).then_inc(s_seen, 1)
                                dve.tensor_copy(sacc[:, bass.ds(b, 1), :].squeeze(1), small_ps[0:ROWS, 0:2 * SUMS]).then_inc(s_seen, 1)
                            with dve.Else():
                                dve.nop().then_inc(s_seen, 2)

                        def body(i, j, p):
                            sl = slice(4 * i, 4 * i + 4) if isinstance(i, int) else bass.ds(4 * i, 4)
                            if not early(i, 2):
                                dve.wait_ge(s_done, 4 * (i - 1))
                            dve.tensor_copy(pk16[:, p, :, :], PK[:, sl, :]).then_inc(s_pk, 1)
                            dve.tensor_copy(pk[:, p, :, :], PK[:, sl, :]).then_inc(s_pk, 1)
                            dve.wait_ge(s_pk, 2 * i + 2)
                            for k in range(4):
                                if not early(i, 1):
                                    dve.wait_ge(s_done, 4 * i - 3 + k)
                                dve.tensor_scalar(O[:, k, 0, 0:ROWS], iota16[:, 0:ROWS], pk[:, p, k, 0:1], None, ALU.is_equal)
                                for part in range(2):
                                    for h in range(HEADS):
                                        w = 1 + SUMS * part + h
                                        ins = dve.tensor_scalar(O[:, k, 1 + HEADS * part + h, 0:ROWS], iota16[:, 0:ROWS], pk[:, p, k, 0:1],
                                                                pk[:, p, k, w:w + 1], ALU.is_equal, ALU.mult)
                                ins.then_inc(s_built, 1)
                                if not (early(i, 1) and k < 2):
                                    evac(4 * i + k - 2)
                        steps(dve, GROUPS, body)
                        evac(VISITS - 2)
                        evac(VISITS - 1)

                    @block.tensor
                    def _(pe):
                        def products(p, k, first):
                            pe.matmul(small_ps[0:ROWS, 0:2 * SUMS], O[:, k, 0, 0:ROWS], pk16[:, p, k, 1:1 + 2 * SUMS],
                                      start=first, stop=True, skip_group_check=True)
                            for h in range(HEADS):
                                for a, b in ((0, 0), (0, 1), (1, 0)):
                                    ins = pe.matmul(main_ps[0:ROWS, h * C:(h + 1) * C], O[:, k, 1 + HEADS * a + h, 0:ROWS],
                                                    rows[:, 4 * p + k, b, h * C:(h + 1) * C],
                                                    start=first and h % 2 == 0 and a == b, stop=True, skip_group_check=True)
                            ins.then_inc(s_done, 1)

                        def body(i, j, p):
                            for k in range(4):
                                v = 4 * i + k
                                one = lambda r: r[:, v:v + 1] if isinstance(v, int) else r[:, bass.ds(v, 1)]
                                first = pe.value_load(one(first_r), min_val=0, max_val=1)
                                pe.wait_ge(s_built, v + 1)
                                pe.wait_ge(s_row[4 * p + k], 16 * (j + 1))
                                with pe.If(first == 1):
                                    if not early(v, 1):
                                        pe.wait_ge(s_seen, 2 * v)
                                    products(p, k, True)
                                with pe.Else():
                                    products(p, k, False)
                        steps(pe, GROUPS, body)

        with edge_ctx, acc_ctx:
            with ExitStack() as c:
                xt = sbuf(c, "n_xt", [ROWS, 2, D])
                own16 = sbuf(c, "n_own16", [ROWS, 2, 2, D], F16)
                own = sbuf(c, "n_own", [ROWS, 2, D])
                x2 = sbuf(c, "n_x2", [ROWS, 2, D])
                xn = sbuf(c, "n_xn", [ROWS, D])
                bias_b = sbuf(c, "n_bias", [ROWS, D])
                spare = PK[:, :, :].rearrange("k v n -> k (v n)")
                n_T = 4 * KD * ROWS
                xsT = spare[:, 0:n_T].rearrange("k (p n c r) -> k p n c r", p=2, n=2, c=KD)
                xs = spare[0:ROWS, n_T:n_T + 4 * D].rearrange("k (p n d) -> k p n d", p=2, n=2)
                stat = sbuf(c, "n_stat", [ROWS, 2, 2, 6])
                ln = sbuf(c, "n_ln", [ROWS, 2, 10])
                wk = sbuf(c, "n_wk", [ROWS, 4, BLOCKS, HEADS])
                cn = sbuf(c, "n_cn", [ROWS, 3, BLOCKS])
                tr_ps = c.enter_context(nc.psum_tensor("n_tr", [P, 2, KD, P], F16))
                pj_ps = psum(c, "n_pj", [P, 2, D])
                sc_ps = psum(c, "n_sc", [P, 2, 512])
                s_b, s_ch, s_d, s_e = sem("nd_bias"), sem("nd_chain"), sem("nd_d"), sem("nd_e")
                s_x = [sem(f"nd_x{p}") for p in range(2)]
                s_own, s_x2c, s_x2, s_ln, s_var, s_std = sem("nd_own"), sem("nd_x2c"), sem("nd_x2"), sem("nd_ln"), sem("nd_var"), sem("nd_std")
                s_sum, s_xf, s_xh = sem("nd_sum"), sem("nd_xf"), sem("nd_xh")
                s_xn, s_tr, s_xnT, s_mm, s_sq, s_sc = sem("nd_xn"), sem("nd_tr"), sem("nd_xnT"), sem("nd_mm"), sem("nd_sq"), sem("nd_sc")
                s_out = [sem(f"nd_out{p}") for p in range(2)]
                w_own, z_inv = wk[:, 2, :, :], wk[:, 3, :, :]
                with nc.Block() as block:
                    @block.sync
                    def _(sp):
                        sp.dma_start(bias_b[:, :], bias.partition_broadcast(ROWS)).then_inc(s_b, 16)

                        def load(i, j, p):
                            if not early(i, 2):
                                sp.wait_ge(s_x2, i - 1)
                            sp.dma_start(xt[:, p, :], rows_of(x, i)).then_inc(s_x[p], 16)
                            sp.dma_start(own16[:, p, :, :].rearrange("r n d -> r (n d)"), rows_of(xp_d, i)).then_inc(s_x[p], 16)
                        steps(sp, BLOCKS, load)

                    @block.gpsimd
                    def _(pool):
                        def store(i, p):
                            pool.wait_ge(s_xn, i + 1)
                            pool.dma_start(rows_of(x2_d, i), x2[:, p, :]).then_inc(s_out[p], 16)
                            pool.dma_start(rows_of(x2n_d, i), xs[:, p, :, :].rearrange("r n d -> r (n d)")).then_inc(s_out[p], 16)

                        def body(i, j, p):
                            pool.wait_ge(s_x[p], 32 * (j + 1))
                            if not early(i, 2):
                                pool.wait_ge(s_x2, i - 1)
                            pool.tensor_tensor(own[:, p, :], own16[:, p, 0, :], own16[:, p, 1, :], ALU.add).then_inc(s_sum, 1)
                            if not early(i, 1):
                                store(i - 1, 1 - p)
                        steps(pool, BLOCKS, body)
                        store(BLOCKS - 1, (BLOCKS - 1) % 2)
                        pool.wait_ge(s_out[0], 32 * (BLOCKS - BLOCKS // 2))
                        pool.wait_ge(s_out[1], 32 * (BLOCKS // 2))

                    @block.vector
                    def _(dve):
                        link = Chain(dve, s_ch)
                        link(dve.tensor_tensor(sacc[:, :, 0:SUMS], sacc[:, :, 0:SUMS], sacc[:, :, SUMS:2 * SUMS], ALU.add))
                        s_n, t_n = stN[:, :, 0:HEADS], stN[:, :, HEADS:2 * HEADS]
                        wide = lambda a: a.unsqueeze(2).broadcast_to([ROWS, BLOCKS, HEADS])
                        link(dve.tensor_scalar(cn[:, 0, :], sacc[:, :, 2 * HEADS], 1.0, None, ALU.max))
                        link(dve.reciprocal(cn[:, 1, :], cn[:, 0, :]))
                        link(dve.tensor_scalar(cn[:, 0, :], sacc[:, :, 2 * HEADS], 1.0, None, ALU.min))
                        link(dve.tensor_scalar(cn[:, 2, :], cn[:, 0, :], -1.0, BIG, ALU.add, ALU.mult))
                        link(dve.tensor_tensor(wk[:, 0, :, :], sacc[:, :, HEADS:2 * HEADS], wide(cn[:, 1, :]), ALU.mult))
                        link(dve.tensor_tensor(wk[:, 0, :, :], wk[:, 0, :, :], wide(cn[:, 2, :]), ALU.add))
                        link(dve.tensor_tensor(wk[:, 0, :, :], wk[:, 0, :, :], s_n, ALU.max))
                        link(dve.tensor_tensor(wk[:, 0, :, :], wk[:, 0, :, :], t_n, ALU.add))
                        link(dve.tensor_tensor(wk[:, 1, :, :], s_n, t_n, ALU.add))
                        fl = wk[:, 0:2, :, :].rearrange("r n b h -> r (n b h)")
                        link(dve.scalar_tensor_tensor(fl, fl, SLOPE, fl, ALU.mult, ALU.max))
                        link(dve.tensor_tensor(wk[:, 0, :, :], wk[:, 1, :, :], wk[:, 0, :, :], ALU.subtract))
                        dve.tensor_scalar(wk[:, 1, :, :], wk[:, 0, :, :], 0.0, None, ALU.min).then_inc(s_d, 1)
                        dve.wait_ge(s_e, 1)
                        link(dve.tensor_tensor(wk[:, 1, :, :], wk[:, 0, :, :], sacc[:, :, 0:HEADS], ALU.add))
                        link(dve.reciprocal(z_inv, wk[:, 1, :, :]))
                        dve.tensor_tensor(w_own, wk[:, 0, :, :], z_inv, ALU.mult).then_inc(s_d, 1)
                        dve.wait_ge(s_b, 16)

                        def take_scores(i, p):
                            dve.wait_ge(s_mm, i + 1)
                            dve.tensor_scalar(at(scores, i), sc_ps[0:ROWS, p, 0:NX], 1.0 / WS, None, ALU.mult).then_inc(s_sc, 1)

                        def body(i, j, p):
                            link = Chain(dve, s_x2c, 2 * i)
                            dve.wait_ge(s_own, i + 1)
                            if not early(i, 2):
                                dve.wait_ge(s_out[p], 32 * j)
                            for h in range(HEADS):
                                sl = slice(h * C, (h + 1) * C)
                                a = acc[:, i, sl] if isinstance(i, int) else acc[:, bass.ds(i, 1), sl].squeeze(1)
                                z = z_inv[:, i, h:h + 1] if isinstance(i, int) else z_inv[:, bass.ds(i, 1), h:h + 1].squeeze(1)
                                ins = dve.scalar_tensor_tensor(x2[:, p, sl], a, z, own[:, p, sl], ALU.mult, ALU.add)
                            link(ins)
                            link(dve.tensor_tensor(own[:, p, :], x2[:, p, :], bias_b[:, :], ALU.add))
                            dve.scalar_tensor_tensor(x2[:, p, :], own[:, p, :], 0.0, xt[:, p, :], ALU.max, ALU.add).then_inc(s_x2, 1)
                            dve.wait_ge(s_x2, i + 1)
                            layer_norm(dve, x2[:, p, :], xn[:, :], xs[:, p, :, :], stat[:, p, :, :], ln[:, p, :],
                                       s_ln, s_var, s_std, s_met, s_xf, s_xh, s_xn, i)
                            if not early(i, 1):
                                take_scores(i - 1, 1 - p)
                        steps(dve, BLOCKS, body)
                        take_scores(BLOCKS - 1, (BLOCKS - 1) % 2)

                    @block.scalar
                    def _(act):
                        act.wait_ge(s_d, 1)
                        act.activation(wk[:, 0, :, :], wk[:, 1, :, :], ACT.Exp).then_inc(s_e, 1)
                        act.wait_ge(s_d, 2)

                        def square(i, p):
                            act.wait_ge(s_mm, i + 1)
                            act.activation(pj_ps[0:ROWS, p, :], pj_ps[0:ROWS, p, :], ACT.Square, scale=1.0 / WS,
                                           accum_out=nsq[:, i:i + 1] if isinstance(i, int) else nsq[:, bass.ds(i, 1)]).then_inc(s_sq, 1)

                        def scale_own(i, j, p):
                            act.wait_ge(s_sum, i + 1)
                            for h in range(HEADS):
                                w = w_own[:, i, h:h + 1] if isinstance(i, int) else w_own[:, bass.ds(i, 1), h:h + 1].squeeze(1)
                                ins = act.activation(own[:, p, h * C:(h + 1) * C], own[:, p, h * C:(h + 1) * C], ACT.Copy, scale=w)
                            ins.then_inc(s_own, 1)

                        def body(i, j, p):
                            scale_own(i, j, p)
                            act.wait_ge(s_var, i + 1)
                            act.activation(ln[:, p, 3:4], ln[:, p, 2:3], ACT.Sqrt).then_inc(s_std, 1)
                            act.wait_ge(s_xf, i + 1)
                            if not early(i, 2):
                                act.wait_ge(s_tr, i - 1)
                                act.wait_ge(s_out[p], 32 * j)
                            act.activation(xs[:, p, 0, :], xn[:, :], ACT.Copy).then_inc(s_xh, 1)
                            act.wait_ge(s_tr, i + 1)
                            if not early(i, 2):
                                act.wait_ge(s_mm, i - 1)
                            act.activation(xsT[:, p, :, :, :], tr_ps[:, :, :, 0:ROWS], ACT.Copy).then_inc(s_xnT, 1)
                            if not early(i, 1):
                                square(i - 1, 1 - p)
                        steps(act, BLOCKS, body)
                        square(BLOCKS - 1, (BLOCKS - 1) % 2)

                    @block.tensor
                    def _(pe):
                        def turn(i, p):
                            pe.wait_ge(s_xn, i + 1)
                            if not early(i, 1):
                                pe.wait_ge(s_xnT, i)
                            turn_parts(pe, tr_ps, xs[:, p, :, :], ident16).then_inc(s_tr, 1)

                        def body(i, j, p):
                            pe.wait_ge(s_xnT, i + 1)
                            if not early(i, 2):
                                pe.wait_ge(s_sq, i - 1)
                                pe.wait_ge(s_sc, i - 1)
                            lhs = xsT[:, p, :, :, :]
                            product(pe, pj_ps[0:ROWS, p, 0:512], lhs, WpT[:, :, :, 0:512], range(KD), KD)
                            product(pe, sc_ps[0:ROWS, p, 0:NX], lhs, Msim[:, :, :, :], range(KD), KD)
                            product(pe, pj_ps[0:ROWS, p, 512:D], lhs, WpT[:, :, :, 512:D], range(KD // 2), KD)
                            if not (isinstance(i, int) and i == BLOCKS - 1):
                                turn(i + 1, 1 - p)
                            product(pe, pj_ps[0:ROWS, p, 512:D], lhs, WpT[:, :, :, 512:D], range(KD // 2, KD), KD).then_inc(s_mm, 1)
                        turn(0, 0)
                        steps(pe, BLOCKS, body)

        with ExitStack() as c:
            tcol = sbuf(c, "tcol", [ROWS, 2])
            rn = sbuf(c, "rn", [ROWS, 3, BLOCKS])
            top = sbuf(c, "top", [ROWS, BLOCKS, 8])
            top_u = sbuf(c, "top_u", [ROWS, BLOCKS, 8], U32)
            top_f = sbuf(c, "top_f", [ROWS, BLOCKS, 2])
            oh = sbuf(c, "oh", [ROWS, 2, BLOCKS, NX])
            both = sbuf(c, "both", [ROWS, BLOCKS, NX])
            strict = sbuf(c, "strict", [ROWS, ROWS])
            base = sbuf(c, "base", [ROWS, BLOCKS + 1, NX])
            tot = sbuf(c, "tot", [ROWS, BLOCKS, NX])
            pad_i = sbuf(c, "pad_i", [ROWS, 2, NX], I32)
            start_e = sbuf(c, "start_e", [ROWS, NX + 1])
            padded = sbuf(c, "padded", [ROWS, NX])
            place = sbuf(c, "place", [ROWS, BLOCKS, NX])
            hit = sbuf(c, "hit", [ROWS, 2, BLOCKS, NX])
            slot_f = sbuf(c, "slot_f", [ROWS, 2, BLOCKS])
            dif = sbuf(c, "dif", [ROWS, 3, BLOCKS])
            token = sbuf(c, "token", [ROWS, BLOCKS], I32)
            tile_r = sbuf(c, "tile_r", [1, XTILES])
            xcmp = sbuf(c, "xcmp", [1, XTILES, NX - 1])
            xe_f = sbuf(c, "xe_f", [1, XTILES + 1])
            x_flag = sbuf(c, "x_flag", [1, 2, XTILES])
            zero_i = sbuf(c, "zero_i", [XTILES, P], I32)
            b_ps = psum(c, "b_ps", [P, 2, 256])
            b_ps2 = psum(c, "b_ps2", [P, 2, 256])
            s_t, s_k, s_n, s_c, s_sm, s_em = sem("rt_temp"), sem("rt_const"), sem("rt_n"), sem("rt_chain"), sem("rt_sm"), sem("rt_em")
            s_oh, s_mm, s_slot, s_z, s_sc, s_q = sem("rt_oh"), sem("rt_mm"), sem("rt_slot"), sem("rt_zero"), sem("rt_scatter"), sem("rt_q")
            with nc.Block() as block:
                @block.sync
                def _(sp):
                    sp.dma_start(tcol[:, 0:1], temp.partition_broadcast(ROWS)).then_inc(s_t, 16)
                    sp.wait_ge(s_q, 1)
                    sp.dma_start(tok_d.rearrange("(a b) n -> a (b n)", b=P), zero_i[:, :]).then_inc(s_z, 16)

                @block.gpsimd
                def _(pool):
                    pool.memset(zero_i[:, :], 0).then_inc(s_q, 1)
                    pool.memset(strict[:, :], 1.0).then_inc(s_k, 1)
                    pool.iota(token[:, :], pattern=[[ROWS, BLOCKS]], base=0, channel_multiplier=1).then_inc(s_k, 1)
                    pool.iota(tile_r[:, :], pattern=[[P, XTILES]], base=0, channel_multiplier=0,
                              allow_small_or_imprecise_dtypes=True).then_inc(s_k, 1)
                    pool.wait_ge(s_k, 3)
                    pool.affine_select(out=strict[:, :], in_=strict[:, :], compare_op=ALU.is_gt, fill=0.0, base=0,
                                       pattern=[[1, ROWS]], channel_multiplier=-1).then_inc(s_k, 1)
                    pool.wait_ge(s_slot, 1)
                    pool.wait_ge(s_z, 16)
                    for b in range(BLOCKS):
                        for n in range(2):
                            pool.indirect_dma_start(out=tok_d[:, :], out_offset=bass.IndirectOffsetOnAxis(ap=slot_i[:, b, n:n + 1], axis=0),
                                                    in_=token[:, b:b + 1], in_offset=None).then_inc(s_sc, 16)
                    pool.wait_ge(s_sc, 32 * BLOCKS)

                @block.scalar
                def _(act):
                    act.activation(rn[:, 0, :], nsq[:, :], ACT.Sqrt).then_inc(s_n, 1)
                    act.wait_ge(s_sm, 1)
                    act.activation(dif[:, 1, :], dif[:, 0, :], ACT.Exp).then_inc(s_em, 1)

                @block.vector
                def _(dve):
                    link = Chain(dve, s_c)
                    wide = lambda a: a.unsqueeze(2).broadcast_to([ROWS, BLOCKS, NX])
                    dve.wait_ge(s_n, 1)
                    dve.wait_ge(s_t, 16)
                    link(dve.reciprocal(tcol[:, 1:2], tcol[:, 0:1]))
                    link(dve.tensor_scalar(rn[:, 1, :], rn[:, 0, :], NORM_EPS, None, ALU.max))
                    link(dve.reciprocal(rn[:, 2, :], rn[:, 1, :]))
                    link(dve.tensor_scalar(rn[:, 0, :], rn[:, 2, :], tcol[:, 1:2], None, ALU.mult))
                    link(dve.tensor_tensor(scores[:, :, :], scores[:, :, :], wide(rn[:, 0, :]), ALU.mult))
                    for b in range(BLOCKS):
                        ins = dve.max(top[:, b, :], scores[:, b, :])
                    link(ins)
                    for b in range(BLOCKS):
                        ins = dve.max_index(top_u[:, b, :], top[:, b, :], scores[:, b, :])
                    link(ins)
                    dve.tensor_tensor(dif[:, 0, :], top[:, :, 1], top[:, :, 0], ALU.subtract).then_inc(s_sm, 1)
                    link(dve.tensor_copy(top_f[:, :, :], top_u[:, :, 0:2]))
                    for n in range(2):
                        ins = dve.tensor_tensor(oh[:, n, :, :], iota_row[0:ROWS, 0:NX].unsqueeze(1).broadcast_to([ROWS, BLOCKS, NX]),
                                                wide(top_f[:, :, n]), ALU.is_equal)
                    link(ins)
                    dve.tensor_tensor(both[:, :, :], oh[:, 0, :, :], oh[:, 1, :, :], ALU.add).then_inc(s_oh, 1)
                    dve.memset(base[:, 0, :], 0.0)
                    dve.wait_ge(s_em, 1)
                    link(dve.tensor_scalar(dif[:, 2, :], dif[:, 1, :], 1.0, None, ALU.add))
                    link(dve.reciprocal(gates[:, :, 0], dif[:, 2, :]))
                    link(dve.tensor_tensor(gates[:, :, 1], gates[:, :, 0], dif[:, 1, :], ALU.mult))
                    for n in range(2):
                        ins = dve.tensor_tensor(hit[:, n, :, :], oh[:, n, :, :], wide(gates[:, :, n]), ALU.mult)
                    link(ins)
                    link(dve.tensor_tensor(comb[:, :, :], hit[:, 0, :, :], hit[:, 1, :, :], ALU.add))
                    dve.wait_ge(s_mm, 2)
                    link(dve.tensor_copy(tot[:, :, :], b_ps[0:ROWS, 0, 0:BLOCKS * NX].rearrange("r (b e) -> r b e", e=NX)))
                    for b in range(BLOCKS):
                        link(dve.tensor_tensor(base[:, b + 1, :], base[:, b, :], tot[:, b, :], ALU.add))
                    link(dve.tensor_scalar(padded[:, :], base[:, BLOCKS, :], float(P - 1), float(P), ALU.add, ALU.max))
                    link(dve.tensor_copy(pad_i[:, 0, :], padded[:, :]))
                    link(dve.tensor_scalar(pad_i[:, 1, :], pad_i[:, 0, :], -P, None, ALU.bitwise_and))
                    link(dve.memset(start_e[:, :], 0.0))
                    link(dve.tensor_copy(padded[:, :], pad_i[:, 1, :]))
                    for e in range(NX):
                        link(dve.tensor_tensor(start_e[:, e + 1:e + 2], start_e[:, e:e + 1], padded[:, e:e + 1], ALU.add))
                    link(dve.tensor_tensor(place[:, :, :], base[:, 0:BLOCKS, :],
                                           start_e[:, 0:NX].unsqueeze(1).broadcast_to([ROWS, BLOCKS, NX]), ALU.add))
                    link(dve.tensor_tensor(tot[:, :, :], place[:, :, :],
                                           b_ps2[0:ROWS, 0, 0:BLOCKS * NX].rearrange("r (b e) -> r b e", e=NX), ALU.add))
                    for n in range(2):
                        ins = dve.tensor_tensor(hit[:, n, :, :], oh[:, n, :, :], tot[:, :, :], ALU.mult)
                    link(ins)
                    link(dve.tensor_reduce(slot_f[:, :, :], hit[:, :, :, :], AX.X, ALU.add))
                    dve.tensor_copy(slot_i[:, :, :].rearrange("r b n -> r n b"), slot_f[:, :, :]).then_inc(s_slot, 1)
                    dve.wait_ge(s_k, 4)
                    link(dve.tensor_tensor(xcmp[:, :, :], tile_r[:, :].unsqueeze(2).broadcast_to([1, XTILES, NX - 1]),
                                           start_e[0:1, 1:NX].unsqueeze(1).broadcast_to([1, XTILES, NX - 1]), ALU.is_ge))
                    dve.memset(xe_f[:, 0:1], -1.0)
                    link(dve.tensor_reduce(xe_f[:, 1:XTILES + 1], xcmp[:, :, :], AX.X, ALU.add))
                    link(dve.tensor_copy(x_i[:, 0, :], xe_f[:, 1:XTILES + 1]))
                    link(dve.tensor_scalar(x_i[:, 1, :], x_i[:, 0, :], 1, None, ALU.bitwise_and))
                    dve.tensor_tensor(x_flag[:, 0, :], xe_f[:, 1:XTILES + 1], xe_f[:, 0:XTILES], ALU.not_equal)
                    link(dve.tensor_scalar(x_flag[:, 1, :], xe_f[:, 1:XTILES + 1], float(NX - 1), None, ALU.is_lt))
                    dve.tensor_tensor(x_i[:, 2, :], x_flag[:, 0, :], x_flag[:, 1, :], ALU.mult)

                @block.tensor
                def _(pe):
                    pe.wait_ge(s_oh, 1)
                    pe.wait_ge(s_k, 4)
                    flat = both[:, :, :].rearrange("r b e -> r (b e)")
                    pe.matmul(b_ps[0:ROWS, 0, 0:BLOCKS * NX], ones[0:ROWS, 0:ROWS], flat, start=True, stop=True).then_inc(s_mm, 1)
                    pe.matmul(b_ps2[0:ROWS, 0, 0:BLOCKS * NX], strict[:, :], flat, start=True, stop=True).then_inc(s_mm, 1)

        with ExitStack() as c:
            tok_r = sbuf(c, "tok_r", [XTILES, P], I32)
            tok_f = sbuf(c, "tok_f", [XTILES, P])
            tokT = sbuf(c, "tokT", [P, XTILES], I32)
            b1_b = sbuf(c, "b1_b", [P, NX, FF])
            xi = sbuf(c, "xi", [P, 2, 1], I32)
            xg = sbuf(c, "xg", [P, 2, 2, D], F16)
            xgT = sbuf(c, "xgT", [P, 2, 2, KD, P], F16)
            w_f = sbuf(c, "w_f", [P, WPIECES, WCOLS])
            w_p = sbuf(c, "w_p", [P, 2, 2, WPIECES, WCOLS], F16)
            h_b = sbuf(c, "h_b", [P, FF])
            h_g = sbuf(c, "h_g", [P, FF])
            h_s = sbuf(c, "h_s", [P, 2, FF], F16)
            hT = sbuf(c, "hT", [P, 2, 2, KF, P], F16)
            eo = sbuf(c, "eo", [P, 2, D])
            tr_ps = c.enter_context(nc.psum_tensor("x_tr", [P, 2, KD, P], F16))
            ht_ps = c.enter_context(nc.psum_tensor("x_ht", [P, 2, KF, P], F16))
            h_ps = psum(c, "x_h", [P, FF])
            o_ps = psum(c, "x_o", [P, 2, D])
            s_ld, s_c, s_t0, s_xi = sem("xp_load"), sem("xp_chain"), sem("xp_t0"), sem("xp_xi")
            s_g = [sem(f"xp_g{p}") for p in range(2)]
            s_st = [sem(f"xp_st{p}") for p in range(2)]
            s_w, s_whi, s_wlo = sem("xp_w"), sem("xp_whi"), sem("xp_wlo")
            s_tr, s_xT, s_h, s_hb, s_gel = sem("xp_tr"), sem("xp_xT"), sem("xp_h"), sem("xp_hb"), sem("xp_gelu")
            s_hi, s_lo, s_ht, s_hT, s_o, s_eo = sem("xp_hi"), sem("xp_lo"), sem("xp_ht"), sem("xp_hT"), sem("xp_o"), sem("xp_eo")

            def tile_value(eng, n, i, top):
                one = x_i[:, n, i:i + 1] if isinstance(i, int) else x_i[:, n, bass.ds(i, 1)]
                return eng.value_load(one, min_val=0, max_val=top)

            def w_pieces(e):
                one = (lambda t: t[e:e + 1]) if isinstance(e, int) else (lambda t: t[bass.ds(e, 1), :, :])
                return (one(W1).rearrange("a (k p) f -> p (a k) f", p=P), one(W2).rearrange("a (k p) f -> p (a k) f", p=P))

            with nc.Block() as block:
                @block.sync
                def _(sp):
                    def load(e):
                        for n, w in enumerate(w_pieces(e)):
                            half = w_f[:, n * WPIECES // 2:(n + 1) * WPIECES // 2, :].rearrange("p a b -> p (a b)")
                            sp.dma_start(half.rearrange("p (k f) -> p k f", f=(FF, D)[n]), w).then_inc(s_w, 16)
                    sp.dma_start(tok_r[:, :], tok_d.rearrange("(a b) n -> a (b n)", b=P)).then_inc(s_ld, 16)
                    sp.dma_start(b1_b[:, :, :].rearrange("p e f -> p (e f)"), b1.rearrange("e f -> (e f)").partition_broadcast(P)).then_inc(s_ld, 16)
                    load(0)

                    def body(i, j, p):
                        flag = tile_value(sp, 2, i, 1)
                        with sp.If(flag == 1):
                            e = tile_value(sp, 0, i, NX - 2)
                            sp.wait_ge(s_wlo, WPIECES * (e + 1))
                            load(e + 1)
                    steps(sp, XTILES, body)

                @block.gpsimd
                def _(pool):
                    pool.wait_ge(s_c, 2)

                    def store(i, j, p):
                        pool.wait_ge(s_eo, i + 1)
                        d = eo_d[P * i:P * (i + 1), :] if isinstance(i, int) else eo_d[bass.ds(P * i, P), :]
                        pool.dma_start(d, eo[:, p, :]).then_inc(s_st[p], 16)

                    def body(i, j, p):
                        if not early(i, 2):
                            pool.wait_ge(s_tr, i - 1)
                        pool.tensor_copy(xi[:, p, :], tokT[:, i:i + 1] if isinstance(i, int) else tokT[:, bass.ds(i, 1)]).then_inc(s_xi, 1)
                        wait_apart(pool, s_met, s_xi, i + 1)
                        pool.indirect_dma_start(out=xg[:, p, :, :].rearrange("k n d -> k (n d)"), out_offset=None, in_=x2n_d[:, :],
                                                in_offset=bass.IndirectOffsetOnAxis(ap=xi[:, p, :], axis=0)).then_inc(s_g[p], 16)
                        if not early(i, 2):
                            store(i - 2, j, p)
                    steps(pool, XTILES, body)
                    store(XTILES - 2, 0, 0)
                    store(XTILES - 1, 0, 1)
                    pool.wait_ge(s_st[0], 8 * XTILES)
                    pool.wait_ge(s_st[1], 8 * XTILES)

                @block.vector
                def _(dve):
                    dve.wait_ge(s_ld, 32)
                    dve.tensor_copy(tok_f[:, :], tok_r[:, :]).then_inc(s_c, 1)
                    dve.wait_ge(s_t0, 1)
                    dve.tensor_copy(tokT[:, :], o_ps[:, 1, 0:XTILES]).then_inc(s_c, 1)

                    def low(e, q):
                        for n in range(WPIECES):
                            wait_apart(dve, s_met, s_whi, WPIECES * e + n + 1)
                            buf = (lambda part: w_p[:, q, part, n, :]) if isinstance(q, int) else (lambda part: w_p[:, bass.ds(q, 1), part, n, :].squeeze(1))
                            dve.scalar_tensor_tensor(buf(1), w_f[:, n, :], WS, buf(0), ALU.mult, ALU.subtract).then_inc(s_wlo, 1)

                    def take(i, j, p):
                        dve.wait_ge(s_o, i + 1)
                        if not early(i, 2):
                            dve.wait_ge(s_st[p], 16 * j)
                        dve.tensor_scalar(eo[:, p, :], o_ps[:, p, :], 1.0 / WS, None, ALU.mult).then_inc(s_eo, 1)

                    def body(i, j, p):
                        e = tile_value(dve, 0, i, NX - 1)
                        flag = tile_value(dve, 2, i, 1)
                        dve.wait_ge(s_h, i + 1)
                        if not early(i, 1):
                            dve.wait_ge(s_gel, i)
                        dve.scalar_tensor_tensor(h_b[:, :], h_ps[:, :], 1.0 / WS, b1_b[:, bass.ds(e, 1), :].squeeze(1),
                                                 ALU.mult, ALU.add).then_inc(s_hb, 1)
                        dve.wait_ge(s_hi, i + 1)
                        dve.tensor_tensor(h_s[:, 1, :], h_g[:, :], h_s[:, 0, :], ALU.subtract).then_inc(s_lo, 1)
                        if not early(i, 1):
                            take(i - 1, j - 1 + p, 1 - p)
                        with dve.If(flag == 1):
                            q = tile_value(dve, 1, i, 1)
                            low(e + 1, 1 - q)
                    low(0, 0)
                    steps(dve, XTILES, body)
                    take(XTILES - 1, (XTILES - 1) // 2, (XTILES - 1) % 2)

                @block.scalar
                def _(act):
                    def high(e, q):
                        act.wait_ge(s_w, 32 * (e + 1))
                        for n in range(WPIECES):
                            buf = w_p[:, q, 0, n, :] if isinstance(q, int) else w_p[:, bass.ds(q, 1), 0, n, :].squeeze(1)
                            act.activation(buf, w_f[:, n, :], ACT.Copy, scale=WS).then_inc(s_whi, 1)

                    def take_x(i, p):
                        act.wait_ge(s_tr, i + 1)
                        if not early(i, 2):
                            act.wait_ge(s_h, i - 1)
                        act.activation(xgT[:, p, :, :, :], tr_ps[:, :, :, :], ACT.Copy).then_inc(s_xT, 1)

                    def body(i, j, p):
                        flag = tile_value(act, 2, i, 1)
                        act.wait_ge(s_hb, i + 1)
                        if not early(i, 1):
                            act.wait_ge(s_lo, i)
                            act.wait_ge(s_ht, i)
                        act.activation(h_g[:, :], h_b[:, :], ACT.Gelu).then_inc(s_gel, 1)
                        act.wait_ge(s_gel, i + 1)
                        act.activation(h_s[:, 0, :], h_g[:, :], ACT.Copy).then_inc(s_hi, 1)
                        if not (isinstance(i, int) and i == XTILES - 1):
                            take_x(i + 1, 1 - p)
                        act.wait_ge(s_ht, i + 1)
                        if not early(i, 2):
                            act.wait_ge(s_o, i - 1)
                        act.activation(hT[:, p, :, :, :], ht_ps[:, :, :, :], ACT.Copy).then_inc(s_hT, 1)
                        if not (isinstance(i, int) and i == XTILES - 1):
                            with act.If(flag == 1):
                                e = tile_value(act, 0, i, NX - 2)
                                q = tile_value(act, 1, i, 1)
                                if not early(i, 1):
                                    act.wait_ge(s_o, i)
                                high(e + 1, 1 - q)
                    high(0, 0)
                    take_x(0, 0)
                    steps_even(act, XTILES, body)

                @block.tensor
                def _(pe):
                    pe.wait_ge(s_c, 1)
                    pe.transpose(o_ps[:, 1, 0:XTILES], tok_f[:, :], ident[0:XTILES, 0:XTILES]).then_inc(s_t0, 1)
                    pe.wait_ge(s_c, 2)

                    def turn(i, p, g):
                        pe.wait_ge(s_g[p], g)
                        if not early(i, 1):
                            pe.wait_ge(s_xT, i)
                        turn_parts(pe, tr_ps, xg[:, p, :, :], ident16).then_inc(s_tr, 1)

                    def first(i, p):
                        e = tile_value(pe, 0, i, NX - 1)
                        q = tile_value(pe, 1, i, 1)
                        pe.wait_ge(s_wlo, WPIECES * (e + 1))
                        pe.wait_ge(s_xT, i + 1)
                        if not early(i, 1):
                            pe.wait_ge(s_hb, i)
                        per = WCOLS // FF
                        for k in range(KD):
                            for a, b in ((0, 0), (0, 1), (1, 0)):
                                w = w_p[:, bass.ds(q, 1), b, k // per, (k % per) * FF:(k % per + 1) * FF].squeeze(1)
                                ins = pe.matmul(h_ps[:, :], xgT[:, p, a, k, :], w, start=(k == 0 and a == b), stop=(k == KD - 1 and a == 1))
                        ins.then_inc(s_h, 1)
                        return q

                    def second(i, p, q, n):
                        if n == 0:
                            pe.wait_ge(s_hT, i + 1)
                            if not early(i, 2):
                                pe.wait_ge(s_eo, i - 1)
                        per = WCOLS // D
                        for f in range(KF):
                            for a, b in ((0, 0), (0, 1), (1, 0)):
                                at_col = (f % per) * D + n * 512
                                w = w_p[:, bass.ds(q, 1), b, WPIECES // 2 + f // per, at_col:at_col + 512].squeeze(1)
                                ins = pe.matmul(o_ps[:, p, n * 512:(n + 1) * 512], hT[:, p, a, f, :], w,
                                                start=(f == 0 and a == b), stop=(f == KF - 1 and a == 1))
                        if n == 1:
                            ins.then_inc(s_o, 1)

                    def turn_h(i):
                        pe.wait_ge(s_lo, i + 1)
                        if not early(i, 1):
                            pe.wait_ge(s_hT, i)
                        for part in range(2):
                            for f in range(KF):
                                ins = pe.transpose(ht_ps[:, part, f, :], h_s[:, part, f * P:(f + 1) * P], ident16[:, :])
                        ins.then_inc(s_ht, 1)

                    def body(i, j, p):
                        first(i, p)
                        old = tile_value(pe, 1, i - 1, 1) if not early(i, 1) else None
                        if old is not None:
                            second(i - 1, 1 - p, old, 0)
                        if not (isinstance(i, int) and i == XTILES - 1):
                            turn(i + 1, 1 - p, 16 * (j + 1 + p))
                        if old is not None:
                            second(i - 1, 1 - p, old, 1)
                        turn_h(i)
                    turn(0, 0, 16)
                    steps_even(pe, XTILES, body)
                    q = tile_value(pe, 1, XTILES - 1, 1)
                    for n in range(2):
                        second(XTILES - 1, (XTILES - 1) % 2, q, n)

        with ExitStack() as c:
            b2_sb = sbuf(c, "b2_sb", [NX, D])
            s_cs = sem("cb_comb")
            comb_s = sbuf(c, "comb_s", [ROWS, 2, NX])
            combT = sbuf(c, "combT", [NX, 2, ROWS])
            ci = sbuf(c, "ci", [ROWS, 2, 2], I32)
            x2 = sbuf(c, "c_x2", [ROWS, 2, D])
            r = [sbuf(c, f"c_r{n}", [ROWS, 2, D]) for n in range(2)]
            y = sbuf(c, "c_y", [ROWS, 2, D])
            t_ps = psum(c, "c_t", [P, 2, 512])
            b_ps = psum(c, "c_b", [P, 2, D])
            s_b2, s_ci, s_tr, s_cT, s_bb, s_y, s_yc = sem("cb_b2"), sem("cb_ci"), sem("cb_tr"), sem("cb_cT"), sem("cb_bb"), sem("cb_y"), sem("cb_yc")
            s_x = [sem(f"cb_x{p}") for p in range(2)]
            s_r = [sem(f"cb_r{p}") for p in range(2)]
            s_out = [sem(f"cb_out{p}") for p in range(2)]
            with nc.Block() as block:
                @block.sync
                def _(sp):
                    sp.dma_start(b2_sb[:, :], b2).then_inc(s_b2, 16)

                    def body(i, j, p):
                        if not early(i, 2):
                            sp.wait_ge(s_y, i - 1)
                        sp.dma_start(x2[:, p, :], rows_of(x2_d, i)).then_inc(s_x[p], 16)
                        if not early(i, 1):
                            store(i - 1, 1 - p)

                    def store(i, p):
                        sp.wait_ge(s_y, i + 1)
                        sp.dma_start(rows_of(out, i), y[:, p, :]).then_inc(s_out[p], 16)
                    steps(sp, BLOCKS, body)
                    store(BLOCKS - 1, (BLOCKS - 1) % 2)
                    sp.wait_ge(s_out[0], 16 * (BLOCKS - BLOCKS // 2))
                    sp.wait_ge(s_out[1], 16 * (BLOCKS // 2))

                @block.gpsimd
                def _(pool):
                    def body(i, j, p):
                        s = slot_i[:, i, :] if isinstance(i, int) else slot_i[:, bass.ds(i, 1), :].squeeze(1)
                        if not early(i, 2):
                            pool.wait_ge(s_y, i - 1)
                        pool.tensor_copy(ci[:, p, :], s).then_inc(s_ci, 1)
                        wait_apart(pool, s_met, s_ci, i + 1)
                        for n in range(2):
                            pool.indirect_dma_start(out=r[n][:, p, :], out_offset=None, in_=eo_d[:, :],
                                                    in_offset=bass.IndirectOffsetOnAxis(ap=ci[:, p, n:n + 1], axis=0)).then_inc(s_r[p], 16)
                    steps(pool, BLOCKS, body)

                @block.tensor
                def _(pe):
                    pe.wait_ge(s_b2, 16)

                    def body(i, j, p):
                        pe.wait_ge(s_cs, i + 1)
                        if not early(i, 2):
                            pe.wait_ge(s_cT, i - 1)
                        pe.transpose(t_ps[0:NX, p, 0:ROWS], comb_s[:, p, :], ident[0:ROWS, 0:ROWS]).then_inc(s_tr, 1)
                        pe.wait_ge(s_cT, i + 1)
                        if not early(i, 2):
                            pe.wait_ge(s_y, i - 1)
                        for n in range(2):
                            ins = pe.matmul(b_ps[0:ROWS, p, n * 512:(n + 1) * 512], combT[:, p, :], b2_sb[:, n * 512:(n + 1) * 512], start=True, stop=True)
                        ins.then_inc(s_bb, 1)

                    steps(pe, BLOCKS, body)

                @block.scalar
                def _(act):
                    def body(i, j, p):
                        cb = comb[:, i, :] if isinstance(i, int) else comb[:, bass.ds(i, 1), :].squeeze(1)
                        if not early(i, 2):
                            act.wait_ge(s_tr, i - 1)
                        act.activation(comb_s[:, p, :], cb, ACT.Copy).then_inc(s_cs, 1)
                        act.wait_ge(s_tr, i + 1)
                        if not early(i, 2):
                            act.wait_ge(s_bb, i - 1)
                        act.activation(combT[:, p, :], t_ps[0:NX, p, 0:ROWS], ACT.Copy).then_inc(s_cT, 1)
                    steps(act, BLOCKS, body)

                @block.vector
                def _(dve):
                    def body(i, j, p):
                        link = Chain(dve, s_yc, 2 * i)
                        g = lambda n: (gates[:, i, n:n + 1] if isinstance(i, int) else gates[:, bass.ds(i, 1), n:n + 1].squeeze(1))
                        dve.wait_ge(s_x[p], 16 * (j + 1))
                        dve.wait_ge(s_bb, i + 1)
                        if not early(i, 2):
                            dve.wait_ge(s_out[p], 16 * j)
                        link(dve.tensor_tensor(y[:, p, :], x2[:, p, :], b_ps[0:ROWS, p, :], ALU.add))
                        dve.wait_ge(s_r[p], 32 * (j + 1))
                        link(dve.scalar_tensor_tensor(y[:, p, :], r[0][:, p, :], g(0), y[:, p, :], ALU.mult, ALU.add))
                        dve.scalar_tensor_tensor(y[:, p, :], r[1][:, p, :], g(1), y[:, p, :], ALU.mult, ALU.add).then_inc(s_y, 1)
                    steps(dve, BLOCKS, body)


def steps_even(eng, n, body):
    body(0, 0, 0)
    body(1, 0, 1)
    with eng.Fori(1, n // 2 - 1) as j:
        body(2 * j, j, 0)
        body(2 * j + 1, j, 1)
    body(n - 2, n // 2 - 1, 0)
    body(n - 1, n // 2 - 1, 1)


def product(pe, out, lhs, rhs, chunks, last):
    for k in chunks:
        for a, b in ((0, 0), (0, 1), (1, 0)):
            ins = pe.matmul(out, lhs[:, a, k, :], rhs[:, b, k, :], start=(k == 0 and a == b), stop=(k == last - 1 and a == 1))
    return ins


def turn_parts(pe, out, parts, ident16):
    n = parts.shape[0]
    for part in range(2):
        for k in range(KD):
            ins = pe.transpose(out[:, part, k, 0:n], parts[:, part, k * P:(k + 1) * P], ident16[0:n, 0:n])
    return ins


def layer_norm(dve, xt, xn, xs, stat, ln, s_ln, s_var, s_std, s_met, s_xf, s_xh, s_xn, i):
    link = Chain(dve, s_ln, 6 * i)
    dve.bn_stats(stat[:, 0, :], xt[:, 0:512])
    link(dve.bn_stats(stat[:, 1, :], xt[:, 512:1024]), s_met)
    link(dve.bn_aggr(ln[:, 0:2], stat))
    dve.tensor_scalar(ln[:, 2:3], ln[:, 1:2], LN_EPS, None, ALU.add).then_inc(s_var, 1)
    dve.wait_ge(s_std, i + 1)
    link(dve.reciprocal(ln[:, 4:5], ln[:, 3:4]))
    link(dve.tensor_scalar(ln[:, 5:6], ln[:, 4:5], ln[:, 4:5], ln[:, 2:3], ALU.mult, ALU.mult))
    link(dve.tensor_scalar(ln[:, 6:7], ln[:, 5:6], -0.5, 1.5, ALU.mult, ALU.add))
    dve.tensor_tensor(ln[:, 7:8], ln[:, 6:7], ln[:, 4:5], ALU.mult).then_inc(s_ln, 1)
    if not early(i, 1):
        dve.wait_ge(s_xn, i)
    dve.wait_ge(s_ln, 6 * i + 6)
    dve.tensor_scalar(xn, xt, ln[:, 0:1], ln[:, 7:8], ALU.subtract, ALU.mult).then_inc(s_xf, 1)
    dve.wait_ge(s_xf, i + 1)
    dve.wait_ge(s_xh, i + 1)
    dve.tensor_tensor(xs[:, 1, :], xn, xs[:, 0, :], ALU.subtract).then_inc(s_xn, 1)


_INS = ['x', 'src', 'dst', 'L0_gnn_W', 'L0_gnn_att_src', 'L0_gnn_att_dst', 'L0_gnn_bias', 'L0_ffn_Wp',
        'L0_ffn_sim_matrix', 'L0_ffn_temperature', 'L0_ffn_W1', 'L0_ffn_b1', 'L0_ffn_W2', 'L0_ffn_b2']


def kernel(**inputs):
    import numpy as _np
    import concourse.bacc as _bacc
    from concourse import mybir as _mybir
    from concourse.bass_utils import run_bass_kernel_spmd as _run

    nc = _bacc.Bacc("TRN2", target_bir_lowering=False, num_devices=1)
    arrays, args = {}, []
    for name in _INS:
        a = _np.ascontiguousarray(inputs[name])
        if a.ndim == 0:
            a = a.reshape(1)
        arrays[f"in_{name}_dram"] = a
        args.append(nc.dram_tensor(f"in_{name}_dram", a.shape, _mybir.dt.from_np(a.dtype), kind="ExternalInput").ap())
    args.append(nc.dram_tensor("out_0_dram", (NODES, D), F32, kind="ExternalOutput").ap())
    program(nc, *args)
    r = _run(nc, [arrays], core_ids=[0])
    return r.results[0]["out_0_dram"]
```

```python
from contextlib import ExitStack

import concourse.bass as bass
from concourse import mybir

F32 = mybir.dt.float32
I32 = mybir.dt.int32
U32 = mybir.dt.uint32
F16 = mybir.dt.float16
ALU = mybir.AluOpType
ACT = mybir.ActivationFunctionType
AX = mybir.AxisListType

P = 128
NODES, EDGES, D = 3125, 50000, 1024
HEADS, C = 4, 256
NX, FF = 8, 512
ROWS = 125
BLOCKS = NODES // ROWS
KD, KF = D // P, FF // P
TILES = -(-EDGES // P)
VISITS = TILES + BLOCKS
VP = VISITS // 4
ROW4 = 4 * P
CHUNK = VISITS // 8
HI = -(-NODES // P)
WS = 64.0
SUMS = 2 * HEADS + 1
PACK = 2 + 2 * SUMS
PAIRS = 2 * NODES
XTILES = (PAIRS + NX * P - 1) // P
WPIECES, WCOLS = 4, 2 * D * FF // P // 4
BITS = 5
BIG = 1e30
LN_EPS = 1e-5
NORM_EPS = 1e-12
SLOPE = 0.2


def steps(eng, n, body, peel=2, tail=0):
    end = (n - tail) // 2
    for i in range(peel):
        body(i, i // 2, i % 2)
    with eng.Fori(peel // 2, end) as j:
        body(2 * j, j, 0)
        body(2 * j + 1, j, 1)
    for i in range(2 * end, n):
        body(i, i // 2, i % 2)


def early(i, n):
    return isinstance(i, int) and i < n


def rows_of(t, i):
    if isinstance(i, int):
        return t[ROWS * i:ROWS * (i + 1), :]
    return t[bass.ds(ROWS * i, ROWS), :]


def at(t, i):
    return t[:, i] if isinstance(i, int) else t[:, bass.ds(i, 1)].squeeze(1)


def wait_apart(eng, met, sem, value):
    if not isinstance(value, int):
        eng.lower_val(value)
    eng.wait_ge(met, 1)
    eng.wait_ge(sem, value)


def visit_word(eng, words, n, g):
    w = eng.value_load(words[:, n, g:g + 1] if isinstance(g, int) else words[:, n, bass.ds(g, 1)])

    def block(u):
        return ((w >> (BITS * u)) & ((1 << BITS) - 1)).with_bounds(min_val=0, max_val=BLOCKS - 1)

    def flag(u):
        return (w >> (4 * BITS + u)) & 1
    return block, flag


class Chain:

    def __init__(self, eng, sem, base=0):
        self.eng, self.sem, self.n = eng, sem, base

    def __call__(self, instruction, apart=None):
        instruction.then_inc(self.sem, 1)
        self.n = self.n + 1
        if apart is not None:
            wait_apart(self.eng, apart, self.sem, self.n)
        else:
            self.eng.wait_ge(self.sem, self.n)


def program(nc, x, src, dst, W, att_src, att_dst, bias, Wp, sim, temp, W1, b1, W2, b2, out):
    def dram(name, shape, dt=F32):
        return nc.dram_tensor(name, shape, dt).ap()

    src_d = dram("src_padded", (VISITS - BLOCKS + 1, P), I32)
    dst_d = dram("dst_padded", (VISITS - BLOCKS + 1, P), I32)
    lo_d = dram("src_lo_by_visit", (VISITS, P), F16)
    dloc_d = dram("dst_local_by_visit", (VISITS, P), F16)
    xp_d = dram("projected", (NODES, 2 * D), F16)
    st_d = dram("node_terms", (NODES, 4 * HEADS), F16)
    x2_d = dram("x_after_gnn", (NODES, D))
    x2n_d = dram("x_after_gnn_normed", (NODES, 2 * D), F16)
    tok_d = dram("token_of_slot", (XTILES * P, 1), I32)
    eo_d = dram("expert_rows", (XTILES * P, D))

    ctx = ExitStack()

    def sem(name):
        return ctx.enter_context(nc.semaphore(name))

    def sbuf(c, name, shape, dt=F32):
        return c.enter_context(nc.sbuf_tensor(name, shape, dt))

    def psum(c, name, shape):
        return c.enter_context(nc.psum_tensor(name, shape, F32))

    s_met = sem("always_met")

    with ctx:
        shifted = sbuf(ctx, "shifted", [P, P + 2])
        ident = shifted[:, 1:P + 1]
        iota_col = sbuf(ctx, "iota_col", [P, 1])
        unit = sbuf(ctx, "unit", [P, 1])
        iota_row = sbuf(ctx, "iota_row", [P, P])
        ones = sbuf(ctx, "ones", [P, P])
        words = sbuf(ctx, "visit_words", [1, 2, VP], I32)
        WpT = sbuf(ctx, "WpT", [P, 2, KD, D], F16)
        Msim = sbuf(ctx, "Msim", [P, 2, KD, NX], F16)
        ident16 = sbuf(ctx, "ident16", [P, P], F16)
        iota16 = sbuf(ctx, "iota16", [P, P], F16)
        stN = sbuf(ctx, "node_terms_sb", [ROWS, BLOCKS, 2 * HEADS])
        nsq = sbuf(ctx, "proj_sq", [ROWS, BLOCKS])
        scores = sbuf(ctx, "scores", [ROWS, BLOCKS, NX])
        slot_i = sbuf(ctx, "slots", [ROWS, BLOCKS, 2], I32)
        gates = sbuf(ctx, "gates", [ROWS, BLOCKS, 2])
        comb = sbuf(ctx, "comb", [ROWS, BLOCKS, NX])
        x_i = sbuf(ctx, "tile_experts", [1, 4, XTILES], I32)

        edge_ctx = ExitStack()
        srcT = sbuf(edge_ctx, "srcT", [P, VISITS], I32)
        dlocT = sbuf(edge_ctx, "dlocT", [P, VISITS])
        PK = sbuf(edge_ctx, "PK", [P, VISITS, PACK], F16)
        early_ctx = ExitStack()
        hiT = sbuf(early_ctx, "hiT", [P, VISITS])
        dstV = sbuf(early_ctx, "dstV", [VP, ROW4])

        load_ctx = ExitStack()
        Wp_f = sbuf(load_ctx, "Wp_f", [P, KD, D])
        W_f = sbuf(load_ctx, "W_f", [P, KD, D])
        s_ldp, s_ldw = sem("rw_wp_in"), sem("rw_w_in")
        with ExitStack() as c:
            e_i = [sbuf(c, f"edges_i{n}", [98, ROW4], I32) for n in range(2)]
            dst_f = sbuf(c, "dst_f", [98, ROW4])
            junk = sbuf(c, "junk", [98, ROW4])
            cnt = sbuf(c, "cnt", [98, BLOCKS - 1])
            thr_i = sbuf(c, "thr_i", [P, 2, BLOCKS - 1], I32)
            thr = sbuf(c, "thr", [P, 2, BLOCKS - 1])
            visit_x = sbuf(c, "visit_x", [VP, 8])
            cmp_x = sbuf(c, "cmp_x", [VP, 8, BLOCKS - 1])
            b_x = sbuf(c, "b_x", [VP, 8])
            coef = sbuf(c, "word_coef", [VP, 8])
            parts_x = sbuf(c, "word_parts", [VP, 2, 8])
            word_v = sbuf(c, "word_v", [VP, 2])
            nb_v = sbuf(c, "nb_v", [VP, 4])
            tile_v = sbuf(c, "tile_v", [VP, 4])
            tile_i = sbuf(c, "tile_i", [VP, 4], I32)
            srcVi = sbuf(c, "srcVi", [VP, ROW4], I32)
            dstVi = sbuf(c, "dstVi", [VP, ROW4], I32)
            bitsVi = sbuf(c, "bitsVi", [VP, 2, ROW4], I32)
            fV = sbuf(c, "fV", [VP, 4, ROW4])
            rowV = sbuf(c, "rowV", [VP, 2, ROW4], F16)
            cnt_ps = psum(c, "cnt_ps", [P, 512])
            t_ps = psum(c, "t_ps", [P, 3, 4, P])
            s_const, s_pad, s_edges, s_dram = sem("ix_const"), sem("ix_pad"), sem("ix_edges"), sem("ix_dram")
            s_chain, s_cnt, s_cntps, s_idx = sem("ix_chain"), sem("ix_cnt"), sem("ix_cntps"), sem("ix_idx")
            s_vload, s_vals, s_tr, s_vstore = sem("ix_vload"), sem("ix_vals"), sem("ix_tr"), sem("ix_vstore")
            s_sel, s_rowv, s_word, s_wordT = sem("ix_sel"), sem("ix_rowv"), sem("ix_word"), sem("ix_wordT")
            full = (EDGES // ROW4)
            with nc.Block() as block:
                @block.scalar
                def _(act):
                    act.wait_ge(s_edges, 64)
                    act.dma_start(Wp_f[:, :, :], Wp.rearrange("(k p) d -> p k d", p=P)).then_inc(s_ldp, 16)
                    act.dma_start(W_f[:, :, :], W.rearrange("(k p) n -> p k n", p=P)).then_inc(s_ldw, 16)

                @block.gpsimd
                def _(pool):
                    pool.memset(shifted[:, :], 0.0).then_inc(s_sel, 1)
                    pool.memset(ones[:, :], 1.0).then_inc(s_const, 1)
                    pool.memset(unit[:, :], 1.0).then_inc(s_met, 1)
                    pool.iota(iota_col[:, :], pattern=[[0, 1]], base=0, channel_multiplier=1,
                              allow_small_or_imprecise_dtypes=True).then_inc(s_const, 1)
                    pool.iota(iota_row[:, :], pattern=[[1, P]], base=0, channel_multiplier=0,
                              allow_small_or_imprecise_dtypes=True).then_inc(s_const, 1)
                    pool.iota(visit_x[:, :], pattern=[[1, 8]], base=-3, channel_multiplier=4,
                              allow_small_or_imprecise_dtypes=True).then_inc(s_const, 1)
                    for u in range(4):
                        pool.memset(coef[:, u:u + 1], float(1 << (BITS * u)))
                        ins = pool.memset(coef[:, 4 + u:5 + u], float(1 << (4 * BITS + u)))
                    ins.then_inc(s_const, 1)
                    pool.wait_ge(s_sel, 1)
                    pool.affine_select(out=shifted[:, :], in_=shifted[:, :], compare_op=ALU.not_equal,
                                       fill=1.0, base=1, pattern=[[-1, P + 2]],
                                       channel_multiplier=1).then_inc(s_const, 1)
                    pool.wait_ge(s_idx, 1)
                    pool.wait_ge(s_dram, 32)
                    for q in range(4):
                        for dram_t, sb_t in ((src_d, srcVi), (dst_d, dstVi)):
                            pool.indirect_dma_start(
                                out=sb_t[:, q * P:(q + 1) * P], out_offset=None, in_=dram_t[:, :],
                                in_offset=bass.IndirectOffsetOnAxis(ap=tile_i[:, q:q + 1], axis=0),
                            ).then_inc(s_vload, 16)

                @block.sync
                def _(sp):
                    sp.wait_ge(s_pad, 2)
                    for t, d in ((e_i[0], src), (e_i[1], dst)):
                        sp.dma_start(t[0:full, :], d[0:full * ROW4].rearrange("(p n) -> p n", n=ROW4)).then_inc(s_edges, 16)
                        sp.dma_start(t[full:full + 1, 0:EDGES - full * ROW4],
                                     d[full * ROW4:EDGES].rearrange("(a n) -> a n", a=1)).then_inc(s_edges, 16)
                    sp.wait_ge(s_edges, 64)
                    for t, d in ((e_i[0], src_d), (e_i[1], dst_d)):
                        sp.dma_start(d.rearrange("(p r) n -> p (r n)", r=4), t[:, :]).then_inc(s_dram, 16)
                    sp.wait_ge(s_rowv, 1)
                    sp.dma_start(lo_d.rearrange("(p r) n -> p (r n)", r=4), rowV[:, 0, :]).then_inc(s_vstore, 16)
                    sp.dma_start(dloc_d.rearrange("(p r) n -> p (r n)", r=4), rowV[:, 1, :]).then_inc(s_vstore, 16)
                    sp.wait_ge(s_vstore, 32)

                @block.vector
                def _(dve):
                    link = Chain(dve, s_chain)
                    dve.memset(e_i[0][:, :], 0).then_inc(s_pad, 1)
                    dve.memset(e_i[1][:, :], NODES).then_inc(s_pad, 1)
                    dve.wait_ge(s_edges, 64)
                    link(dve.tensor_copy(dst_f[:, :], e_i[1][:, :]))
                    for b in range(1, BLOCKS):
                        dve.tensor_scalar(junk[:, :], dst_f[:, :], float(ROWS * b), None, ALU.is_lt, ALU.add,
                                          accum_out=cnt[:, b - 1:b]).then_inc(s_cnt, 1)
                        dve.wait_ge(s_cnt, b)
                    dve.wait_ge(s_cntps, 1)
                    dve.wait_ge(s_const, 6)
                    link(dve.tensor_copy(thr_i[:, 0, :], cnt_ps[:, 0:BLOCKS - 1]))
                    link(dve.tensor_scalar(thr_i[:, 1, :], thr_i[:, 0, :], 7, None, ALU.arith_shift_right))
                    link(dve.tensor_copy(thr[:, 0, :], thr_i[:, 1, :]))
                    link(dve.tensor_tensor(thr[:, 1, :], thr[:, 0, :], iota_row[:, 1:BLOCKS], ALU.add))
                    link(dve.tensor_tensor(cmp_x[:, :, :], visit_x[:, :].unsqueeze(2).broadcast_to([VP, 8, BLOCKS - 1]),
                                           thr[0:VP, 1, :].unsqueeze(1).broadcast_to([VP, 8, BLOCKS - 1]), ALU.is_ge))
                    link(dve.tensor_reduce(b_x[:, :], cmp_x[:, :, :], AX.X, ALU.add))
                    link(dve.tensor_tensor(tile_v[:, :], visit_x[:, 3:7], b_x[:, 3:7], ALU.subtract))
                    dve.tensor_copy(tile_i[:, :], tile_v[:, :]).then_inc(s_idx, 1)
                    dve.tensor_scalar(nb_v[:, :], b_x[:, 3:7], float(ROWS), None, ALU.mult)
                    dve.tensor_copy(parts_x[:, 0, 0:4], b_x[:, 3:7])
                    dve.tensor_copy(parts_x[:, 1, 0:4], b_x[:, 1:5])
                    dve.tensor_tensor(parts_x[:, 0, 4:8], b_x[:, 3:7], b_x[:, 2:6], ALU.not_equal)
                    link(dve.tensor_tensor(parts_x[:, 1, 4:8], b_x[:, 1:5], b_x[:, 2:6], ALU.not_equal))
                    link(dve.tensor_tensor(parts_x[:, :, :], parts_x[:, :, :],
                                           coef[:, :].unsqueeze(1).broadcast_to([VP, 2, 8]), ALU.mult))
                    dve.tensor_reduce(word_v[:, :], parts_x[:, :, :], AX.X, ALU.add).then_inc(s_word, 1)
                    dve.tensor_copy(ident16[:, :], ident)
                    dve.tensor_copy(iota16[:, :], iota_row[:, :])
                    dve.wait_ge(s_wordT, 1)
                    dve.tensor_copy(words[:, :, :], cnt_ps[0:1, P:3 * P].rearrange("a (n g) -> a n g", n=2)[:, :, 0:VP])
                    dve.wait_ge(s_vload, 128)
                    dve.tensor_scalar(bitsVi[:, 0, :], srcVi[:, :], 7, None, ALU.arith_shift_right)
                    link(dve.tensor_scalar(bitsVi[:, 1, :], srcVi[:, :], P - 1, None, ALU.bitwise_and))
                    dve.tensor_copy(fV[:, 0, :], srcVi[:, :])
                    dve.tensor_copy(fV[:, 1:3, :], bitsVi[:, :, :])
                    link(dve.tensor_copy(dstV[:, :], dstVi[:, :]))
                    for q in range(4):
                        ins = dve.tensor_scalar(fV[:, 3, q * P:(q + 1) * P], dstV[:, q * P:(q + 1) * P],
                                                nb_v[:, q:q + 1], None, ALU.subtract)
                    ins.then_inc(s_vals, 1)
                    dve.wait_ge(s_vals, 1)
                    dve.tensor_copy(rowV[:, :, :], fV[:, 2:4, :]).then_inc(s_rowv, 1)
                    dve.wait_ge(s_tr, 3)
                    for n, t in enumerate((srcT, hiT, dlocT)):
                        dve.tensor_copy(t[:, :].rearrange("k (p q) -> k q p", q=4), t_ps[:, n, :, 0:VP])

                @block.tensor
                def _(pe):
                    pe.wait_ge(s_cnt, BLOCKS - 1)
                    pe.wait_ge(s_const, 6)
                    pe.matmul(cnt_ps[:, 0:BLOCKS - 1], ones[0:98, :], cnt[:, :], start=True, stop=True).then_inc(s_cntps, 1)
                    pe.wait_ge(s_word, 1)
                    for n in range(2):
                        ins = pe.transpose(cnt_ps[0:1, P * (n + 1):P * (n + 1) + VP], word_v[:, n:n + 1], ident[0:VP, 0:VP])
                    ins.then_inc(s_wordT, 1)
                    pe.wait_ge(s_vals, 1)
                    for n, f in enumerate((0, 1, 3)):
                        for q in range(4):
                            ins = pe.transpose(t_ps[:, n, q, 0:VP], fV[:, f, q * P:(q + 1) * P], ident[0:VP, 0:VP])
                        ins.then_inc(s_tr, 1)

        w_ctx = ExitStack()
        W_sb = sbuf(w_ctx, "W_sb", [P, 2, KD, D], F16)
        Watt = sbuf(w_ctx, "Watt", [P, 2, KD, 2 * HEADS], F16)
        with ExitStack() as c:
            att = sbuf(c, "att", [P, 2, D])
            prod = sbuf(c, "w_prod", [P, 4, 2, D])
            watt_f = sbuf(c, "watt_f", [P, KD, 2 * HEADS])
            sim_sb = sbuf(c, "sim_sb", [NX, D])
            simn = sbuf(c, "simn", [NX, D])
            sq = simn
            col = sbuf(c, "sim_col", [NX, 4])
            simT = sbuf(c, "simT", [P, KD, NX])
            w_ps = psum(c, "w_ps", [P, 4, 512])
            m_ps = psum(c, "m_ps", [P, 2, KD, NX])
            s_sim, s_lda, s_c, s_n, s_sn = sem("rw_sim_in"), sem("rw_att_in"), sem("rw_chain"), sem("rw_norm"), sem("rw_sim")
            s_wt, s_we, s_wl, s_st, s_se, s_m = sem("rw_wt"), sem("rw_whi"), sem("rw_wlo"), sem("rw_simt"), sem("rw_simevac"), sem("rw_m")
            s_wh, s_prod, s_sum = sem("rw_w_hi"), sem("rw_prod"), sem("rw_sum")
            with nc.Block() as block:
                @block.sync
                def _(sp):
                    sp.dma_start(sim_sb[:, :], sim).then_inc(s_sim, 16)
                    for n, a in enumerate((att_src, att_dst)):
                        sp.dma_start(att[:, n, :], a.rearrange("h c -> (h c)").partition_broadcast(P)).then_inc(s_lda, 16)

                @block.gpsimd
                def _(pool):
                    pool.wait_ge(s_ldw, 16)
                    pool.wait_ge(s_lda, 32)
                    for k in range(KD):
                        if k >= 4:
                            pool.wait_ge(s_sum, k - 3)
                        for n in range(2):
                            ins = pool.tensor_tensor(prod[:, k % 4, n, :], W_f[:, k, :], att[:, n, :], ALU.mult)
                        ins.then_inc(s_prod, 1)

                @block.scalar
                def _(act):
                    act.wait_ge(s_c, 2)
                    act.activation(col[:, 1:2], col[:, 0:1], ACT.Sqrt).then_inc(s_n, 1)
                    for n in range(2 * KD):
                        act.wait_ge(s_wt, n + 1)
                        act.activation(WpT[:, 0, n // 2, (n % 2) * 512:(n % 2 + 1) * 512], w_ps[:, n % 4, :],
                                       ACT.Copy, scale=WS).then_inc(s_we, 1)
                    act.wait_ge(s_ldw, 16)
                    for k in range(KD):
                        act.activation(W_sb[:, 0, k, :], W_f[:, k, :], ACT.Copy, scale=WS).then_inc(s_wh, 1)

                @block.vector
                def _(dve):
                    link = Chain(dve, s_c)
                    dve.wait_ge(s_sim, 16)
                    link(dve.tensor_tensor(sq[:, :], sim_sb[:, :], sim_sb[:, :], ALU.mult))
                    link(dve.tensor_reduce(col[:, 0:1], sq[:, :], AX.X, ALU.add))
                    dve.wait_ge(s_n, 1)
                    link(dve.tensor_scalar(col[:, 2:3], col[:, 1:2], NORM_EPS, None, ALU.max))
                    link(dve.reciprocal(col[:, 3:4], col[:, 2:3]))
                    dve.tensor_scalar(simn[:, :], sim_sb[:, :], col[:, 3:4], None, ALU.mult).then_inc(s_sn, 1)
                    dve.wait_ge(s_st, 1)
                    dve.tensor_copy(simT[:, :, :], m_ps[:, 0, :, :]).then_inc(s_se, 1)
                    for n in range(2 * KD):
                        dve.wait_ge(s_we, n + 1)
                        cols = slice((n % 2) * 512, (n % 2 + 1) * 512)
                        dve.scalar_tensor_tensor(WpT[:, 1, n // 2, cols], w_ps[:, n % 4, :], WS, WpT[:, 0, n // 2, cols],
                                                 ALU.mult, ALU.subtract).then_inc(s_wl, 1)
                    dve.wait_ge(s_m, 1)
                    link(dve.tensor_scalar(Msim[:, 0, :, :], m_ps[:, 1, :, :], WS, None, ALU.mult))
                    dve.scalar_tensor_tensor(Msim[:, 1, :, :], m_ps[:, 1, :, :], WS, Msim[:, 0, :, :], ALU.mult, ALU.subtract)
                    dve.wait_ge(s_ldw, 16)
                    dve.wait_ge(s_lda, 32)
                    for k in range(KD):
                        dve.wait_ge(s_prod, k + 1)
                        dve.tensor_reduce(watt_f[:, k, :], prod[:, k % 4, :, :].rearrange("r n (h c) -> r (n h) c", h=HEADS),
                                          AX.X, ALU.add).then_inc(s_sum, 1)
                        dve.wait_ge(s_wh, k + 1)
                        dve.scalar_tensor_tensor(W_sb[:, 1, k, :], W_f[:, k, :], WS, W_sb[:, 0, k, :], ALU.mult, ALU.subtract)
                    dve.wait_ge(s_sum, KD)
                    link(dve.tensor_scalar(Watt[:, 0, :, :], watt_f[:, :, :], WS, None, ALU.mult))
                    dve.scalar_tensor_tensor(Watt[:, 1, :, :], watt_f[:, :, :], WS, Watt[:, 0, :, :], ALU.mult, ALU.subtract)

                @block.tensor
                def _(pe):
                    pe.wait_ge(s_sn, 1)
                    for k in range(KD):
                        ins = pe.transpose(m_ps[:, 0, k, :], simn[:, k * P:(k + 1) * P], ident[0:NX, 0:NX])
                    ins.then_inc(s_st, 1)
                    pe.wait_ge(s_ldp, 16)
                    for n in range(2 * KD):
                        if n >= 4:
                            pe.wait_ge(s_wl, n - 3)
                        for q in range(4):
                            e = (n % 2) * 4 + q
                            ins = pe.transpose(w_ps[:, n % 4, q * P:(q + 1) * P],
                                               Wp_f[:, e, (n // 2) * P:(n // 2 + 1) * P], ident)
                        ins.then_inc(s_wt, 1)
                    pe.wait_ge(s_se, 1)
                    for k in range(KD):
                        for e in range(KD):
                            ins = pe.matmul(m_ps[:, 1, k, :], Wp_f[:, e, k * P:(k + 1) * P], simT[:, e, :],
                                            start=(e == 0), stop=(e == KD - 1))
                    ins.then_inc(s_m, 1)

        with load_ctx, w_ctx, ExitStack() as c:
            xt = sbuf(c, "xt", [ROWS, 2, D])
            xn = sbuf(c, "xn", [ROWS, D])
            xs = sbuf(c, "xs", [ROWS, 2, 2, D], F16)
            xsT = sbuf(c, "xsT", [P, 2, 2, KD, ROWS], F16)
            xp = sbuf(c, "xp", [ROWS, 2, 2, D], F16)
            stat = sbuf(c, "stat", [ROWS, 2, 2, 6])
            ln = sbuf(c, "ln", [ROWS, 2, 10])
            tr_ps = c.enter_context(nc.psum_tensor("tr_ps", [P, 2, KD, P], F16))
            pj_ps = psum(c, "pj_ps", [P, 2, D])
            st_ps = psum(c, "st_ps", [P, 2, 512])
            s_ln, s_var, s_std = sem("pj_ln"), sem("pj_var"), sem("pj_std")
            s_x = [sem(f"pj_x{p}") for p in range(2)]
            s_xf, s_xh, s_xn, s_tr, s_xnT, s_mm, s_xp, s_lo = (
                sem("pj_xf"), sem("pj_xh"), sem("pj_xn"), sem("pj_tr"), sem("pj_xnT"), sem("pj_mm"), sem("pj_xp"), sem("pj_lo"))
            s_out = [sem(f"pj_out{p}") for p in range(2)]
            with nc.Block() as block:
                @block.sync
                def _(sp):
                    def load(i, j, p):
                        if not early(i, 2):
                            sp.wait_ge(s_xf, i - 1)
                        sp.dma_start(xt[:, p, :], rows_of(x, i)).then_inc(s_x[p], 16)
                    steps(sp, BLOCKS, load)

                @block.gpsimd
                def _(pool):
                    def store(i, j, p):
                        pool.wait_ge(s_lo, i + 1)
                        pool.dma_start(rows_of(xp_d, i), xp[:, p, :, :].rearrange("r n d -> r (n d)")).then_inc(s_out[p], 16)
                    steps(pool, BLOCKS, store)
                    pool.wait_ge(s_out[0], 16 * (BLOCKS - BLOCKS // 2))
                    pool.wait_ge(s_out[1], 16 * (BLOCKS // 2))

                @block.scalar
                def _(act):
                    def hi_proj(i, p):
                        act.wait_ge(s_mm, i + 1)
                        if not early(i, 2):
                            act.wait_ge(s_out[p], 8 * i if p == 0 else 8 * (i - 1))
                        act.activation(xp[:, p, 0, :], pj_ps[0:ROWS, p, :], ACT.Copy, scale=1.0 / WS).then_inc(s_xp, 1)

                    def body(i, j, p):
                        act.wait_ge(s_var, i + 1)
                        act.activation(ln[:, p, 3:4], ln[:, p, 2:3], ACT.Sqrt).then_inc(s_std, 1)
                        act.wait_ge(s_xf, i + 1)
                        if not early(i, 2):
                            act.wait_ge(s_tr, i - 1)
                        act.activation(xs[:, p, 0, :], xn[:, :], ACT.Copy).then_inc(s_xh, 1)
                        if not early(i, 1):
                            take_turned(i - 1, 1 - p)
                        if not early(i, 2):
                            hi_proj(i - 2, p)

                    def take_turned(i, p):
                        act.wait_ge(s_tr, i + 1)
                        if not early(i, 2):
                            act.wait_ge(s_mm, i - 1)
                        act.activation(xsT[:, p, :, :, :], tr_ps[:, :, :, 0:ROWS], ACT.Copy).then_inc(s_xnT, 1)
                    steps(act, BLOCKS, body, peel=4)
                    take_turned(BLOCKS - 1, (BLOCKS - 1) % 2)
                    for i in (BLOCKS - 2, BLOCKS - 1):
                        hi_proj(i, i % 2)

                @block.vector
                def _(dve):
                    def lo_proj(i, p):
                        dve.wait_ge(s_xp, i + 1)
                        dve.tensor_scalar(at(stN, i), st_ps[0:ROWS, p, 0:2 * HEADS], 1.0 / WS, None, ALU.mult)
                        dve.scalar_tensor_tensor(xp[:, p, 1, :], pj_ps[0:ROWS, p, :], 1.0 / WS, xp[:, p, 0, :],
                                                 ALU.mult, ALU.subtract).then_inc(s_lo, 1)

                    def body(i, j, p):
                        dve.wait_ge(s_x[p], 16 * (j + 1))
                        layer_norm(dve, xt[:, p, :], xn[:, :], xs[:, p, :, :], stat[:, p, :, :], ln[:, p, :],
                                   s_ln, s_var, s_std, s_met, s_xf, s_xh, s_xn, i)
                        if not early(i, 2):
                            lo_proj(i - 2, p)
                    steps(dve, BLOCKS, body, peel=4)
                    for i in (BLOCKS - 2, BLOCKS - 1):
                        lo_proj(i, i % 2)

                @block.tensor
                def _(pe):
                    def turn(i, p):
                        pe.wait_ge(s_xn, i + 1)
                        if not early(i, 1):
                            pe.wait_ge(s_xnT, i)
                        turn_parts(pe, tr_ps, xs[:, p, :, :], ident16).then_inc(s_tr, 1)

                    def body(i, j, p):
                        pe.wait_ge(s_xnT, i + 1)
                        if not early(i, 2):
                            pe.wait_ge(s_lo, i - 1)
                        lhs = xsT[:, p, :, :, :]
                        product(pe, pj_ps[0:ROWS, p, 0:512], lhs, W_sb[:, :, :, 0:512], range(KD), KD)
                        product(pe, st_ps[0:ROWS, p, 0:2 * HEADS], lhs, Watt[:, :, :, :], range(KD), KD)
                        product(pe, pj_ps[0:ROWS, p, 512:D], lhs, W_sb[:, :, :, 512:D], range(KD // 2), KD)
                        if not (isinstance(i, int) and i == BLOCKS - 1):
                            turn(i + 1, 1 - p)
                        product(pe, pj_ps[0:ROWS, p, 512:D], lhs, W_sb[:, :, :, 512:D], range(KD // 2, KD), KD).then_inc(s_mm, 1)
                    turn(0, 0)
                    steps(pe, BLOCKS, body)

        with ExitStack() as c:
            st16 = sbuf(c, "node_terms_parts", [ROWS, BLOCKS, 4 * HEADS], F16)
            lo_tab = sbuf(c, "lo_tab", [P, HI, 4 * HEADS], F16)
            lo_b = sbuf(c, "lo_b", [P, 2, CHUNK, P], F16)
            dl_b = sbuf(c, "dl_b", [ROWS, 2, CHUNK, P], F16)
            hi_oh = sbuf(c, "hi_oh", [P, 2, 4, HI])
            pick = sbuf(c, "pick", [P, 4, HEADS, HI])
            sT = sbuf(c, "sT", [P, VISITS, HEADS])
            dT = sbuf(c, "dT", [P, VISITS, 2 * HEADS])
            d_p = sbuf(c, "d_p", [P, VISITS, 2, 2 * HEADS])
            s_ps = [psum(c, f"s_ps{n}", [P, 4, HI * HEADS]) for n in range(2)]
            d_ps = [psum(c, f"d_ps{n}", [P, 512]) for n in range(2)]
            s_stw, s_tab, s_zero, s_st16 = sem("ed_stw"), sem("ed_tab"), sem("ed_zero"), sem("ed_st16")
            s_row = [sem(f"ed_row{p}") for p in range(2)]
            s_hioh = sem("ed_hioh")
            s_oh, s_grp, s_got, s_got_d, s_sel = sem("ed_oh"), sem("ed_grp"), sem("ed_got"), sem("ed_got_d"), sem("ed_sel")
            GR = CHUNK // 4
            with nc.Block() as block:
                @block.sync
                def _(sp):
                    def load(i, j, p):
                        if not early(i, 2):
                            sp.wait_ge(s_grp, GR * (i - 1))
                        for t, d, n in ((lo_b, lo_d, P), (dl_b, dloc_d, ROWS)):
                            part = d[CHUNK * i:CHUNK * (i + 1), :] if isinstance(i, int) else d[bass.ds(CHUNK * i, CHUNK), :]
                            sp.dma_start(t[:, p, :, :], part.partition_broadcast(n)).then_inc(s_row[p], 16)
                        if early(i, 1):
                            tables()

                    def tables():
                        sp.wait_ge(s_st16, 2)
                        sp.dma_start(st_d.rearrange("(b r) h -> r b h", r=ROWS), st16[:, :, :]).then_inc(s_stw, 16)
                        sp.wait_ge(s_stw, 16)
                        sp.wait_ge(s_zero, 1)
                        whole = NODES // P
                        sp.dma_start(lo_tab[:, 0:whole, :],
                                     st_d[0:whole * P, :].rearrange("(a p) h -> p a h", p=P)).then_inc(s_tab, 16)
                        sp.dma_start(lo_tab[0:NODES - whole * P, whole, :], st_d[whole * P:NODES, :]).then_inc(s_tab, 16)
                    steps(sp, 8, load)

                @block.vector
                def _(dve):
                    dve.memset(lo_tab[:, :, :], 0.0).then_inc(s_zero, 1)
                    dve.tensor_copy(st16[:, :, 0:2 * HEADS], stN[:, :, :]).then_inc(s_st16, 1)
                    dve.wait_ge(s_st16, 1)
                    dve.tensor_tensor(st16[:, :, 2 * HEADS:], stN[:, :, :], st16[:, :, 0:2 * HEADS], ALU.subtract).then_inc(s_st16, 1)

                    def build(i, j, p):
                        dve.wait_ge(s_row[p], 32 * (j + 1))
                        dve.tensor_scalar(lo_b[:, p, :, :], lo_b[:, p, :, :], iota_col[:, 0:1], None, ALU.is_equal)
                        dve.tensor_scalar(dl_b[:, p, :, :], dl_b[:, p, :, :], iota_col[0:ROWS, 0:1], None,
                                          ALU.is_equal).then_inc(s_oh, 1)

                    def body(i, j, p):
                        for q in range(GR):
                            if q == GR - 4 and not (isinstance(i, int) and i == 7):
                                build(i + 1, j + p, 1 - p)
                            n = GR * i + q
                            v = 4 * n
                            sl = slice(v, v + 4) if isinstance(v, int) else bass.ds(v, 4)
                            dve.wait_ge(s_hioh, n + 1)
                            if not early(n, 1):
                                dve.wait_ge(s_got, n)
                            dve.wait_ge(s_grp, n + 1)
                            dve.tensor_tensor(pick[:, :, :, :], s_ps[(p + q) % 2][:, :, :].rearrange("k v (a h) -> k v h a", h=HEADS),
                                              hi_oh[:, (p + q) % 2, :, :].unsqueeze(2).broadcast_to([P, 4, HEADS, HI]), ALU.mult).then_inc(s_sel, 1)
                            if not (isinstance(n, int) and n == VISITS // 4 - 1):
                                source_block(n + 1, (p + q + 1) % 2)
                            dve.wait_ge(s_sel, n + 1)
                            dve.tensor_reduce(sT[:, sl, :], pick[:, :, :, :], AX.X, ALU.add).then_inc(s_got, 1)

                    def source_block(n, p):
                        sl = slice(4 * n, 4 * n + 4) if isinstance(n, int) else bass.ds(4 * n, 4)
                        if not early(n, 2):
                            dve.wait_ge(s_sel, n - 1)
                        dve.tensor_tensor(hi_oh[:, p, :, :], iota_row[:, 0:HI].unsqueeze(1).broadcast_to([P, 4, HI]),
                                          hiT[:, sl].unsqueeze(2).broadcast_to([P, 4, HI]), ALU.is_equal).then_inc(s_hioh, 1)
                    source_block(0, 0)
                    build(0, 0, 0)
                    body(0, 0, 0)
                    with dve.Fori(0, 3) as j:
                        body(2 * j + 1, j, 1)
                        body(2 * j + 2, j + 1, 0)
                    body(7, 3, 1)
                    dve.wait_ge(s_got_d, VISITS // 4)
                    dve.tensor_tensor(dT[:, :, :], d_p[:, :, 0, :], d_p[:, :, 1, :], ALU.add)

                @block.scalar
                def _(act):
                    def body(n, j, p):
                        act.wait_ge(s_grp, n + 1)
                        d = d_p[:, 4 * n:4 * n + 4, :, :] if isinstance(n, int) else d_p[:, bass.ds(4 * n, 4), :, :]
                        act.activation(d, d_ps[p][:, 0:16 * HEADS].rearrange("k (v n h) -> k v n h", v=4, n=2), ACT.Copy).then_inc(s_got_d, 1)
                    steps(act, VISITS // 4, body)

                @block.tensor
                def _(pe):
                    pe.wait_ge(s_tab, 32)

                    def body(i, j, p):
                        pe.wait_ge(s_oh, i + 1)
                        for q in range(GR):
                            n = GR * i + q
                            if not early(n, 2):
                                pe.wait_ge(s_got, n - 1)
                            for u in range(4):
                                for part in range(2):
                                    h0 = 2 * HEADS * part
                                    pe.matmul(s_ps[(p + q) % 2][:, u, :].rearrange("k (a h) -> k a h", h=HEADS), lo_b[:, p, 4 * q + u, :],
                                              lo_tab[:, :, h0:h0 + HEADS], start=(part == 0), stop=(part == 1))
                            if not early(n, 2):
                                pe.wait_ge(s_got_d, n - 1)
                            block_at, _ = visit_word(pe, words, 0, n)
                            for u in range(4):
                                ins = pe.matmul(d_ps[(p + q) % 2][:, 4 * HEADS * u:4 * HEADS * (u + 1)], dl_b[:, p, 4 * q + u, :],
                                                st16[:, bass.ds(block_at(u), 1), :].squeeze(1), start=True, stop=True)
                            ins.then_inc(s_grp, 1)
                    steps(pe, 8, body)

            with ExitStack() as c2:
                sV = sbuf(c2, "sV", [VP, HEADS, ROW4])
                run = sbuf(c2, "run", [VP, HEADS, ROW4])
                run2 = sbuf(c2, "run2", [VP, HEADS, ROW4])
                pen = sbuf(c2, "pen", [VP, 2, ROW4])
                ids = sbuf(c2, "ids", [VP, 2])
                cc = sbuf(c2, "cc", [VP, 2, 16])
                last4 = sbuf(c2, "last4", [VP, 2, 2, HEADS])
                sm = sbuf(c2, "sm", [HEADS, 2, 3, VP])
                carry = sbuf(c2, "carry", [VP, 2, 2, HEADS])
                spare = d_p[:, :, :, :].rearrange("k v n h -> k (v n h)")
                n_vh = VISITS * HEADS
                mT = spare[:, 0:n_vh].rearrange("k (v h) -> k v h", h=HEADS)
                mx = spare[:, n_vh:2 * n_vh].rearrange("k (v h) -> k v h", h=HEADS)
                work = spare[:, 2 * n_vh:4 * n_vh].rearrange("k (n v h) -> k n v h", n=2, h=HEADS)
                v_ps = [psum(c2, f"v_ps{h}", [P, 4, P]) for h in range(HEADS)]
                q_ps, r_ps = s_ps[0], s_ps[1]
                s_tv, s_ev, s_c, s_pq, s_dq, s_run, s_tb, s_d, s_e = (
                    sem("mx_tv"), sem("mx_ev"), sem("mx_chain"), sem("mx_pe"), sem("mx_dve"), sem("mx_run"),
                    sem("mx_tb"), sem("mx_d"), sem("mx_e"))
                with nc.Block() as block:
                    @block.tensor
                    def _(pe):
                        for h in range(HEADS):
                            for q in range(4):
                                ins = pe.transpose(v_ps[h][0:VP, q, :], sT[:, q::4, h], ident)
                            ins.then_inc(s_tv, 1)
                        flat = lambda t: t[:, :, :].rearrange("k v a -> k (v a)")
                        for w in range(2):
                            fwd = w == 0
                            hop = shifted[0:VP, 0:VP] if fwd else shifted[0:VP, 2:VP + 2]
                            src_id = ids[:, 1:2] if fwd else ids[:, 0:1]
                            pe.wait_ge(s_dq, 5 * w + 1)
                            pe.matmul(flat(q_ps)[0:VP, 0:1], hop, src_id, start=True, stop=True).then_inc(s_pq, 1)
                            pe.wait_ge(s_dq, 5 * w + 2)
                            pe.transpose(flat(r_ps)[0:HEADS, 0:VP], last4[:, w, 0, :], ident[0:VP, 0:VP])
                            pe.transpose(flat(r_ps)[0:HEADS, P:P + VP], last4[:, w, 1, :], ident[0:VP, 0:VP]).then_inc(s_pq, 1)
                            pe.wait_ge(s_dq, 5 * w + 3)
                            pe.transpose(flat(q_ps)[0:VP, 8:8 + HEADS], sm[:, w, 2, :], ident[0:HEADS, 0:HEADS]).then_inc(s_pq, 1)
                            pe.wait_ge(s_dq, 5 * w + 4)
                            pe.matmul(flat(q_ps)[0:VP, 16:16 + HEADS], hop, carry[:, w, 0, :], start=True, stop=True).then_inc(s_pq, 1)
                        pe.wait_ge(s_dq, 10)
                        for h in range(HEADS):
                            for q in range(4):
                                ins = pe.transpose(v_ps[h][:, q, 0:VP], run[:, h, q * P:(q + 1) * P], ident[0:VP, 0:VP])
                            ins.then_inc(s_tb, 1)

                    @block.scalar
                    def _(act):
                        for h in range(HEADS):
                            act.wait_ge(s_tv, h + 1)
                            act.activation(sV[:, h, :], v_ps[h][0:VP, :, :].rearrange("k q n -> k (q n)"), ACT.Copy).then_inc(s_ev, 1)
                        act.wait_ge(s_d, 1)
                        act.activation(work[:, 1, :, :], work[:, 0, :, :], ACT.Exp).then_inc(s_e, 1)

                    @block.vector
                    def _(dve):
                        link = Chain(dve, s_c)
                        flat = lambda t: t[:, :, :].rearrange("k v a -> k (v a)")
                        dve.tensor_scalar(ids[:, 0:1], dstV[:, 0:1], 1.0, None, ALU.add)
                        dve.tensor_scalar(ids[:, 1:2], dstV[:, ROW4 - 1:ROW4], 1.0, None, ALU.add)
                        dve.memset(pen[:, :, :], 0.0)
                        dve.memset(PK[:, :, SUMS:SUMS + 1], 1.0)
                        link(dve.memset(PK[:, :, 2 * SUMS:PACK], 0.0))
                        link(dve.tensor_tensor(pen[:, 0, 1:ROW4], dstV[:, 1:ROW4], dstV[:, 0:ROW4 - 1], ALU.not_equal))
                        link(dve.tensor_copy(pen[:, 1, 0:ROW4 - 1], pen[:, 0, 1:ROW4]))
                        link(dve.tensor_scalar(pen[:, :, :], pen[:, :, :], -BIG, None, ALU.mult))
                        dve.wait_ge(s_ev, HEADS)
                        for w in range(2):
                            fwd = w == 0
                            turn = (lambda a: a) if fwd else (lambda a: a[:, ::-1])
                            data = sV if fwd else run2
                            res = run2 if fwd else run
                            end = ROW4 - 1 if fwd else 0
                            f_id, l_id = (ids[:, 0:1], ids[:, 1:2]) if fwd else (ids[:, 1:2], ids[:, 0:1])
                            k = cc[:, w, :]
                            for h in range(HEADS):
                                ins = dve.tensor_tensor_scan(turn(res[:, h, :]), turn(pen[:, w, :]), turn(data[:, h, :]), -BIG, ALU.add, ALU.max)
                            link(ins)
                            dve.tensor_copy(last4[:, w, 0, :], res[:, :, end]).then_inc(s_dq, 1)
                            dve.wait_ge(s_pq, 4 * w + 1)
                            link(dve.tensor_tensor(k[:, 0:1], flat(q_ps)[0:VP, 0:1], f_id, ALU.is_equal))
                            link(dve.tensor_tensor(k[:, 1:2], f_id, l_id, ALU.is_equal))
                            link(dve.tensor_tensor(k[:, 2:3], k[:, 0:1], k[:, 1:2], ALU.mult))
                            link(dve.tensor_scalar(k[:, 3:5], k[:, 0:3:2], -1.0, BIG, ALU.add, ALU.mult))
                            link(dve.tensor_copy(last4[:, w, 1, :], k[:, 4:5].broadcast_to([VP, HEADS])))
                            dve.tensor_copy(k[:, 8:9], k[:, 4:5]).then_inc(s_dq, 1)
                            dve.wait_ge(s_pq, 4 * w + 2)
                            dve.tensor_copy(sm[:, w, 0, :], flat(r_ps)[0:HEADS, 0:VP])
                            link(dve.tensor_copy(sm[:, w, 1, :], flat(r_ps)[0:HEADS, P:P + VP]))
                            dve.tensor_tensor_scan(turn(sm[:, w, 2, :]), turn(sm[:, w, 1, :]), turn(sm[:, w, 0, :]), -BIG, ALU.add, ALU.max).then_inc(s_dq, 1)
                            dve.wait_ge(s_pq, 4 * w + 3)
                            dve.tensor_copy(carry[:, w, 0, :], flat(q_ps)[0:VP, 8:8 + HEADS]).then_inc(s_dq, 1)
                            dve.wait_ge(s_pq, 4 * w + 4)
                            link(dve.tensor_scalar(carry[:, w, 1, :], flat(q_ps)[0:VP, 16:16 + HEADS], k[:, 3:4], None, ALU.add))
                            for h in range(HEADS):
                                ins = dve.tensor_tensor_scan(turn(res[:, h, :]), turn(pen[:, w, :]), turn(data[:, h, :]),
                                                             carry[:, w, 1, h:h + 1], ALU.add, ALU.max)
                            ins.then_inc(s_dq, 1)
                            dve.wait_ge(s_dq, 5 * w + 5)
                        for h in range(HEADS):
                            dve.wait_ge(s_tb, h + 1)
                            ins = dve.tensor_copy(mT[:, :, h].rearrange("k (p q) -> k q p", q=4), v_ps[h][:, :, 0:VP])
                        link(ins)
                        t_d = dT[:, :, HEADS:2 * HEADS]
                        dve.tensor_copy(PK[:, :, 0:1], dlocT[:, :].unsqueeze(2))
                        link(dve.tensor_tensor(mx[:, :, :], mT[:, :, :], dT[:, :, 0:HEADS], ALU.max))
                        link(dve.tensor_tensor(work[:, 0, :, :], mx[:, :, :], t_d, ALU.add))
                        link(dve.tensor_tensor(work[:, 1, :, :], sT[:, :, :], t_d, ALU.add))
                        fw = work[:, :, :, :].rearrange("k n v h -> k n (v h)")
                        link(dve.scalar_tensor_tensor(fw, fw, SLOPE, fw, ALU.mult, ALU.max))
                        link(dve.tensor_tensor(work[:, 0, :, :], work[:, 1, :, :], work[:, 0, :, :], ALU.subtract))
                        dve.tensor_scalar(work[:, 0, :, :], work[:, 0, :, :], 0.0, None, ALU.min).then_inc(s_d, 1)
                        his = [slice(1 + HEADS, 1 + 2 * HEADS), slice(1, 1 + HEADS)]
                        for n, t in enumerate((mx[:, :, :], work[:, 1, :, :])):
                            if n == 1:
                                dve.wait_ge(s_e, 1)
                            lo = slice(his[n].start + SUMS, his[n].stop + SUMS)
                            link(dve.tensor_copy(PK[:, :, his[n]], t))
                            dve.tensor_tensor(PK[:, :, lo], t, PK[:, :, his[n]], ALU.subtract)
        early_ctx.close()

        acc_ctx = ExitStack()
        acc = sbuf(acc_ctx, "acc", [ROWS, BLOCKS, D])
        sacc = sbuf(acc_ctx, "sacc", [ROWS, BLOCKS, 2 * SUMS])
        with ExitStack() as c:
            rows = sbuf(c, "rows", [P, 8, 2, D], F16)
            O = sbuf(c, "O", [P, 4, 1 + 2 * HEADS, P], F16)
            pk = sbuf(c, "pk", [P, 2, 4, PACK])
            pk16 = sbuf(c, "pk16", [P, 2, 4, PACK], F16)
            idx = sbuf(c, "idx", [P, 2, 4], I32)
            main_ps = psum(c, "main_ps", [P, D])
            small_ps = psum(c, "small_ps", [P, 512])
            s_idx, s_done, s_pk, s_seen = sem("ms_idx"), sem("ms_done"), sem("ms_pk"), sem("ms_seen")
            s_oh, s_hi, s_lo = sem("ms_onehot"), sem("ms_hi"), sem("ms_lo")
            s_row = [sem(f"ms_row{k}") for k in range(8)]
            GROUPS = VISITS // 4
            with nc.Block() as block:
                @block.gpsimd
                def _(pool):
                    def body(i, j, p):
                        sl = slice(4 * i, 4 * i + 4) if isinstance(i, int) else bass.ds(4 * i, 4)
                        if not early(i, 2):
                            for k in range(4):
                                wait_apart(pool, s_met, s_row[4 * p + k], 16 * j)
                        pool.tensor_copy(idx[:, p, :], srcT[:, sl]).then_inc(s_idx, 1)
                        wait_apart(pool, s_met, s_idx, i + 1)
                        for k in range(4):
                            if not early(i, 2):
                                wait_apart(pool, s_met, s_done, 4 * i - 7 + k)
                            pool.indirect_dma_start(
                                out=rows[:, 4 * p + k, :, :].rearrange("k n d -> k (n d)"), out_offset=None, in_=xp_d[:, :],
                                in_offset=bass.IndirectOffsetOnAxis(ap=idx[:, p, k:k + 1], axis=0)).then_inc(s_row[4 * p + k], 16)
                    steps(pool, GROUPS, body)

                @block.vector
                def _(dve):
                    def take(b):
                        for n in range(2):
                            half = slice(n * 512, (n + 1) * 512)
                            a = acc[:, b, half] if isinstance(b, int) else acc[:, bass.ds(b, 1), half].squeeze(1)
                            dve.tensor_copy(a, main_ps[0:ROWS, half]).then_inc(s_seen, 1)
                        dve.tensor_copy(at(sacc, b), small_ps[0:ROWS, 0:2 * SUMS]).then_inc(s_seen, 1)

                    def body(i, j, p):
                        sl = slice(4 * i, 4 * i + 4) if isinstance(i, int) else bass.ds(4 * i, 4)
                        if not early(i, 2):
                            dve.wait_ge(s_done, 4 * (i - 1))
                        dve.tensor_copy(pk16[:, p, :, :], PK[:, sl, :]).then_inc(s_pk, 1)
                        dve.tensor_copy(pk[:, p, :, :], PK[:, sl, :]).then_inc(s_pk, 1)
                        block_at, last_at = visit_word(dve, words, 1, i)
                        dve.wait_ge(s_pk, 2 * i + 2)
                        for k in range(4):
                            v = 4 * i + k
                            if not early(i, 1):
                                dve.wait_ge(s_done, v - 3)
                            dve.tensor_scalar(O[:, k, 0, 0:ROWS], iota16[:, 0:ROWS], pk[:, p, k, 0:1], None,
                                              ALU.is_equal).then_inc(s_oh, 1)
                            dve.wait_ge(s_oh, v + 1)
                            for h in range(HEADS):
                                ins = dve.tensor_scalar(O[:, k, 1 + h, 0:ROWS], O[:, k, 0, 0:ROWS], pk[:, p, k, 1 + h:2 + h],
                                                        None, ALU.mult)
                            ins.then_inc(s_hi, 1)
                            if k % 2 == 1 and not early(v, 2):
                                with dve.If(last_at(k - 1) + last_at(k) > 0):
                                    for u in (k - 1, k):
                                        wait_apart(dve, s_met, s_done, v + u - k - 1)
                                        with dve.If(last_at(u) == 1):
                                            take(block_at(u))
                                        with dve.Else():
                                            dve.nop().then_inc(s_seen, 3)
                                with dve.Else():
                                    dve.nop().then_inc(s_seen, 6)
                    steps(dve, GROUPS, body)
                    dve.wait_ge(s_done, VISITS)
                    take(BLOCKS - 1)

                @block.scalar
                def _(act):
                    def body(i, j, p):
                        for k in range(4):
                            act.wait_ge(s_oh, 4 * i + k + 1)
                            for h in range(HEADS):
                                w = 1 + SUMS + h
                                ins = act.activation(O[:, k, 1 + HEADS + h, 0:ROWS], O[:, k, 0, 0:ROWS], ACT.Copy, scale=pk[:, p, k, w:w + 1])
                            ins.then_inc(s_lo, 1)
                    steps(act, GROUPS, body)

                @block.tensor
                def _(pe):
                    def products(p, k, first, v=0):
                        for h in range(HEADS):
                            if first and h % 2 == 0 and not early(v, 1):
                                pe.wait_ge(s_seen, 3 * v - 2 + h // 2)
                            for a, b in ((0, 0), (0, 1), (1, 0)):
                                pe.matmul(main_ps[0:ROWS, h * C:(h + 1) * C], O[:, k, 1 + HEADS * a + h, 0:ROWS],
                                          rows[:, 4 * p + k, b, h * C:(h + 1) * C],
                                          start=first and h % 2 == 0 and a == b, stop=True, skip_group_check=True)
                        if first and not early(v, 1):
                            pe.wait_ge(s_seen, 3 * v)
                        pe.matmul(small_ps[0:ROWS, 0:2 * SUMS], O[:, k, 0, 0:ROWS], pk16[:, p, k, 1:1 + 2 * SUMS],
                                  start=first, stop=True, skip_group_check=True).then_inc(s_done, 1)

                    def body(i, j, p):
                        _, first_at = visit_word(pe, words, 0, i)
                        for k in range(4):
                            v = 4 * i + k
                            pe.wait_ge(s_hi, v + 1)
                            pe.wait_ge(s_lo, v + 1)
                            pe.wait_ge(s_row[4 * p + k], 16 * (j + 1))
                            if early(v, 1):
                                products(p, k, True)
                                continue
                            with pe.If(first_at(k) == 1):
                                products(p, k, True, v)
                            with pe.Else():
                                products(p, k, False)
                    steps(pe, GROUPS, body)

        with edge_ctx, acc_ctx:
            with ExitStack() as c:
                xt = sbuf(c, "n_xt", [ROWS, 2, D])
                own16 = sbuf(c, "n_own16", [ROWS, 2, 2, D], F16)
                own = sbuf(c, "n_own", [ROWS, 2, D])
                x2 = sbuf(c, "n_x2", [ROWS, 2, D])
                xn = sbuf(c, "n_xn", [ROWS, D])
                bias_b = sbuf(c, "n_bias", [ROWS, D])
                spare = PK[:, :, :].rearrange("k v n -> k (v n)")
                n_T = 4 * KD * ROWS
                xsT = spare[:, 0:n_T].rearrange("k (p n c r) -> k p n c r", p=2, n=2, c=KD)
                xs = spare[0:ROWS, n_T:n_T + 4 * D].rearrange("k (p n d) -> k p n d", p=2, n=2)
                stat = sbuf(c, "n_stat", [ROWS, 2, 2, 6])
                ln = sbuf(c, "n_ln", [ROWS, 2, 10])
                wk = sbuf(c, "n_wk", [ROWS, 4, BLOCKS, HEADS])
                cn = sbuf(c, "n_cn", [ROWS, 3, BLOCKS])
                tr_ps = c.enter_context(nc.psum_tensor("n_tr", [P, 2, KD, P], F16))
                pj_ps = psum(c, "n_pj", [P, 2, D])
                sc_ps = psum(c, "n_sc", [P, 2, 512])
                s_b, s_ch, s_d, s_e = sem("nd_bias"), sem("nd_chain"), sem("nd_d"), sem("nd_e")
                s_x = [sem(f"nd_x{p}") for p in range(2)]
                s_own, s_x2c, s_x2, s_ln, s_var, s_std = sem("nd_own"), sem("nd_x2c"), sem("nd_x2"), sem("nd_ln"), sem("nd_var"), sem("nd_std")
                s_sum, s_xf, s_xh = sem("nd_sum"), sem("nd_xf"), sem("nd_xh")
                s_xn, s_tr, s_xnT, s_mm, s_sq, s_sc = sem("nd_xn"), sem("nd_tr"), sem("nd_xnT"), sem("nd_mm"), sem("nd_sq"), sem("nd_sc")
                s_out = [sem(f"nd_out{p}") for p in range(2)]
                w_own, z_inv = wk[:, 2, :, :], wk[:, 3, :, :]
                with nc.Block() as block:
                    @block.sync
                    def _(sp):
                        sp.dma_start(bias_b[:, :], bias.partition_broadcast(ROWS)).then_inc(s_b, 16)

                        def load(i, j, p):
                            if not early(i, 2):
                                sp.wait_ge(s_x2, i - 1)
                            sp.dma_start(xt[:, p, :], rows_of(x, i)).then_inc(s_x[p], 16)
                            sp.dma_start(own16[:, p, :, :].rearrange("r n d -> r (n d)"), rows_of(xp_d, i)).then_inc(s_x[p], 16)
                        steps(sp, BLOCKS, load)

                    @block.gpsimd
                    def _(pool):
                        def store(i, p):
                            pool.wait_ge(s_xn, i + 1)
                            pool.dma_start(rows_of(x2_d, i), x2[:, p, :]).then_inc(s_out[p], 16)
                            pool.dma_start(rows_of(x2n_d, i), xs[:, p, :, :].rearrange("r n d -> r (n d)")).then_inc(s_out[p], 16)

                        def body(i, j, p):
                            pool.wait_ge(s_x[p], 32 * (j + 1))
                            if not early(i, 2):
                                pool.wait_ge(s_x2, i - 1)
                            pool.tensor_tensor(own[:, p, :], own16[:, p, 0, :], own16[:, p, 1, :], ALU.add).then_inc(s_sum, 1)
                            if not early(i, 1):
                                store(i - 1, 1 - p)
                        steps(pool, BLOCKS, body)
                        store(BLOCKS - 1, (BLOCKS - 1) % 2)
                        pool.wait_ge(s_out[0], 32 * (BLOCKS - BLOCKS // 2))
                        pool.wait_ge(s_out[1], 32 * (BLOCKS // 2))

                    @block.vector
                    def _(dve):
                        link = Chain(dve, s_ch)
                        link(dve.tensor_tensor(sacc[:, :, 0:SUMS], sacc[:, :, 0:SUMS], sacc[:, :, SUMS:2 * SUMS], ALU.add))
                        s_n, t_n = stN[:, :, 0:HEADS], stN[:, :, HEADS:2 * HEADS]
                        wide = lambda a: a.unsqueeze(2).broadcast_to([ROWS, BLOCKS, HEADS])
                        link(dve.tensor_scalar(cn[:, 0, :], sacc[:, :, 2 * HEADS], 1.0, None, ALU.max))
                        link(dve.reciprocal(cn[:, 1, :], cn[:, 0, :]))
                        link(dve.tensor_scalar(cn[:, 0, :], sacc[:, :, 2 * HEADS], 1.0, None, ALU.min))
                        link(dve.tensor_scalar(cn[:, 2, :], cn[:, 0, :], -1.0, BIG, ALU.add, ALU.mult))
                        link(dve.tensor_tensor(wk[:, 0, :, :], sacc[:, :, HEADS:2 * HEADS], wide(cn[:, 1, :]), ALU.mult))
                        link(dve.tensor_tensor(wk[:, 0, :, :], wk[:, 0, :, :], wide(cn[:, 2, :]), ALU.add))
                        link(dve.tensor_tensor(wk[:, 0, :, :], wk[:, 0, :, :], s_n, ALU.max))
                        link(dve.tensor_tensor(wk[:, 0, :, :], wk[:, 0, :, :], t_n, ALU.add))
                        link(dve.tensor_tensor(wk[:, 1, :, :], s_n, t_n, ALU.add))
                        fl = wk[:, 0:2, :, :].rearrange("r n b h -> r (n b h)")
                        link(dve.scalar_tensor_tensor(fl, fl, SLOPE, fl, ALU.mult, ALU.max))
                        link(dve.tensor_tensor(wk[:, 0, :, :], wk[:, 1, :, :], wk[:, 0, :, :], ALU.subtract))
                        dve.tensor_scalar(wk[:, 1, :, :], wk[:, 0, :, :], 0.0, None, ALU.min).then_inc(s_d, 1)
                        dve.wait_ge(s_e, 1)
                        link(dve.tensor_tensor(wk[:, 1, :, :], wk[:, 0, :, :], sacc[:, :, 0:HEADS], ALU.add))
                        link(dve.reciprocal(z_inv, wk[:, 1, :, :]))
                        dve.tensor_tensor(w_own, wk[:, 0, :, :], z_inv, ALU.mult).then_inc(s_d, 1)
                        dve.wait_ge(s_b, 16)

                        def take_scores(i, p):
                            dve.wait_ge(s_mm, i + 1)
                            dve.tensor_scalar(at(scores, i), sc_ps[0:ROWS, p, 0:NX], 1.0 / WS, None, ALU.mult).then_inc(s_sc, 1)

                        def body(i, j, p):
                            link = Chain(dve, s_x2c, 2 * i)
                            dve.wait_ge(s_own, i + 1)
                            if not early(i, 2):
                                dve.wait_ge(s_out[p], 32 * j)
                            for h in range(HEADS):
                                sl = slice(h * C, (h + 1) * C)
                                a = acc[:, i, sl] if isinstance(i, int) else acc[:, bass.ds(i, 1), sl].squeeze(1)
                                z = z_inv[:, i, h:h + 1] if isinstance(i, int) else z_inv[:, bass.ds(i, 1), h:h + 1].squeeze(1)
                                ins = dve.scalar_tensor_tensor(x2[:, p, sl], a, z, own[:, p, sl], ALU.mult, ALU.add)
                            link(ins)
                            link(dve.tensor_tensor(own[:, p, :], x2[:, p, :], bias_b[:, :], ALU.add))
                            dve.scalar_tensor_tensor(x2[:, p, :], own[:, p, :], 0.0, xt[:, p, :], ALU.max, ALU.add).then_inc(s_x2, 1)
                            dve.wait_ge(s_x2, i + 1)
                            layer_norm(dve, x2[:, p, :], xn[:, :], xs[:, p, :, :], stat[:, p, :, :], ln[:, p, :],
                                       s_ln, s_var, s_std, s_met, s_xf, s_xh, s_xn, i)
                            if not early(i, 2):
                                take_scores(i - 2, p)
                        steps(dve, BLOCKS, body, peel=4)
                        for i in (BLOCKS - 2, BLOCKS - 1):
                            take_scores(i, i % 2)

                    @block.scalar
                    def _(act):
                        act.wait_ge(s_d, 1)
                        act.activation(wk[:, 0, :, :], wk[:, 1, :, :], ACT.Exp).then_inc(s_e, 1)
                        act.wait_ge(s_d, 2)

                        def square(i, p):
                            act.wait_ge(s_mm, i + 1)
                            act.activation(pj_ps[0:ROWS, p, :], pj_ps[0:ROWS, p, :], ACT.Square, scale=1.0 / WS,
                                           accum_out=nsq[:, i:i + 1] if isinstance(i, int) else nsq[:, bass.ds(i, 1)]).then_inc(s_sq, 1)

                        def scale_own(i, p):
                            act.wait_ge(s_sum, i + 1)
                            for h in range(HEADS):
                                w = w_own[:, i, h:h + 1] if isinstance(i, int) else w_own[:, bass.ds(i, 1), h:h + 1].squeeze(1)
                                ins = act.activation(own[:, p, h * C:(h + 1) * C], own[:, p, h * C:(h + 1) * C], ACT.Copy, scale=w)
                            ins.then_inc(s_own, 1)

                        def body(i, j, p):
                            act.wait_ge(s_var, i + 1)
                            act.activation(ln[:, p, 3:4], ln[:, p, 2:3], ACT.Sqrt).then_inc(s_std, 1)
                            if not early(i, 1):
                                take_turned(i - 1, 1 - p)
                            act.wait_ge(s_xf, i + 1)
                            if not early(i, 2):
                                act.wait_ge(s_tr, i - 1)
                                act.wait_ge(s_out[p], 32 * j)
                            act.activation(xs[:, p, 0, :], xn[:, :], ACT.Copy).then_inc(s_xh, 1)
                            if not (isinstance(i, int) and i == BLOCKS - 1):
                                scale_own(i + 1, 1 - p)
                            if not early(i, 2):
                                square(i - 2, p)

                        def take_turned(i, p):
                            act.wait_ge(s_tr, i + 1)
                            if not early(i, 2):
                                act.wait_ge(s_mm, i - 1)
                            act.activation(xsT[:, p, :, :, :], tr_ps[:, :, :, 0:ROWS], ACT.Copy).then_inc(s_xnT, 1)
                        scale_own(0, 0)
                        steps(act, BLOCKS, body, peel=4)
                        take_turned(BLOCKS - 1, (BLOCKS - 1) % 2)
                        for i in (BLOCKS - 2, BLOCKS - 1):
                            square(i, i % 2)

                    @block.tensor
                    def _(pe):
                        def turn(i, p):
                            pe.wait_ge(s_xn, i + 1)
                            if not early(i, 1):
                                pe.wait_ge(s_xnT, i)
                            turn_parts(pe, tr_ps, xs[:, p, :, :], ident16).then_inc(s_tr, 1)

                        def body(i, j, p):
                            pe.wait_ge(s_xnT, i + 1)
                            if not early(i, 2):
                                pe.wait_ge(s_sq, i - 1)
                                pe.wait_ge(s_sc, i - 1)
                            lhs = xsT[:, p, :, :, :]
                            product(pe, pj_ps[0:ROWS, p, 0:512], lhs, WpT[:, :, :, 0:512], range(KD), KD)
                            product(pe, sc_ps[0:ROWS, p, 0:NX], lhs, Msim[:, :, :, :], range(KD), KD)
                            product(pe, pj_ps[0:ROWS, p, 512:D], lhs, WpT[:, :, :, 512:D], range(KD // 2), KD)
                            if not (isinstance(i, int) and i == BLOCKS - 1):
                                turn(i + 1, 1 - p)
                            product(pe, pj_ps[0:ROWS, p, 512:D], lhs, WpT[:, :, :, 512:D], range(KD // 2, KD), KD).then_inc(s_mm, 1)
                        turn(0, 0)
                        steps(pe, BLOCKS, body)

        expert_ctx = ExitStack()
        b1_b = sbuf(expert_ctx, "b1_b", [P, NX, FF])
        w_f = sbuf(expert_ctx, "w_f", [P, WPIECES, WCOLS])
        w_p = sbuf(expert_ctx, "w_p", [P, 3, 2, WPIECES, WCOLS], F16)
        s_b1, s_w, s_whi, s_wlo = sem("xp_b1"), sem("xp_w"), sem("xp_whi"), sem("xp_wlo")

        def load_weights(sp, e):
            one = (lambda t: t[e:e + 1]) if isinstance(e, int) else (lambda t: t[bass.ds(e, 1), :, :])
            for n, w in enumerate((W1, W2)):
                half = w_f[:, n * WPIECES // 2:(n + 1) * WPIECES // 2, :].rearrange("p a b -> p (a b)")
                sp.dma_start(half.rearrange("p (k f) -> p k f", f=(FF, D)[n]),
                             one(w).rearrange("a (k p) f -> p (a k) f", p=P)).then_inc(s_w, 16)

        def high(act, pieces, e, q):
            act.wait_ge(s_w, 32 * (e + 1))
            for n in pieces:
                buf = w_p[:, q, 0, n, :] if isinstance(q, int) else w_p[:, bass.ds(q, 1), 0, n, :].squeeze(1)
                act.activation(buf, w_f[:, n, :], ACT.Copy, scale=WS).then_inc(s_whi, 1)

        def low(dve, pieces, e, q):
            for n in pieces:
                wait_apart(dve, s_met, s_whi, WPIECES * e + n + 1)
                buf = (lambda part: w_p[:, q, part, n, :]) if isinstance(q, int) else (lambda part: w_p[:, bass.ds(q, 1), part, n, :].squeeze(1))
                dve.scalar_tensor_tensor(buf(1), w_f[:, n, :], WS, buf(0), ALU.mult, ALU.subtract).then_inc(s_wlo, 1)

        with ExitStack() as c:
            tcol = sbuf(c, "tcol", [ROWS, 2])
            rn = sbuf(c, "rn", [ROWS, 3, BLOCKS])
            top = sbuf(c, "top", [ROWS, BLOCKS, 8])
            top_u = sbuf(c, "top_u", [ROWS, BLOCKS, 8], U32)
            top_f = sbuf(c, "top_f", [ROWS, BLOCKS, 2])
            oh = sbuf(c, "oh", [ROWS, 2, BLOCKS, NX])
            both = sbuf(c, "both", [ROWS, BLOCKS, NX])
            strict = sbuf(c, "strict", [ROWS, ROWS])
            base = sbuf(c, "base", [ROWS, BLOCKS + 1, NX])
            tot = sbuf(c, "tot", [ROWS, BLOCKS, NX])
            pad_i = sbuf(c, "pad_i", [ROWS, 2, NX], I32)
            start_e = sbuf(c, "start_e", [ROWS, NX + 1])
            padded = sbuf(c, "padded", [ROWS, NX])
            place = sbuf(c, "place", [ROWS, BLOCKS, NX])
            hit = sbuf(c, "hit", [ROWS, 2, BLOCKS, NX])
            slot_f = sbuf(c, "slot_f", [ROWS, 2, BLOCKS])
            dif = sbuf(c, "dif", [ROWS, 3, BLOCKS])
            token = sbuf(c, "token", [ROWS, BLOCKS], I32)
            tile_r = sbuf(c, "tile_r", [1, XTILES])
            xcmp = sbuf(c, "xcmp", [1, XTILES, NX - 1])
            xe_f = sbuf(c, "xe_f", [1, XTILES + 1])
            x_t = sbuf(c, "x_t", [1, 5, XTILES + 1])
            zero_i = sbuf(c, "zero_i", [XTILES, P], I32)
            b_ps = psum(c, "b_ps", [P, 2, 256])
            b_ps2 = psum(c, "b_ps2", [P, 2, 256])
            s_t, s_k, s_n, s_c, s_sm, s_em = sem("rt_temp"), sem("rt_const"), sem("rt_n"), sem("rt_chain"), sem("rt_sm"), sem("rt_em")
            s_oh, s_mm, s_slot, s_z, s_sc, s_q = sem("rt_oh"), sem("rt_mm"), sem("rt_slot"), sem("rt_zero"), sem("rt_scatter"), sem("rt_q")
            with nc.Block() as block:
                @block.sync
                def _(sp):
                    sp.dma_start(tcol[:, 0:1], temp.partition_broadcast(ROWS)).then_inc(s_t, 16)
                    load_weights(sp, 0)
                    sp.dma_start(b1_b[:, :, :].rearrange("p e f -> p (e f)"), b1.rearrange("e f -> (e f)").partition_broadcast(P)).then_inc(s_b1, 16)
                    sp.wait_ge(s_q, 1)
                    sp.dma_start(tok_d.rearrange("(a b) n -> a (b n)", b=P), zero_i[:, :]).then_inc(s_z, 16)
                    sp.wait_ge(s_wlo, WPIECES)
                    load_weights(sp, 1)

                @block.gpsimd
                def _(pool):
                    pool.memset(zero_i[:, :], 0).then_inc(s_q, 1)
                    pool.memset(strict[:, :], 1.0).then_inc(s_k, 1)
                    pool.iota(token[:, :], pattern=[[ROWS, BLOCKS]], base=0, channel_multiplier=1).then_inc(s_k, 1)
                    pool.iota(tile_r[:, :], pattern=[[P, XTILES]], base=0, channel_multiplier=0,
                              allow_small_or_imprecise_dtypes=True).then_inc(s_k, 1)
                    pool.wait_ge(s_k, 3)
                    pool.affine_select(out=strict[:, :], in_=strict[:, :], compare_op=ALU.is_gt, fill=0.0, base=0,
                                       pattern=[[1, ROWS]], channel_multiplier=-1).then_inc(s_k, 1)
                    pool.wait_ge(s_slot, 1)
                    pool.wait_ge(s_z, 16)
                    for b in range(BLOCKS):
                        for n in range(2):
                            pool.indirect_dma_start(out=tok_d[:, :], out_offset=bass.IndirectOffsetOnAxis(ap=slot_i[:, b, n:n + 1], axis=0),
                                                    in_=token[:, b:b + 1], in_offset=None).then_inc(s_sc, 16)
                    pool.wait_ge(s_sc, 32 * BLOCKS)

                @block.scalar
                def _(act):
                    act.activation(rn[:, 0, :], nsq[:, :], ACT.Sqrt).then_inc(s_n, 1)
                    act.wait_ge(s_sm, 1)
                    act.activation(dif[:, 1, :], dif[:, 0, :], ACT.Exp).then_inc(s_em, 1)
                    for e in range(2):
                        high(act, range(WPIECES), e, e)

                @block.vector
                def _(dve):
                    link = Chain(dve, s_c)
                    wide = lambda a: a.unsqueeze(2).broadcast_to([ROWS, BLOCKS, NX])
                    dve.wait_ge(s_n, 1)
                    dve.wait_ge(s_t, 16)
                    link(dve.reciprocal(tcol[:, 1:2], tcol[:, 0:1]))
                    link(dve.tensor_scalar(rn[:, 1, :], rn[:, 0, :], NORM_EPS, None, ALU.max))
                    link(dve.reciprocal(rn[:, 2, :], rn[:, 1, :]))
                    link(dve.tensor_scalar(rn[:, 0, :], rn[:, 2, :], tcol[:, 1:2], None, ALU.mult))
                    link(dve.tensor_tensor(scores[:, :, :], scores[:, :, :], wide(rn[:, 0, :]), ALU.mult))
                    for b in range(BLOCKS):
                        ins = dve.max(top[:, b, :], scores[:, b, :])
                    link(ins)
                    for b in range(BLOCKS):
                        ins = dve.max_index(top_u[:, b, :], top[:, b, :], scores[:, b, :])
                    link(ins)
                    dve.tensor_tensor(dif[:, 0, :], top[:, :, 1], top[:, :, 0], ALU.subtract).then_inc(s_sm, 1)
                    link(dve.tensor_copy(top_f[:, :, :], top_u[:, :, 0:2]))
                    for n in range(2):
                        ins = dve.tensor_tensor(oh[:, n, :, :], iota_row[0:ROWS, 0:NX].unsqueeze(1).broadcast_to([ROWS, BLOCKS, NX]),
                                                wide(top_f[:, :, n]), ALU.is_equal)
                    link(ins)
                    dve.tensor_tensor(both[:, :, :], oh[:, 0, :, :], oh[:, 1, :, :], ALU.add).then_inc(s_oh, 1)
                    dve.memset(base[:, 0, :], 0.0)
                    dve.wait_ge(s_em, 1)
                    link(dve.tensor_scalar(dif[:, 2, :], dif[:, 1, :], 1.0, None, ALU.add))
                    link(dve.reciprocal(gates[:, :, 0], dif[:, 2, :]))
                    link(dve.tensor_tensor(gates[:, :, 1], gates[:, :, 0], dif[:, 1, :], ALU.mult))
                    for n in range(2):
                        ins = dve.tensor_tensor(hit[:, n, :, :], oh[:, n, :, :], wide(gates[:, :, n]), ALU.mult)
                    link(ins)
                    link(dve.tensor_tensor(comb[:, :, :], hit[:, 0, :, :], hit[:, 1, :, :], ALU.add))
                    dve.wait_ge(s_mm, 2)
                    link(dve.tensor_copy(tot[:, :, :], b_ps[0:ROWS, 0, 0:BLOCKS * NX].rearrange("r (b e) -> r b e", e=NX)))
                    for b in range(BLOCKS):
                        link(dve.tensor_tensor(base[:, b + 1, :], base[:, b, :], tot[:, b, :], ALU.add))
                    link(dve.tensor_scalar(padded[:, :], base[:, BLOCKS, :], float(P - 1), float(P), ALU.add, ALU.max))
                    link(dve.tensor_copy(pad_i[:, 0, :], padded[:, :]))
                    link(dve.tensor_scalar(pad_i[:, 1, :], pad_i[:, 0, :], -P, None, ALU.bitwise_and))
                    link(dve.memset(start_e[:, :], 0.0))
                    link(dve.tensor_copy(padded[:, :], pad_i[:, 1, :]))
                    for e in range(NX):
                        link(dve.tensor_tensor(start_e[:, e + 1:e + 2], start_e[:, e:e + 1], padded[:, e:e + 1], ALU.add))
                    link(dve.tensor_tensor(place[:, :, :], base[:, 0:BLOCKS, :],
                                           start_e[:, 0:NX].unsqueeze(1).broadcast_to([ROWS, BLOCKS, NX]), ALU.add))
                    link(dve.tensor_tensor(tot[:, :, :], place[:, :, :],
                                           b_ps2[0:ROWS, 0, 0:BLOCKS * NX].rearrange("r (b e) -> r b e", e=NX), ALU.add))
                    for n in range(2):
                        ins = dve.tensor_tensor(hit[:, n, :, :], oh[:, n, :, :], tot[:, :, :], ALU.mult)
                    link(ins)
                    link(dve.tensor_reduce(slot_f[:, :, :], hit[:, :, :, :], AX.X, ALU.add))
                    dve.tensor_copy(slot_i[:, :, :].rearrange("r b n -> r n b"), slot_f[:, :, :]).then_inc(s_slot, 1)
                    dve.wait_ge(s_k, 4)
                    link(dve.tensor_tensor(xcmp[:, :, :], tile_r[:, :].unsqueeze(2).broadcast_to([1, XTILES, NX - 1]),
                                           start_e[0:1, 1:NX].unsqueeze(1).broadcast_to([1, XTILES, NX - 1]), ALU.is_ge))
                    dve.memset(xe_f[:, 0:1], -1.0)
                    dve.memset(x_t[:, 4, 0:1], 0.0)
                    link(dve.tensor_reduce(xe_f[:, 1:XTILES + 1], xcmp[:, :, :], AX.X, ALU.add))
                    buf, buf2, first = x_t[:, 2, :], x_t[:, 3, :], x_t[:, 4, :]
                    now, ago = slice(1, XTILES + 1), slice(0, XTILES)
                    for n in range(2):
                        ins = dve.tensor_scalar(x_t[:, n, :], xe_f[:, :], 3.0 * (n + 1), -3.0, ALU.is_ge, ALU.mult)
                    link(ins)
                    link(dve.tensor_tensor(buf, x_t[:, 0, :], x_t[:, 1, :], ALU.add))
                    link(dve.tensor_tensor(buf, buf, xe_f[:, :], ALU.add))
                    link(dve.tensor_scalar(buf, buf, 0.0, None, ALU.max))
                    link(dve.tensor_scalar(x_t[:, 0, :], buf, 0.0, 3.0, ALU.is_equal, ALU.mult))
                    link(dve.scalar_tensor_tensor(buf2, buf, -1.0, x_t[:, 0, :], ALU.add, ALU.add))
                    dve.tensor_tensor(x_t[:, 0, now], xe_f[:, now], xe_f[:, ago], ALU.not_equal)
                    link(dve.tensor_scalar(x_t[:, 1, now], xe_f[:, now], float(NX - 2), None, ALU.is_lt))
                    link(dve.tensor_tensor(first[:, now], x_t[:, 0, now], x_t[:, 1, now], ALU.mult))
                    link(dve.tensor_copy(x_t[:, 0, now], xe_f[:, now]))
                    for part, shift in ((buf[:, now], 3), (buf[:, ago], 5), (first[:, now], 7), (first[:, ago], 8)):
                        link(dve.scalar_tensor_tensor(x_t[:, 0, now], part, float(1 << shift), x_t[:, 0, now], ALU.mult, ALU.add))
                    for n, row in enumerate((x_t[:, 0, now], buf2[:, now], xe_f[:, ago], buf2[:, ago])):
                        dve.tensor_copy(x_i[:, n, :], row)
                    for e in range(2):
                        low(dve, range(WPIECES), e, e)

                @block.tensor
                def _(pe):
                    pe.wait_ge(s_oh, 1)
                    pe.wait_ge(s_k, 4)
                    flat = both[:, :, :].rearrange("r b e -> r (b e)")
                    pe.matmul(b_ps[0:ROWS, 0, 0:BLOCKS * NX], ones[0:ROWS, 0:ROWS], flat, start=True, stop=True).then_inc(s_mm, 1)
                    pe.matmul(b_ps2[0:ROWS, 0, 0:BLOCKS * NX], strict[:, :], flat, start=True, stop=True).then_inc(s_mm, 1)

        with expert_ctx, ExitStack() as c:
            tok_r = sbuf(c, "tok_r", [XTILES, P], I32)
            tok_f = sbuf(c, "tok_f", [XTILES, P])
            tokT = sbuf(c, "tokT", [P, XTILES], I32)
            xi = sbuf(c, "xi", [P, 2, 1], I32)
            spare = WpT[:, :, :, :].rearrange("p n k d -> p (n k d)")
            n_x, n_h = 4 * D, 4 * FF
            xg = spare[:, 0:n_x].rearrange("p (a n d) -> p a n d", a=2, n=2)
            xgT = spare[:, n_x:2 * n_x].rearrange("p (a n k c) -> p a n k c", a=2, n=2, k=KD)
            hT = spare[:, 2 * n_x:2 * n_x + n_h].rearrange("p (a n f c) -> p a n f c", a=2, n=2, f=KF)
            h_b = sbuf(c, "h_b", [P, FF])
            h_g = sbuf(c, "h_g", [P, FF])
            h_s = sbuf(c, "h_s", [P, 2, FF], F16)
            eo = sbuf(c, "eo", [P, 2, D])
            tr_ps = c.enter_context(nc.psum_tensor("x_tr", [P, 2, KD, P], F16))
            ht_ps = c.enter_context(nc.psum_tensor("x_ht", [P, 2, KF, P], F16))
            h_ps = psum(c, "x_h", [P, FF])
            o_ps = psum(c, "x_o", [P, 2, D])
            s_ld, s_c, s_t0, s_xi = sem("xp_load"), sem("xp_chain"), sem("xp_t0"), sem("xp_xi")
            s_g = [sem(f"xp_g{p}") for p in range(2)]
            s_st = [sem(f"xp_st{p}") for p in range(2)]
            s_tr, s_xT, s_h, s_hb, s_gel = sem("xp_tr"), sem("xp_xT"), sem("xp_h"), sem("xp_hb"), sem("xp_gelu")
            s_hi, s_lo, s_ht, s_hT, s_o, s_eo = sem("xp_hi"), sem("xp_lo"), sem("xp_ht"), sem("xp_hT"), sem("xp_o"), sem("xp_eo")

            def tile_value(eng, n, i, **bounds):
                return eng.value_load(x_i[:, n, i:i + 1] if isinstance(i, int) else x_i[:, n, bass.ds(i, 1)], **bounds)

            def tile_word(eng, i):
                w = tile_value(eng, 0, i)
                return ((w & 7).with_bounds(min_val=0, max_val=NX - 1), ((w >> 3) & 3).with_bounds(min_val=0, max_val=2),
                        ((w >> 5) & 3).with_bounds(min_val=0, max_val=2), (w >> 7) & 1, (w >> 8) & 1)

            def split(eng, part, i, e, flag, flag_ago):
                half = WPIECES // 2
                if not early(i, 1):
                    with eng.If(flag_ago == 1):
                        e_ago = tile_value(eng, 2, i, min_val=0, max_val=NX - 3)
                        q = tile_value(eng, 3, i, min_val=0, max_val=2)
                        part(eng, range(half, WPIECES), e_ago + 2, q)
                with eng.If(flag == 1):
                    q = tile_value(eng, 1, i, min_val=0, max_val=2)
                    part(eng, range(half), e + 2, q)

            with nc.Block() as block:
                @block.sync
                def _(sp):
                    sp.dma_start(tok_r[:, :], tok_d.rearrange("(a b) n -> a (b n)", b=P)).then_inc(s_ld, 16)

                    def body(i, j, p):
                        e, _, _, flag, _ = tile_word(sp, i)
                        with sp.If(flag == 1):
                            e = e.with_bounds(min_val=0, max_val=NX - 3)
                            sp.wait_ge(s_wlo, WPIECES * (e + 2))
                            load_weights(sp, e + 2)
                    steps(sp, XTILES, body)

                @block.gpsimd
                def _(pool):
                    pool.wait_ge(s_c, 2)

                    def store(i, j, p):
                        pool.wait_ge(s_eo, i + 1)
                        d = eo_d[P * i:P * (i + 1), :] if isinstance(i, int) else eo_d[bass.ds(P * i, P), :]
                        pool.dma_start(d, eo[:, p, :]).then_inc(s_st[p], 16)

                    def body(i, j, p):
                        if not early(i, 2):
                            pool.wait_ge(s_tr, i - 1)
                        pool.tensor_copy(xi[:, p, :], tokT[:, i:i + 1] if isinstance(i, int) else tokT[:, bass.ds(i, 1)]).then_inc(s_xi, 1)
                        wait_apart(pool, s_met, s_xi, i + 1)
                        pool.indirect_dma_start(out=xg[:, p, :, :].rearrange("k n d -> k (n d)"), out_offset=None, in_=x2n_d[:, :],
                                                in_offset=bass.IndirectOffsetOnAxis(ap=xi[:, p, :], axis=0)).then_inc(s_g[p], 16)
                        if not early(i, 2):
                            store(i - 2, j, p)
                    steps(pool, XTILES, body)
                    store(XTILES - 2, 0, 0)
                    store(XTILES - 1, 0, 1)
                    pool.wait_ge(s_st[0], 8 * XTILES)
                    pool.wait_ge(s_st[1], 8 * XTILES)

                @block.vector
                def _(dve):
                    dve.wait_ge(s_b1, 16)
                    dve.wait_ge(s_ld, 16)
                    dve.tensor_copy(tok_f[:, :], tok_r[:, :]).then_inc(s_c, 1)
                    dve.wait_ge(s_t0, 1)
                    dve.tensor_copy(tokT[:, :], o_ps[:, 1, 0:XTILES]).then_inc(s_c, 1)

                    def take(i, j, p):
                        dve.wait_ge(s_o, i + 1)
                        if not early(i, 2):
                            dve.wait_ge(s_st[p], 16 * j)
                        dve.tensor_scalar(eo[:, p, :], o_ps[:, p, :], 1.0 / WS, None, ALU.mult).then_inc(s_eo, 1)

                    def body(i, j, p):
                        e, _, _, flag, flag_ago = tile_word(dve, i)
                        dve.wait_ge(s_h, i + 1)
                        if not early(i, 1):
                            dve.wait_ge(s_gel, i)
                        dve.scalar_tensor_tensor(h_b[:, :], h_ps[:, :], 1.0 / WS, b1_b[:, bass.ds(e, 1), :].squeeze(1),
                                                 ALU.mult, ALU.add).then_inc(s_hb, 1)
                        dve.wait_ge(s_hi, i + 1)
                        dve.tensor_tensor(h_s[:, 1, :], h_g[:, :], h_s[:, 0, :], ALU.subtract).then_inc(s_lo, 1)
                        if not early(i, 1):
                            take(i - 1, j - 1 + p, 1 - p)
                        split(dve, low, i, e, flag, flag_ago)
                    steps(dve, XTILES, body)
                    take(XTILES - 1, (XTILES - 1) // 2, (XTILES - 1) % 2)

                @block.scalar
                def _(act):
                    def take_x(i, p):
                        act.wait_ge(s_tr, i + 1)
                        if not early(i, 2):
                            act.wait_ge(s_h, i - 1)
                        act.activation(xgT[:, p, :, :, :], tr_ps[:, :, :, :], ACT.Copy).then_inc(s_xT, 1)

                    def body(i, j, p):
                        e, _, _, flag, flag_ago = tile_word(act, i)
                        act.wait_ge(s_hb, i + 1)
                        if not early(i, 1):
                            act.wait_ge(s_lo, i)
                            act.wait_ge(s_ht, i)
                        act.activation(h_g[:, :], h_b[:, :], ACT.Gelu).then_inc(s_gel, 1)
                        act.wait_ge(s_gel, i + 1)
                        act.activation(h_s[:, 0, :], h_g[:, :], ACT.Copy).then_inc(s_hi, 1)
                        if not (isinstance(i, int) and i == XTILES - 1):
                            take_x(i + 1, 1 - p)
                        act.wait_ge(s_ht, i + 1)
                        if not early(i, 2):
                            act.wait_ge(s_o, i - 1)
                        act.activation(hT[:, p, :, :, :], ht_ps[:, :, :, :], ACT.Copy).then_inc(s_hT, 1)
                        if not (isinstance(i, int) and i == XTILES - 1):
                            if not early(i, 1):
                                act.wait_ge(s_o, i)
                            split(act, high, i, e, flag, flag_ago)
                    take_x(0, 0)
                    steps(act, XTILES, body, tail=2)

                @block.tensor
                def _(pe):
                    pe.wait_ge(s_c, 1)
                    pe.transpose(o_ps[:, 1, 0:XTILES], tok_f[:, :], ident[0:XTILES, 0:XTILES]).then_inc(s_t0, 1)
                    pe.wait_ge(s_c, 2)

                    def turn(i, p, g):
                        pe.wait_ge(s_g[p], g)
                        if not early(i, 1):
                            pe.wait_ge(s_xT, i)
                        turn_parts(pe, tr_ps, xg[:, p, :, :], ident16).then_inc(s_tr, 1)

                    def first(i, p):
                        e, q, q_ago, _, _ = tile_word(pe, i)
                        pe.wait_ge(s_wlo, WPIECES * (e + 1))
                        pe.wait_ge(s_xT, i + 1)
                        if not early(i, 1):
                            pe.wait_ge(s_hb, i)
                        per = WCOLS // FF
                        for k in range(KD):
                            for a, b in ((0, 0), (0, 1), (1, 0)):
                                w = w_p[:, bass.ds(q, 1), b, k // per, (k % per) * FF:(k % per + 1) * FF].squeeze(1)
                                ins = pe.matmul(h_ps[:, :], xgT[:, p, a, k, :], w, start=(k == 0 and a == b), stop=(k == KD - 1 and a == 1))
                        ins.then_inc(s_h, 1)
                        return q_ago

                    def second(i, p, q, n):
                        if n == 0:
                            pe.wait_ge(s_hT, i + 1)
                            if not early(i, 2):
                                pe.wait_ge(s_eo, i - 1)
                        per = WCOLS // D
                        for f in range(KF):
                            for a, b in ((0, 0), (0, 1), (1, 0)):
                                at_col = (f % per) * D + n * 512
                                w = w_p[:, bass.ds(q, 1), b, WPIECES // 2 + f // per, at_col:at_col + 512].squeeze(1)
                                ins = pe.matmul(o_ps[:, p, n * 512:(n + 1) * 512], hT[:, p, a, f, :], w,
                                                start=(f == 0 and a == b), stop=(f == KF - 1 and a == 1))
                        if n == 1:
                            ins.then_inc(s_o, 1)

                    def turn_h(i):
                        pe.wait_ge(s_lo, i + 1)
                        if not early(i, 1):
                            pe.wait_ge(s_hT, i)
                        for part in range(2):
                            for f in range(KF):
                                ins = pe.transpose(ht_ps[:, part, f, :], h_s[:, part, f * P:(f + 1) * P], ident16[:, :])
                        ins.then_inc(s_ht, 1)

                    def body(i, j, p):
                        q_ago = first(i, p)
                        if not early(i, 1):
                            second(i - 1, 1 - p, q_ago, 0)
                        if not (isinstance(i, int) and i == XTILES - 1):
                            turn(i + 1, 1 - p, 16 * (j + 1 + p))
                        if not early(i, 1):
                            second(i - 1, 1 - p, q_ago, 1)
                        turn_h(i)
                    turn(0, 0, 16)
                    steps(pe, XTILES, body, tail=2)
                    _, q, _, _, _ = tile_word(pe, XTILES - 1)
                    for n in range(2):
                        second(XTILES - 1, (XTILES - 1) % 2, q, n)

        with ExitStack() as c:
            b2_sb = sbuf(c, "b2_sb", [NX, D])
            s_cs = sem("cb_comb")
            comb_s = sbuf(c, "comb_s", [ROWS, 2, NX])
            combT = sbuf(c, "combT", [NX, 2, ROWS])
            ci = sbuf(c, "ci", [ROWS, 2, 2], I32)
            x2 = sbuf(c, "c_x2", [ROWS, 2, D])
            r = [sbuf(c, f"c_r{n}", [ROWS, 2, D]) for n in range(2)]
            y = sbuf(c, "c_y", [ROWS, 2, D])
            t_ps = psum(c, "c_t", [P, 2, 512])
            b_ps = psum(c, "c_b", [P, 2, D])
            s_b2, s_ci, s_tr, s_cT, s_bb, s_y, s_yc = sem("cb_b2"), sem("cb_ci"), sem("cb_tr"), sem("cb_cT"), sem("cb_bb"), sem("cb_y"), sem("cb_yc")
            s_x = [sem(f"cb_x{p}") for p in range(2)]
            s_r = [sem(f"cb_r{p}") for p in range(2)]
            s_out = [sem(f"cb_out{p}") for p in range(2)]
            with nc.Block() as block:
                @block.sync
                def _(sp):
                    sp.dma_start(b2_sb[:, :], b2).then_inc(s_b2, 16)

                    def body(i, j, p):
                        if not early(i, 2):
                            sp.wait_ge(s_y, i - 1)
                        sp.dma_start(x2[:, p, :], rows_of(x2_d, i)).then_inc(s_x[p], 16)
                        if not early(i, 1):
                            store(i - 1, 1 - p)

                    def store(i, p):
                        sp.wait_ge(s_y, i + 1)
                        sp.dma_start(rows_of(out, i), y[:, p, :]).then_inc(s_out[p], 16)
                    steps(sp, BLOCKS, body)
                    store(BLOCKS - 1, (BLOCKS - 1) % 2)
                    sp.wait_ge(s_out[0], 16 * (BLOCKS - BLOCKS // 2))
                    sp.wait_ge(s_out[1], 16 * (BLOCKS // 2))

                @block.gpsimd
                def _(pool):
                    def body(i, j, p):
                        s = slot_i[:, i, :] if isinstance(i, int) else slot_i[:, bass.ds(i, 1), :].squeeze(1)
                        if not early(i, 2):
                            pool.wait_ge(s_y, i - 1)
                        pool.tensor_copy(ci[:, p, :], s).then_inc(s_ci, 1)
                        wait_apart(pool, s_met, s_ci, i + 1)
                        for n in range(2):
                            pool.indirect_dma_start(out=r[n][:, p, :], out_offset=None, in_=eo_d[:, :],
                                                    in_offset=bass.IndirectOffsetOnAxis(ap=ci[:, p, n:n + 1], axis=0)).then_inc(s_r[p], 16)
                    steps(pool, BLOCKS, body)

                @block.tensor
                def _(pe):
                    pe.wait_ge(s_b2, 16)

                    def body(i, j, p):
                        pe.wait_ge(s_cs, i + 1)
                        if not early(i, 2):
                            pe.wait_ge(s_cT, i - 1)
                        pe.transpose(t_ps[0:NX, p, 0:ROWS], comb_s[:, p, :], ident[0:ROWS, 0:ROWS]).then_inc(s_tr, 1)
                        pe.wait_ge(s_cT, i + 1)
                        if not early(i, 2):
                            pe.wait_ge(s_y, i - 1)
                        for n in range(2):
                            ins = pe.matmul(b_ps[0:ROWS, p, n * 512:(n + 1) * 512], combT[:, p, :], b2_sb[:, n * 512:(n + 1) * 512], start=True, stop=True)
                        ins.then_inc(s_bb, 1)

                    steps(pe, BLOCKS, body)

                @block.scalar
                def _(act):
                    def body(i, j, p):
                        cb = comb[:, i, :] if isinstance(i, int) else comb[:, bass.ds(i, 1), :].squeeze(1)
                        if not early(i, 2):
                            act.wait_ge(s_tr, i - 1)
                        act.activation(comb_s[:, p, :], cb, ACT.Copy).then_inc(s_cs, 1)
                        act.wait_ge(s_tr, i + 1)
                        if not early(i, 2):
                            act.wait_ge(s_bb, i - 1)
                        act.activation(combT[:, p, :], t_ps[0:NX, p, 0:ROWS], ACT.Copy).then_inc(s_cT, 1)
                    steps(act, BLOCKS, body)

                @block.vector
                def _(dve):
                    def body(i, j, p):
                        link = Chain(dve, s_yc, 2 * i)
                        g = lambda n: (gates[:, i, n:n + 1] if isinstance(i, int) else gates[:, bass.ds(i, 1), n:n + 1].squeeze(1))
                        dve.wait_ge(s_x[p], 16 * (j + 1))
                        dve.wait_ge(s_bb, i + 1)
                        if not early(i, 2):
                            dve.wait_ge(s_out[p], 16 * j)
                        link(dve.tensor_tensor(y[:, p, :], x2[:, p, :], b_ps[0:ROWS, p, :], ALU.add))
                        dve.wait_ge(s_r[p], 32 * (j + 1))
                        link(dve.scalar_tensor_tensor(y[:, p, :], r[0][:, p, :], g(0), y[:, p, :], ALU.mult, ALU.add))
                        dve.scalar_tensor_tensor(y[:, p, :], r[1][:, p, :], g(1), y[:, p, :], ALU.mult, ALU.add).then_inc(s_y, 1)
                    steps(dve, BLOCKS, body)


def product(pe, out, lhs, rhs, chunks, last):
    for k in chunks:
        for a, b in ((0, 0), (0, 1), (1, 0)):
            ins = pe.matmul(out, lhs[:, a, k, :], rhs[:, b, k, :], start=(k == 0 and a == b), stop=(k == last - 1 and a == 1))
    return ins


def turn_parts(pe, out, parts, ident16):
    n = parts.shape[0]
    for part in range(2):
        for k in range(KD):
            ins = pe.transpose(out[:, part, k, 0:n], parts[:, part, k * P:(k + 1) * P], ident16[0:n, 0:n])
    return ins


def layer_norm(dve, xt, xn, xs, stat, ln, s_ln, s_var, s_std, s_met, s_xf, s_xh, s_xn, i):
    link = Chain(dve, s_ln, 6 * i)
    dve.bn_stats(stat[:, 0, :], xt[:, 0:512])
    link(dve.bn_stats(stat[:, 1, :], xt[:, 512:1024]), s_met)
    link(dve.bn_aggr(ln[:, 0:2], stat))
    dve.tensor_scalar(ln[:, 2:3], ln[:, 1:2], LN_EPS, None, ALU.add).then_inc(s_var, 1)
    dve.wait_ge(s_std, i + 1)
    link(dve.reciprocal(ln[:, 4:5], ln[:, 3:4]))
    link(dve.tensor_scalar(ln[:, 5:6], ln[:, 4:5], ln[:, 4:5], ln[:, 2:3], ALU.mult, ALU.mult))
    link(dve.tensor_scalar(ln[:, 6:7], ln[:, 5:6], -0.5, 1.5, ALU.mult, ALU.add))
    dve.tensor_tensor(ln[:, 7:8], ln[:, 6:7], ln[:, 4:5], ALU.mult).then_inc(s_ln, 1)
    if not early(i, 1):
        dve.wait_ge(s_xn, i)
    dve.wait_ge(s_ln, 6 * i + 6)
    dve.tensor_scalar(xn, xt, ln[:, 0:1], ln[:, 7:8], ALU.subtract, ALU.mult).then_inc(s_xf, 1)
    dve.wait_ge(s_xf, i + 1)
    dve.wait_ge(s_xh, i + 1)
    dve.tensor_tensor(xs[:, 1, :], xn, xs[:, 0, :], ALU.subtract).then_inc(s_xn, 1)


_INS = ['x', 'src', 'dst', 'L0_gnn_W', 'L0_gnn_att_src', 'L0_gnn_att_dst', 'L0_gnn_bias', 'L0_ffn_Wp',
        'L0_ffn_sim_matrix', 'L0_ffn_temperature', 'L0_ffn_W1', 'L0_ffn_b1', 'L0_ffn_W2', 'L0_ffn_b2']


def kernel(**inputs):
    import numpy as _np
    import concourse.bacc as _bacc
    from concourse import mybir as _mybir
    from concourse.bass_utils import run_bass_kernel_spmd as _run

    nc = _bacc.Bacc("TRN2", target_bir_lowering=False, num_devices=1)
    arrays, args = {}, []
    for name in _INS:
        a = _np.ascontiguousarray(inputs[name])
        if a.ndim == 0:
            a = a.reshape(1)
        arrays[f"in_{name}_dram"] = a
        args.append(nc.dram_tensor(f"in_{name}_dram", a.shape, _mybir.dt.from_np(a.dtype), kind="ExternalInput").ap())
    args.append(nc.dram_tensor("out_0_dram", (NODES, D), F32, kind="ExternalOutput").ap())
    program(nc, *args)
    r = _run(nc, [arrays], core_ids=[0])
    return r.results[0]["out_0_dram"]
```
